# Optimizing a Trainium2 kernel written in Bass

```python
import numpy as np
import jax
import jax.numpy as jnp

def _softmax(x, axis=-1):
    return jax.nn.softmax(x, axis=axis)

def _gelu(x):
    return jax.nn.gelu(x, approximate=True)

def _silu(x):
    return jax.nn.silu(x)

def _sigmoid(x):
    return jax.nn.sigmoid(x)

def _layernorm(x, axis=-1, eps=1e-05):
    m = jnp.mean(x, axis=axis, keepdims=True)
    v = jnp.var(x, axis=axis, keepdims=True)
    return (x - m) / jnp.sqrt(v + eps)

def _scatter_add(tgt, idx, src, axis=0):
    return tgt.at[idx].add(src)

def _segment_sum(src, seg, n):
    return jax.ops.segment_sum(src, seg, n)
kernel_name = 'mk_xattn_ffn_d2_seqx_r4_1cfae7'

def setup_inputs(seed: int=0):
    np.random.seed(seed)
    _w = jnp.asarray

    def _rec_inputs():
        import jax
        import jax.numpy as jnp
        _rk = jax.random.key(seed)
        x = 7.22e-05 + 1 * jax.random.normal(jax.random.fold_in(_rk, 1), (4, 512, 512), jnp.float32)
        _lenS = 512 - jax.random.randint(jax.random.fold_in(_rk, 7), (4,), 0, max(1, 512 // 4) + 1, jnp.int32)
        _lenS2 = 512 - jax.random.randint(jax.random.fold_in(_rk, 8), (4,), 0, max(1, 512 // 4) + 1, jnp.int32)
        _ctx_1024P = jax.random.normal(jax.random.fold_in(_rk, 11), (4, 16, 256), jnp.float32)
        _ctx_1024c = jax.random.dirichlet(jax.random.fold_in(_rk, 511), 0.3 * jnp.ones((16,), jnp.float32), (4, 512))
        _ctx_1024t = jnp.einsum('bsk,bkd->bsd', _ctx_1024c, _ctx_1024P)
        _ctx_1024t = _ctx_1024t * jax.lax.rsqrt(jnp.mean(jnp.square(_ctx_1024t)) + 1e-12) * 0.953939
        ctx_1024 = 2.81802e-05 + 1.00001 * (_ctx_1024t + 0.3 * jax.random.normal(jax.random.fold_in(_rk, 611), (4, 512, 256), jnp.float32))
        return (x, ctx_1024)
    x, ctx_1024 = _rec_inputs()

    def _L0_xattn_setup():
        import jax, jax.numpy as jnp
        import numpy as np
        key = jax.random.key(seed)
        ks = jax.random.split(key, 6)
        B, L, N, C, D = (8, 128, 512, 256, 128)
        return {'teacher_logits': jax.random.normal(ks[0], (B, L, N), dtype=jnp.float32), 'teacher_features': jax.random.normal(ks[1], (B, N, C), dtype=jnp.float32), 'Wq': jax.random.normal(ks[2], (D, C), dtype=jnp.float32) * (1.0 / np.sqrt(C)), 'bq': jnp.zeros((D,), dtype=jnp.float32), 'Wk': jax.random.normal(ks[3], (D, C), dtype=jnp.float32) * (1.0 / np.sqrt(C)), 'bk': jnp.zeros((D,), dtype=jnp.float32)}
    _L0_xattn_all = _L0_xattn_setup()
    _L0_xattn_in = {k: v for k, v in _L0_xattn_all.items() if k in ('Wq', 'bq', 'Wk', 'bk')}
    del _L0_xattn_all

    def _L0_ffn_setup():
        import jax, jax.numpy as jnp
        import numpy as np
        CAPACITY = 0.125
        HEAD_DIM = 128
        N_HEADS = 16
        N_KV_HEADS = 8
        ROPE_THETA = 10000.0
        EPS = 1e-06

        def _rms_norm(x, w):
            return x * jax.lax.rsqrt(jnp.mean(x * x, axis=-1, keepdims=True) + EPS) * w

        def _rotate_half(t):
            h = t.shape[-1] // 2
            return jnp.concatenate([-t[..., h:], t[..., :h]], axis=-1)
        key = jax.random.key(seed)
        ks = jax.random.split(key, 12)
        B, T, D = (4, 1024, 512)
        I = 2048
        s = 0.02
        return {'hidden_states': jax.random.normal(ks[0], (B, T, D), jnp.float32), 'w_router': jax.random.normal(ks[1], (D,), jnp.float32) * s, 'wq': jax.random.normal(ks[2], (D, N_HEADS * HEAD_DIM), jnp.float32) * s, 'bq': jnp.zeros((N_HEADS * HEAD_DIM,), jnp.float32), 'wk': jax.random.normal(ks[3], (D, N_KV_HEADS * HEAD_DIM), jnp.float32) * s, 'bk': jnp.zeros((N_KV_HEADS * HEAD_DIM,), jnp.float32), 'wv': jax.random.normal(ks[4], (D, N_KV_HEADS * HEAD_DIM), jnp.float32) * s, 'bv': jnp.zeros((N_KV_HEADS * HEAD_DIM,), jnp.float32), 'wo': jax.random.normal(ks[5], (N_HEADS * HEAD_DIM, D), jnp.float32) * s, 'w_gate': jax.random.normal(ks[6], (D, I), jnp.float32) * s, 'w_up': jax.random.normal(ks[7], (D, I), jnp.float32) * s, 'w_down': jax.random.normal(ks[8], (I, D), jnp.float32) * s, 'ln1_w': jnp.ones((D,), jnp.float32), 'ln2_w': jnp.ones((D,), jnp.float32)}
    _L0_ffn_all = _L0_ffn_setup()
    _L0_ffn_in = {k: v for k, v in _L0_ffn_all.items() if k in ('w_router', 'wq', 'bq', 'wk', 'bk', 'wv', 'bv', 'wo', 'w_gate', 'w_up', 'w_down', 'ln1_w', 'ln2_w')}
    del _L0_ffn_all

    def _L1_xattn_setup():
        import jax, jax.numpy as jnp
        import numpy as np
        B, S1, S2, DCA = (2, 512, 256, 16)
        QDIM, KDIM, H = (512, 256, 16)
        HD = QDIM // H
        SCALE = HD ** (-0.5)
        EPS = 1e-06
        DCA_WEIGHT = 1.0

        def _ln(t, w, b):
            m = jnp.mean(t, axis=-1, keepdims=True)
            v = jnp.var(t, axis=-1, keepdims=True)
            return (t - m) * jax.lax.rsqrt(v + EPS) * w + b

        def _attn(q, k, v):
            s = jnp.einsum('bhqd,bhkd->bhqk', q, k) * SCALE
            p = jax.nn.softmax(s, axis=-1)
            return jnp.einsum('bhqk,bhkd->bhqd', p, v)
        key = jax.random.key(seed)
        ks = jax.random.split(key, 8)
        w = lambda k, shape: jax.random.normal(k, shape, jnp.float32) * 0.02
        return {'x': jax.random.normal(ks[0], (B, S1, QDIM), jnp.float32), 'y': jax.random.normal(ks[1], (B, S2 + DCA, KDIM), jnp.float32), 'Wq': w(ks[2], (QDIM, QDIM)), 'bq': jnp.zeros((QDIM,), jnp.float32), 'Wk': w(ks[3], (KDIM, QDIM)), 'bk': jnp.zeros((QDIM,), jnp.float32), 'Wv': w(ks[4], (KDIM, QDIM)), 'bv': jnp.zeros((QDIM,), jnp.float32), 'Wkv_dca': w(ks[5], (KDIM, 2 * QDIM)), 'bkv_dca': jnp.zeros((2 * QDIM,), jnp.float32), 'qn_w': jnp.ones((HD,), jnp.float32), 'qn_b': jnp.zeros((HD,), jnp.float32), 'kn_w': jnp.ones((HD,), jnp.float32), 'kn_b': jnp.zeros((HD,), jnp.float32), 'kn_dca_w': jnp.ones((HD,), jnp.float32), 'kn_dca_b': jnp.zeros((HD,), jnp.float32), 'Wo': w(ks[6], (QDIM, QDIM)), 'bo': jnp.zeros((QDIM,), jnp.float32)}
    _L1_xattn_all = _L1_xattn_setup()
    _L1_xattn_in = {k: v for k, v in _L1_xattn_all.items() if k in ('Wq', 'bq', 'Wk', 'bk', 'Wv', 'bv', 'Wkv_dca', 'bkv_dca', 'qn_w', 'qn_b', 'kn_w', 'kn_b', 'kn_dca_w', 'kn_dca_b', 'Wo', 'bo')}
    del _L1_xattn_all

    def _L1_ffn_setup():
        import jax, jax.numpy as jnp
        import numpy as np
        NUM_EXPERTS = 32
        TOP_K = 6
        N_GROUPS = 4
        N_LIMITED_GROUPS = 2
        key = jax.random.key(seed)
        ks = jax.random.split(key, 8)
        H, M = (512, 352)
        SH = 2 * M
        s = 0.02
        return {'hidden_states': jax.random.normal(ks[0], (4, 512, H), jnp.float32), 'gate_w': jax.random.normal(ks[1], (H, NUM_EXPERTS), jnp.float32) * s, 'w_gate': jax.random.normal(ks[2], (NUM_EXPERTS, H, M), jnp.float32) * s, 'w_up': jax.random.normal(ks[3], (NUM_EXPERTS, H, M), jnp.float32) * s, 'w_down': jax.random.normal(ks[4], (NUM_EXPERTS, M, H), jnp.float32) * s, 'sw_gate': jax.random.normal(ks[5], (H, SH), jnp.float32) * s, 'sw_up': jax.random.normal(ks[6], (H, SH), jnp.float32) * s, 'sw_down': jax.random.normal(ks[7], (SH, H), jnp.float32) * s}
    _L1_ffn_all = _L1_ffn_setup()
    _L1_ffn_in = {k: v for k, v in _L1_ffn_all.items() if k in ('gate_w', 'w_gate', 'w_up', 'w_down', 'sw_gate', 'sw_up', 'sw_down')}
    del _L1_ffn_all
    return {'x': x, 'ctx_1024': ctx_1024, 'L0_xattn_Wq': _L0_xattn_in['Wq'], 'L0_xattn_bq': _L0_xattn_in['bq'], 'L0_xattn_Wk': _L0_xattn_in['Wk'], 'L0_xattn_bk': _L0_xattn_in['bk'], 'L0_ffn_w_router': _L0_ffn_in['w_router'], 'L0_ffn_wq': _L0_ffn_in['wq'], 'L0_ffn_bq': _L0_ffn_in['bq'], 'L0_ffn_wk': _L0_ffn_in['wk'], 'L0_ffn_bk': _L0_ffn_in['bk'], 'L0_ffn_wv': _L0_ffn_in['wv'], 'L0_ffn_bv': _L0_ffn_in['bv'], 'L0_ffn_wo': _L0_ffn_in['wo'], 'L0_ffn_w_gate': _L0_ffn_in['w_gate'], 'L0_ffn_w_up': _L0_ffn_in['w_up'], 'L0_ffn_w_down': _L0_ffn_in['w_down'], 'L0_ffn_ln1_w': _L0_ffn_in['ln1_w'], 'L0_ffn_ln2_w': _L0_ffn_in['ln2_w'], 'L1_xattn_Wq': _L1_xattn_in['Wq'], 'L1_xattn_bq': _L1_xattn_in['bq'], 'L1_xattn_Wk': _L1_xattn_in['Wk'], 'L1_xattn_bk': _L1_xattn_in['bk'], 'L1_xattn_Wv': _L1_xattn_in['Wv'], 'L1_xattn_bv': _L1_xattn_in['bv'], 'L1_xattn_Wkv_dca': _L1_xattn_in['Wkv_dca'], 'L1_xattn_bkv_dca': _L1_xattn_in['bkv_dca'], 'L1_xattn_qn_w': _L1_xattn_in['qn_w'], 'L1_xattn_qn_b': _L1_xattn_in['qn_b'], 'L1_xattn_kn_w': _L1_xattn_in['kn_w'], 'L1_xattn_kn_b': _L1_xattn_in['kn_b'], 'L1_xattn_kn_dca_w': _L1_xattn_in['kn_dca_w'], 'L1_xattn_kn_dca_b': _L1_xattn_in['kn_dca_b'], 'L1_xattn_Wo': _L1_xattn_in['Wo'], 'L1_xattn_bo': _L1_xattn_in['bo'], 'L1_ffn_gate_w': _L1_ffn_in['gate_w'], 'L1_ffn_w_gate': _L1_ffn_in['w_gate'], 'L1_ffn_w_up': _L1_ffn_in['w_up'], 'L1_ffn_w_down': _L1_ffn_in['w_down'], 'L1_ffn_sw_gate': _L1_ffn_in['sw_gate'], 'L1_ffn_sw_up': _L1_ffn_in['sw_up'], 'L1_ffn_sw_down': _L1_ffn_in['sw_down']}

def reference(x, ctx_1024, L0_xattn_Wq, L0_xattn_bq, L0_xattn_Wk, L0_xattn_bk, L0_ffn_w_router, L0_ffn_wq, L0_ffn_bq, L0_ffn_wk, L0_ffn_bk, L0_ffn_wv, L0_ffn_bv, L0_ffn_wo, L0_ffn_w_gate, L0_ffn_w_up, L0_ffn_w_down, L0_ffn_ln1_w, L0_ffn_ln2_w, L1_xattn_Wq, L1_xattn_bq, L1_xattn_Wk, L1_xattn_bk, L1_xattn_Wv, L1_xattn_bv, L1_xattn_Wkv_dca, L1_xattn_bkv_dca, L1_xattn_qn_w, L1_xattn_qn_b, L1_xattn_kn_w, L1_xattn_kn_b, L1_xattn_kn_dca_w, L1_xattn_kn_dca_b, L1_xattn_Wo, L1_xattn_bo, L1_ffn_gate_w, L1_ffn_w_gate, L1_ffn_w_up, L1_ffn_w_down, L1_ffn_sw_gate, L1_ffn_sw_up, L1_ffn_sw_down):
    import jax
    import jax.numpy as jnp

    def _L0_xattn_ref(teacher_logits, teacher_features, Wq, bq, Wk, bk):
        import jax, jax.numpy as jnp
        import numpy as np
        query = jnp.einsum('bnc,dc->bnd', teacher_features, Wq) + bq
        key = jnp.einsum('bnc,dc->bnd', teacher_features, Wk) + bk
        energy = jnp.einsum('bnd,bmd->bnm', query, key)
        attention = jax.nn.softmax(energy, axis=-1)
        x_m = jnp.einsum('bln,bmn->blm', teacher_logits, attention)
        return x_m

    def _L0_ffn_ref(hidden_states, w_router, wq, bq, wk, bk, wv, bv, wo, w_gate, w_up, w_down, ln1_w, ln2_w):
        import jax, jax.numpy as jnp
        import numpy as np
        CAPACITY = 0.125
        HEAD_DIM = 128
        N_HEADS = 16
        N_KV_HEADS = 8
        ROPE_THETA = 10000.0
        EPS = 1e-06

        def _rms_norm(x, w):
            return x * jax.lax.rsqrt(jnp.mean(x * x, axis=-1, keepdims=True) + EPS) * w

        def _rotate_half(t):
            h = t.shape[-1] // 2
            return jnp.concatenate([-t[..., h:], t[..., :h]], axis=-1)
        B, T, D = hidden_states.shape
        k = max(1, int(T * CAPACITY))
        scores = jnp.einsum('btd,d->bt', hidden_states, w_router)
        _, idx = jax.lax.top_k(scores, k)
        idx = jnp.sort(idx, axis=-1)
        b = jnp.arange(B)[:, None]
        sel = hidden_states[b, idx]
        sel_scores = scores[b, idx]
        S = B * k
        x = sel.reshape(S, D)
        pos = idx.reshape(S)
        inv_freq = 1.0 / ROPE_THETA ** (jnp.arange(0, HEAD_DIM, 2, dtype=jnp.float32) / HEAD_DIM)
        ang = pos.astype(jnp.float32)[:, None] * inv_freq
        cos = jnp.concatenate([jnp.cos(ang), jnp.cos(ang)], axis=-1)[:, None, :]
        sin = jnp.concatenate([jnp.sin(ang), jnp.sin(ang)], axis=-1)[:, None, :]
        h = _rms_norm(x, ln1_w)
        q = (h @ wq + bq).reshape(S, N_HEADS, HEAD_DIM)
        kk = (h @ wk + bk).reshape(S, N_KV_HEADS, HEAD_DIM)
        v = (h @ wv + bv).reshape(S, N_KV_HEADS, HEAD_DIM)
        q = q * cos + _rotate_half(q) * sin
        kk = kk * cos + _rotate_half(kk) * sin
        rep = N_HEADS // N_KV_HEADS
        kk = jnp.repeat(kk, rep, axis=1)
        v = jnp.repeat(v, rep, axis=1)
        att = jnp.einsum('shd,thd->hst', q, kk) / np.sqrt(HEAD_DIM)
        causal = jnp.tril(jnp.ones((S, S), bool))
        att = jnp.where(causal[None], att, jnp.finfo(att.dtype).min)
        att = jax.nn.softmax(att, axis=-1)
        attn_out = jnp.einsum('hst,thd->shd', att, v).reshape(S, N_HEADS * HEAD_DIM) @ wo
        x1 = x + attn_out
        h2 = _rms_norm(x1, ln2_w)
        mlp = jax.nn.silu(h2 @ w_gate) * (h2 @ w_up) @ w_down
        processed = x1 + mlp
        gate = jax.nn.sigmoid(sel_scores).reshape(S, 1)
        gated = gate * processed + (1.0 - gate) * x
        output = hidden_states.at[b, idx].set(gated.reshape(B, k, D))
        return output

    def _L1_xattn_ref(x, y, Wq, bq, Wk, bk, Wv, bv, Wkv_dca, bkv_dca, qn_w, qn_b, kn_w, kn_b, kn_dca_w, kn_dca_b, Wo, bo):
        import jax, jax.numpy as jnp
        import numpy as np
        B, S1, S2, DCA = (2, 512, 256, 16)
        QDIM, KDIM, H = (512, 256, 16)
        HD = QDIM // H
        SCALE = HD ** (-0.5)
        EPS = 1e-06
        DCA_WEIGHT = 1.0

        def _ln(t, w, b):
            m = jnp.mean(t, axis=-1, keepdims=True)
            v = jnp.var(t, axis=-1, keepdims=True)
            return (t - m) * jax.lax.rsqrt(v + EPS) * w + b

        def _attn(q, k, v):
            s = jnp.einsum('bhqd,bhkd->bhqk', q, k) * SCALE
            p = jax.nn.softmax(s, axis=-1)
            return jnp.einsum('bhqk,bhkd->bhqd', p, v)
        b, s1, _ = x.shape
        y_dca = y[:, -DCA:, :]
        y_main = y[:, :-DCA, :]
        kv_dca = (y_dca @ Wkv_dca + bkv_dca).reshape(b, DCA, 2, H, HD)
        k_dca = _ln(kv_dca[:, :, 0], kn_dca_w, kn_dca_b)
        v_dca = kv_dca[:, :, 1]
        s2 = y_main.shape[1]
        q = _ln((x @ Wq + bq).reshape(b, s1, H, HD), qn_w, qn_b)
        kv = jnp.concatenate([y_main @ Wk + bk, y_main @ Wv + bv], axis=-1)
        kv = kv.reshape(b, s2, H, 2 * HD)
        k = _ln(kv[..., :HD], kn_w, kn_b)
        v = kv[..., HD:]
        qT = q.transpose(0, 2, 1, 3)
        ctx = _attn(qT, k.transpose(0, 2, 1, 3), v.transpose(0, 2, 1, 3))
        ctx = ctx.transpose(0, 2, 1, 3).reshape(b, s1, QDIM)
        ctx_dca = _attn(qT, k_dca.transpose(0, 2, 1, 3), v_dca.transpose(0, 2, 1, 3))
        ctx_dca = ctx_dca.transpose(0, 2, 1, 3).reshape(b, s1, QDIM)
        ctx = ctx + DCA_WEIGHT * ctx_dca
        return ctx @ Wo + bo

    def _L1_ffn_ref(hidden_states, gate_w, w_gate, w_up, w_down, sw_gate, sw_up, sw_down):
        import jax, jax.numpy as jnp
        import numpy as np
        NUM_EXPERTS = 32
        TOP_K = 6
        N_GROUPS = 4
        N_LIMITED_GROUPS = 2
        B, S, H = hidden_states.shape
        E, K = (NUM_EXPERTS, TOP_K)
        x = hidden_states.reshape(-1, H)
        T = x.shape[0]
        scores = jax.nn.sigmoid(x @ gate_w)
        original_scores = scores
        epg = E // N_GROUPS
        sg = scores.reshape(T, N_GROUPS, epg)
        group_scores = jnp.max(sg, axis=-1)
        _, top_groups = jax.lax.top_k(group_scores, N_LIMITED_GROUPS)
        mask = jnp.ones((T, N_GROUPS), dtype=bool)
        mask = mask.at[jnp.arange(T)[:, None], top_groups].set(False)
        sg = jnp.where(mask[:, :, None], -jnp.inf, sg)
        masked_scores = sg.reshape(T, E)
        _, selected_experts = jax.lax.top_k(masked_scores, K)
        weights = jnp.take_along_axis(original_scores, selected_experts, axis=-1)
        weights = weights / jnp.sum(weights, axis=-1, keepdims=True)
        sel_flat = selected_experts.ravel()
        x_exp = jnp.repeat(x, K, axis=0)
        sort_idx = jnp.argsort(sel_flat)
        xs = x_exp[sort_idx]
        group_sizes = jnp.bincount(sel_flat, length=E).astype(jnp.int32)
        g = jax.lax.ragged_dot(xs, w_gate, group_sizes)
        u = jax.lax.ragged_dot(xs, w_up, group_sizes)
        d = jax.lax.ragged_dot(jax.nn.silu(g) * u, w_down, group_sizes)
        unsort_idx = jnp.argsort(sort_idx)
        out = d[unsort_idx].reshape(T, K, H)
        expert_out = jnp.sum(out * weights[..., None], axis=1)
        shared = jax.nn.silu(x @ sw_gate) * (x @ sw_up) @ sw_down
        return (expert_out + shared).reshape(B, S, H)
    x = x + _L0_xattn_ref(_layernorm(x, axis=-1), ctx_1024, L0_xattn_Wq, L0_xattn_bq, L0_xattn_Wk, L0_xattn_bk)
    x = x + _L0_ffn_ref(_layernorm(x, axis=-1), L0_ffn_w_router, L0_ffn_wq, L0_ffn_bq, L0_ffn_wk, L0_ffn_bk, L0_ffn_wv, L0_ffn_bv, L0_ffn_wo, L0_ffn_w_gate, L0_ffn_w_up, L0_ffn_w_down, L0_ffn_ln1_w, L0_ffn_ln2_w)
    x = x + _L1_xattn_ref(_layernorm(x, axis=-1), ctx_1024, L1_xattn_Wq, L1_xattn_bq, L1_xattn_Wk, L1_xattn_bk, L1_xattn_Wv, L1_xattn_bv, L1_xattn_Wkv_dca, L1_xattn_bkv_dca, L1_xattn_qn_w, L1_xattn_qn_b, L1_xattn_kn_w, L1_xattn_kn_b, L1_xattn_kn_dca_w, L1_xattn_kn_dca_b, L1_xattn_Wo, L1_xattn_bo)
    x = x + _L1_ffn_ref(_layernorm(x, axis=-1), L1_ffn_gate_w, L1_ffn_w_gate, L1_ffn_w_up, L1_ffn_w_down, L1_ffn_sw_gate, L1_ffn_sw_up, L1_ffn_sw_down)
    return x

_drawn_inputs = setup_inputs


def setup_inputs(seed=0):
    import zlib

    import numpy as np

    out = dict(_drawn_inputs(seed))
    spreads = {'L0_xattn_bq': (0.0, 0.1),
     'L0_xattn_bk': (0.0, 2.0),
     'L0_ffn_bq': (0.0, 0.8),
     'L0_ffn_bk': (0.0, 0.8),
     'L0_ffn_bv': (0.0, 0.758),
     'L0_ffn_ln1_w': (1.0, 0.6),
     'L0_ffn_ln2_w': (1.0, 0.6),
     'L1_xattn_bq': (0.0, 0.8),
     'L1_xattn_bk': (0.0, 0.6),
     'L1_xattn_bv': (0.0, 0.566),
     'L1_xattn_bkv_dca': (0.0, 0.4),
     'L1_xattn_qn_w': (1.0, 0.6),
     'L1_xattn_qn_b': (0.0, 0.8),
     'L1_xattn_kn_w': (1.0, 0.6),
     'L1_xattn_kn_b': (0.0, 2.0),
     'L1_xattn_kn_dca_w': (1.0, 0.6),
     'L1_xattn_kn_dca_b': (0.0, 2.0),
     'L1_xattn_bo': (0.0, 0.1)}
    factors = {'L0_ffn_w_router': 3.226,
     'L0_ffn_wq': 8.0,
     'L0_ffn_wk': 8.0,
     'L0_ffn_wv': 5.983,
     'L0_ffn_wo': 4.222,
     'L0_ffn_w_gate': 4.997,
     'L0_ffn_w_up': 4.906,
     'L0_ffn_w_down': 4.886,
     'L1_xattn_Wq': 2.766,
     'L1_ffn_gate_w': 8.0,
     'L1_ffn_w_gate': 7.812,
     'L1_ffn_w_up': 7.679,
     'L1_ffn_w_down': 7.676,
     'L1_ffn_sw_gate': 8.0,
     'L1_ffn_sw_up': 8.0,
     'L1_ffn_sw_down': 8.0}
    for name, (base, spread) in spreads.items():
        noise = np.random.default_rng([zlib.crc32(name.encode()), seed]).standard_normal(out[name].shape)
        drawn = base * np.exp(spread * noise) if base else spread * noise
        out[name] = jnp.asarray(drawn.astype(out[name].dtype))
    for name, factor in factors.items():
        out[name] = (out[name] * factor).astype(out[name].dtype)
    return out
```

```python
from contextlib import ExitStack

import numpy as np

import concourse.bass as bass
from concourse import mybir

F32 = mybir.dt.float32
I32 = mybir.dt.int32
U32 = mybir.dt.uint32
ALU = mybir.AluOpType
ACT = mybir.ActivationFunctionType
AX = mybir.AxisListType

P = 128
B, S, D = 4, 512, 512
TOK = B * S
NT = TOK // P
JT = S // P
CC = D // P
CTX = 256
KC = CTX // P
LAST_STAGE = 99


class Core:
    pass


def sbuf(nc, stack, name, shape, dt=F32):
    return stack.enter_context(nc.sbuf_tensor(name, shape, dt))


def sems(nc, c, prefix, names):
    made = [nc.alloc_semaphore(prefix + n) for n in names.split()]
    c.of_stage += made
    return made


def end_stage(nc, c):
    with nc.Block() as block:
        @block.gpsimd
        def _(pool):
            nc.clear_and_free_semaphores(c.of_stage)
    c.of_stage = []


class Chain:

    def __init__(self, eng, sem, base=0):
        self.eng, self.sem, self.n, self.base = eng, sem, 0, base

    def link(self, ins):
        self.n += 1
        ins.then_inc(self.sem, 1)
        self.eng.wait_ge(self.sem, self.base + self.n)

    def after_loop(self, times):
        self.n += times
        self.eng.wait_ge(self.sem, self.base + self.n)


def load_constants(nc, c):
    with ExitStack() as stack:
        ctx_rows = sbuf(nc, stack, "ctx_rows", [P, 2, JT, CTX])
        x_loaded, const_loaded, ctx_even, ctx_odd, turned, copied = sems(
            nc, c, "c_", "x_loaded const_loaded ctx_even ctx_odd turned copied")
        ctx_loaded = [ctx_even, ctx_odd]
        block = stack.enter_context(nc.Block())

        @block.sync
        def _(sp):
            sp.dma_start(c.ident[:], c.dram["i_ident"]).then_inc(const_loaded, 16)
            for b in range(B):
                if b >= 2:
                    sp.wait_ge(turned, b - 1)
                sp.dma_start(ctx_rows[:, b % 2], c.dram["ctx_1024"][b].rearrange("(j p) d -> p j d", p=P)).then_inc(
                    ctx_loaded[b % 2], 16)
            sp.dma_start(c.X[:], c.dram["x"].rearrange("b (j p) d -> p (b j) d", p=P)).then_inc(x_loaded, 16)
            sp.wait_ge(x_loaded, 16)

        @block.tensor
        def _(pe):
            pe.wait_ge(const_loaded, 16)
            for b in range(B):
                pe.wait_ge(ctx_loaded[b % 2], 16 * (b // 2 + 1))
                if b >= 2:
                    pe.wait_ge(copied, b - 1)
                for k in range(KC):
                    for j in range(JT):
                        last = nc.tensor.transpose(c.bank[2 * (b % 2) + k][:, j * P:(j + 1) * P],
                                                   ctx_rows[:, b % 2, j, k * P:(k + 1) * P], c.ident[:])
                last.then_inc(turned, 1)

        @block.scalar
        def _(act):
            for b in range(B):
                act.wait_ge(turned, b + 1)
                for k in range(KC):
                    last = nc.scalar.copy(c.ctxT[:, b, k, :], c.bank[2 * (b % 2) + k][:])
                last.then_inc(copied, 1)


def map_attention(nc, c):
    with ExitStack() as stack:
        wq = sbuf(nc, stack, "a_wq", [P, 2, CTX])
        wT = sbuf(nc, stack, "a_wT", [P, 2, KC, P])
        bias = sbuf(nc, stack, "a_bias", [P, 2])
        stats = sbuf(nc, stack, "a_stats", [P, JT, 6])
        mv = sbuf(nc, stack, "a_mv", [P, JT, 2])
        rstd = sbuf(nc, stack, "a_rstd", [P, JT])
        xln = sbuf(nc, stack, "a_xln", [P, JT, D])
        xlnT = sbuf(nc, stack, "a_xlnT", [P, CC, S])
        qkT = sbuf(nc, stack, "a_qkT", [P, 2, S])
        prob = sbuf(nc, stack, "a_prob", [P, JT, S])
        attT = sbuf(nc, stack, "a_attT", [P, CC, S])
        nmax = sbuf(nc, stack, "a_nmax", [P, JT])
        rsum = sbuf(nc, stack, "a_rsum", [P, JT])
        rinv = sbuf(nc, stack, "a_rinv", [P, JT])
        w_loaded, w_turned, w_copied = sems(nc, c, "a_", "w_loaded w_turned w_copied")
        var_ready, rstd_ready, xln_ready, xln_turned, xlnT_ready = sems(
            nc, c, "a_", "var_ready rstd_ready xln_ready xln_turned xlnT_ready")
        qk_ready, qkT_ready, energy_ready, max_ready, exp_ready, prob_ready = sems(
            nc, c, "a_", "qk_ready qkT_ready energy_ready max_ready exp_ready prob_ready")
        prob_turned, attT_ready, mixed, added, dve_chain = sems(
            nc, c, "a_", "prob_turned attT_ready mixed added dve_chain")
        block = stack.enter_context(nc.Block())
        energy_bank = [6, 7, 4, 5]

        @block.sync
        def _(sp):
            sp.dma_start(wq[:, 0], c.dram["L0_xattn_Wq"]).then_inc(w_loaded, 16)
            sp.dma_start(wq[:, 1], c.dram["L0_xattn_Wk"]).then_inc(w_loaded, 16)
            sp.dma_start(bias[:, 0:1], c.dram["L0_xattn_bq"].rearrange("(p a) -> p a", a=1)).then_inc(w_loaded, 16)
            sp.dma_start(bias[:, 1:2], c.dram["L0_xattn_bk"].rearrange("(p a) -> p a", a=1)).then_inc(w_loaded, 16)

        @block.gpsimd
        def _(pool):
            with pool.Fori(0, B) as b:
                pool.wait_ge(var_ready, b + 1)
                nc.gpsimd.tensor_tensor(rstd[:], rstd[:], c.minus_half[:, 0:JT], ALU.pow).then_inc(rstd_ready, 1)

        @block.vector
        def _(dve):
            LINKS = 3
            with dve.Fori(0, B) as b:
                chain = Chain(dve, dve_chain, b * LINKS)
                for j in range(JT):
                    last = nc.vector.bn_stats(stats[:, j, :], c.X[:, bass.ds(b * JT + j, 1), :])
                chain.link(last)
                nc.vector.tensor_copy(rinv[:, 0:1], stats[:, 0, 0:1])
                for j in range(JT):
                    last = nc.vector.bn_aggr(mv[:, j, :], stats[:, j, :])
                chain.link(last)
                nc.vector.tensor_scalar(rstd[:], mv[:, :, 1], 1e-5, None, ALU.add).then_inc(var_ready, 1)
                dve.wait_ge(rstd_ready, b + 1)
                for j in range(JT):
                    last = nc.vector.tensor_scalar(xln[:, j, :], c.X[:, bass.ds(b * JT + j, 1), :],
                                                   mv[:, j, 0:1], rstd[:, j:j + 1], ALU.subtract, ALU.mult)
                last.then_inc(xln_ready, 1)
                for m in range(JT):
                    dve.wait_ge(energy_ready, b * JT + m + 1)
                    nc.vector.reduce_max(nmax[:, m:m + 1], c.bank[energy_bank[m]][:], AX.X,
                                         negate=True).then_inc(max_ready, 1)
                dve.wait_ge(exp_ready, b * JT + JT)
                chain.link(nc.vector.reciprocal(rinv[:], rsum[:]))
                for m in range(JT):
                    last = nc.vector.tensor_scalar(prob[:, m, :], prob[:, m, :], rinv[:, m:m + 1], None, ALU.mult)
                last.then_inc(prob_ready, 1)
                for j in range(JT):
                    dve.wait_ge(mixed, b * JT + j + 1)
                    row = c.X[:, bass.ds(b * JT + j, 1), :]
                    nc.vector.tensor_tensor(row, row, c.bank[4 + j][:].unsqueeze(1), ALU.add).then_inc(added, 1)

        @block.scalar
        def _(act):
            act.wait_ge(w_turned, 1)
            for s in range(2):
                last = nc.scalar.copy(wT[:, s], c.bank[s][:, 0:CTX].rearrange("p (k d) -> p k d", k=KC))
            last.then_inc(w_copied, 1)
            with act.Fori(0, B) as b:
                act.wait_ge(qk_ready, b + 1)
                for s in range(2):
                    last = nc.scalar.activation(qkT[:, s, :], c.bank[4 + s][:], ACT.Identity, bias=bias[:, s:s + 1])
                last.then_inc(qkT_ready, 1)
                act.wait_ge(xln_turned, b + 1)
                for k in range(CC):
                    last = nc.scalar.copy(xlnT[:, k, :], c.bank[k][:])
                last.then_inc(xlnT_ready, 1)
                for m in range(JT):
                    act.wait_ge(max_ready, b * JT + m + 1)
                    nc.scalar.activation(prob[:, m, :], c.bank[energy_bank[m]][:], ACT.Exp, bias=nmax[:, m:m + 1],
                                         accum_out=rsum[:, m:m + 1]).then_inc(exp_ready, 1)
                act.wait_ge(prob_turned, b + 1)
                for k in range(CC):
                    last = nc.scalar.copy(attT[:, k, :], c.bank[k][:])
                last.then_inc(attT_ready, 1)

        @block.tensor
        def _(pe):
            pe.wait_ge(w_loaded, 64)
            for s in range(2):
                for k in range(KC):
                    last = nc.tensor.transpose(c.bank[s][:, k * P:(k + 1) * P], wq[:, s, k * P:(k + 1) * P], c.ident[:])
            last.then_inc(w_turned, 1)
            pe.wait_ge(w_copied, 1)
            with pe.Fori(0, B) as b:
                pe.wait_ge(added, b * JT)
                for s in range(2):
                    for k in range(KC):
                        last = nc.tensor.matmul(c.bank[4 + s][:], wT[:, s, k, :], c.ctxT[:, bass.ds(b, 1), k, :],
                                                start=(k == 0), stop=(k == KC - 1))
                last.then_inc(qk_ready, 1)
                pe.wait_ge(xln_ready, b + 1)
                for k in range(CC):
                    for j in range(JT):
                        last = nc.tensor.transpose(c.bank[k][:, j * P:(j + 1) * P], xln[:, j, k * P:(k + 1) * P],
                                                   c.ident[:])
                last.then_inc(xln_turned, 1)
                pe.wait_ge(qkT_ready, b + 1)
                for m in range(JT):
                    nc.tensor.matmul(c.bank[energy_bank[m]][:], qkT[:, 0, m * P:(m + 1) * P], qkT[:, 1, :],
                                     start=True, stop=True).then_inc(energy_ready, 1)
                pe.wait_ge(xlnT_ready, b + 1)
                pe.wait_ge(prob_ready, b + 1)
                for k in range(CC):
                    for m in range(JT):
                        last = nc.tensor.transpose(c.bank[k][:, m * P:(m + 1) * P], prob[:, m, k * P:(k + 1) * P],
                                                   c.ident[:])
                last.then_inc(prob_turned, 1)
                pe.wait_ge(attT_ready, b + 1)
                for j in range(JT):
                    for k in range(CC):
                        last = nc.tensor.matmul(c.bank[4 + j][:], xlnT[:, k, j * P:(j + 1) * P], attT[:, k, :],
                                                start=(k == 0), stop=(k == CC - 1))
                    last.then_inc(mixed, 1)


def norm_rows_into(nc, dve, chain, c, stats, mv, rstd, var_ready, rstd_ready, eps):
    with dve.Fori(0, B) as b:
        for j in range(JT):
            t = bass.ds(b * JT + j, 1)
            last = nc.vector.bn_stats(stats[:, t, :], c.X[:, t, :])
        last.then_inc(chain.sem, 1)
    chain.after_loop(B)
    for t in range(NT):
        last = nc.vector.bn_aggr(mv[:, t, :], stats[:, t, :])
    chain.link(last)
    nc.vector.tensor_scalar(rstd[:], mv[:, :, 1], eps, None, ALU.add).then_inc(var_ready, 1)
    dve.wait_ge(rstd_ready, 1)


def token_choice_ffn(nc, c):
    CAP = S // 8
    GROUPS = B * CAP // P
    DH = 128
    HALF = DH // 2
    KVH = 8
    QH = 2
    HEAD_COLS = (QH + 2) * DH
    SLOTS = GROUPS * P
    INNER = 2048
    with ExitStack() as kept:
        slot_hot_T = sbuf(nc, kept, "b_slot_hot_T", [P, NT, P])
        picked = sbuf(nc, kept, "b_picked", [P, GROUPS, D])
        x1 = sbuf(nc, kept, "b_x1", [P, GROUPS, D])
        angle = sbuf(nc, kept, "b_angle", [P, GROUPS, 3, HALF])
        gate = sbuf(nc, kept, "b_gate", [P, GROUPS])
        hT = sbuf(nc, kept, "b_hT", [P, CC, SLOTS])
        ln_w = sbuf(nc, kept, "b_ln_w", [P, 2, CC])

        with ExitStack() as stack:
            hs = sbuf(nc, stack, "b_hs", [P, NT, D])
            stats = sbuf(nc, stack, "b_stats", [P, NT, 6])
            mv = sbuf(nc, stack, "b_mv", [P, NT, 2])
            rstd = sbuf(nc, stack, "b_rstd", [P, NT])
            w_router = sbuf(nc, stack, "b_w_router", [P, D])
            score = sbuf(nc, stack, "b_score", [P, NT])
            score_T = sbuf(nc, stack, "b_score_T", [NT, P])
            scores_of_batch = sbuf(nc, stack, "b_scores_of_batch", [P, B, S])
            before = sbuf(nc, stack, "b_before", [P, JT, S])
            tri = sbuf(nc, stack, "b_tri", [P, P])
            ones = sbuf(nc, stack, "b_ones", [P, P])
            iota = sbuf(nc, stack, "b_iota", [P, P])
            slot_base = sbuf(nc, stack, "b_slot_base", [P, NT])
            rope = sbuf(nc, stack, "b_rope", [P, JT, DH])
            above = sbuf(nc, stack, "b_above", [P, NT])
            equal = sbuf(nc, stack, "b_equal", [P, NT])
            chosen = sbuf(nc, stack, "b_chosen", [P, NT])
            chosen_before = sbuf(nc, stack, "b_chosen_before", [P, NT])
            slot = sbuf(nc, stack, "b_slot", [P, NT])
            slot_hot = sbuf(nc, stack, "b_slot_hot", [P, NT, P])
            loaded, var_ready, rstd_ready, score_ready, score_turned, score_T_ready, score_stored, scores_spread = sems(
                nc, c, "b_", "loaded var_ready rstd_ready score_ready score_turned score_T_ready score_stored scores_spread")
            chosen_ready, slot_counted, hot_ready, gathered, hot_turned, chain_dve, gate_ready, gate_exp = sems(
                nc, c, "b_", "chosen_ready slot_counted hot_ready gathered hot_turned chain_dve gate_ready gate_exp")
            block = stack.enter_context(nc.Block())

            @block.sync
            def _(sp):
                for dst, src in ((w_router[:], c.dram["L0_ffn_w_router"].partition_broadcast(P)), (before[:], c.dram["i_before"]),
                                 (tri[:], c.dram["i_tri"]), (iota[:], c.dram["i_iota"]), (slot_base[:], c.dram["i_slot_base"]),
                                 (rope[:], c.dram["i_rope"].rearrange("(j p) d -> p j d", p=P)),
                                 (ln_w[:, 0], c.dram["L0_ffn_ln1_w"].rearrange("(k p) -> p k", p=P)),
                                 (ln_w[:, 1], c.dram["L0_ffn_ln2_w"].rearrange("(k p) -> p k", p=P))):
                    sp.dma_start(dst, src, allow_slow_non_contiguous=True).then_inc(loaded, 16)
                sp.wait_ge(score_T_ready, 1)
                sp.dma_start(c.dram["d_scores"], score_T[:]).then_inc(score_stored, 16)
                sp.wait_ge(score_stored, 16)
                sp.dma_start(scores_of_batch[:], c.dram["d_scores"].rearrange("(b j) p -> (b j p)", b=B).partition_broadcast(P)
                             .rearrange("q (b s) -> q b s", b=B)).then_inc(scores_spread, 16)

            @block.gpsimd
            def _(pool):
                nc.gpsimd.memset(ones[:], 1.0)
                pool.wait_ge(var_ready, 1)
                nc.gpsimd.tensor_tensor(rstd[:], rstd[:], c.minus_half[:, 0:NT], ALU.pow).then_inc(rstd_ready, 1)

            @block.vector
            def _(dve):
                chain = Chain(dve, chain_dve)
                dve.wait_ge(loaded, 8 * 16)
                norm_rows_into(nc, dve, chain, c, stats, mv, rstd, var_ready, rstd_ready, 1e-5)
                first = chain.n
                with dve.Fori(0, B) as b:
                    tiles = [bass.ds(b * JT + j, 1) for j in range(JT)]
                    for t in tiles:
                        last = nc.vector.tensor_scalar(hs[:, t, :], c.X[:, t, :], mv[:, t, 0:1], rstd[:, t],
                                                       ALU.subtract, ALU.mult)
                    last.then_inc(chain_dve, 1)
                    dve.wait_ge(chain_dve, b + first + 1)
                    for j, t in enumerate(tiles):
                        nc.vector.scalar_tensor_tensor(c.bank[4 + j][:].unsqueeze(1), hs[:, t, :], 1.0,
                                                       w_router[:].unsqueeze(1), ALU.mult, ALU.mult,
                                                       accum_out=score[:, t])
                        last = nc.vector.tensor_tensor(c.X[:, t, :], c.X[:, t, :], hs[:, t, :], ALU.add)
                    last.then_inc(score_ready, 1)
                chain.n += B
                dve.wait_ge(score_turned, 1)
                nc.vector.tensor_copy(score_T[:], c.bank[0][0:NT, 0:P]).then_inc(score_T_ready, 1)
                dve.wait_ge(score_T_ready, 1)
                dve.wait_ge(scores_spread, 16)
                first = chain.n
                with dve.Fori(0, B) as b:
                    dve.wait_ge(chain_dve, b + first)
                    of_batch = scores_of_batch[:, bass.ds(b, 1), :]
                    for j in range(JT):
                        t = bass.ds(b * JT + j, 1)
                        nc.vector.tensor_scalar(c.bank[j][:].unsqueeze(1), of_batch, score[:, t], None, ALU.is_gt,
                                                ALU.add, accum_out=above[:, t])
                        last = nc.vector.scalar_tensor_tensor(c.bank[4 + j][:].unsqueeze(1), of_batch, score[:, t],
                                                              before[:, j:j + 1, :], ALU.is_equal, ALU.mult,
                                                              accum_out=equal[:, t])
                    last.then_inc(chain_dve, 1)
                chain.after_loop(B)
                chain.link(nc.vector.tensor_tensor(above[:], above[:], equal[:], ALU.add))
                chain.link(nc.vector.tensor_scalar(chosen[:], above[:], float(CAP), None, ALU.is_lt))
                of = lambda tile, j: tile[:].rearrange("p (b j) -> p b j", j=JT)[:, :, j]
                chain.link(nc.vector.memset(chosen_before[:], 0.0))
                for j in range(1, JT):
                    last = nc.vector.tensor_tensor(of(chosen_before, j), of(chosen_before, j - 1), of(chosen, j - 1), ALU.add)
                    if j < JT - 1:
                        chain.link(last)
                last.then_inc(chosen_ready, 1)
                dve.wait_ge(slot_counted, 1)
                chain.link(nc.vector.tensor_tensor(slot[:], c.bank[1][:, 0:NT], slot_base[:], ALU.add))
                chain.link(nc.vector.tensor_tensor(slot[:], slot[:], chosen[:], ALU.mult))
                chain.link(nc.vector.tensor_scalar(slot[:], slot[:], -1.0, None, ALU.add))
                nc.vector.tensor_tensor(slot_hot[:], iota[:].unsqueeze(1).broadcast_to((P, NT, P)),
                                        slot[:].unsqueeze(2).broadcast_to((P, NT, P)), ALU.is_equal).then_inc(hot_ready, 1)
                dve.wait_ge(gathered, 1)
                for g in range(GROUPS):
                    last = nc.vector.tensor_copy(gate[:, g:g + 1], c.bank[2 + g][:, DH:DH + 1])
                last.then_inc(gate_ready, 1)
                for g in range(GROUPS):
                    nc.vector.tensor_copy(picked[:, g, :], c.bank[g][:])
                    nc.vector.tensor_copy(x1[:, g, :], c.bank[g][:])
                    nc.vector.tensor_copy(angle[:, g, 0:2, :], c.bank[2 + g][:, 0:DH].rearrange("p (a d) -> p a d", a=2))
                    nc.vector.tensor_scalar(angle[:, g, 2, :], c.bank[2 + g][:, HALF:DH], -1.0, None, ALU.mult)
                dve.wait_ge(gate_exp, 1)
                chain.link(nc.vector.tensor_scalar(gate[:], gate[:], 1.0, None, ALU.add))
                nc.vector.reciprocal(gate[:], gate[:])

            @block.scalar
            def _(act):
                act.wait_ge(gate_ready, 1)
                nc.scalar.activation(gate[:], gate[:], ACT.Exp, scale=-1.0).then_inc(gate_exp, 1)
                act.wait_ge(hot_turned, 1)
                for q in range(4):
                    nc.scalar.copy(slot_hot_T[:, 4 * q:4 * q + 4, :], c.bank[4 + q][:].rearrange("p (t s) -> p t s", t=4))

            @block.tensor
            def _(pe):
                pe.wait_ge(score_ready, B)
                nc.tensor.transpose(c.bank[0][0:NT, 0:P], score[:], c.ident[:]).then_inc(score_turned, 1)
                pe.wait_ge(chosen_ready, 1)
                nc.tensor.matmul(c.bank[1][:, 0:NT], tri[:], chosen[:], start=True, stop=False)
                nc.tensor.matmul(c.bank[1][:, 0:NT], ones[:], chosen_before[:], start=False, stop=True).then_inc(slot_counted, 1)
                pe.wait_ge(hot_ready, 1)
                per = NT // GROUPS
                for g in range(GROUPS):
                    for n in range(per):
                        t = g * per + n
                        nc.tensor.matmul(c.bank[g][:], slot_hot[:, t, :], hs[:, t, :], start=(n == 0), stop=(n == per - 1))
                    for n in range(per):
                        t = g * per + n
                        nc.tensor.matmul(c.bank[2 + g][:, 0:DH], slot_hot[:, t, :], rope[:, t % JT, :],
                                         start=(n == 0), stop=(n == per - 1))
                    for n in range(per):
                        t = g * per + n
                        last = nc.tensor.matmul(c.bank[2 + g][:, DH:DH + 1], slot_hot[:, t, :], score[:, t:t + 1],
                                                start=(n == 0), stop=(n == per - 1))
                last.then_inc(gathered, 1)
                for t in range(NT):
                    last = nc.tensor.transpose(c.bank[4 + t // 4][:, (t % 4) * P:(t % 4 + 1) * P], slot_hot[:, t, :], c.ident[:])
                last.then_inc(hot_turned, 1)

        def rms_turned(stack, pre, row, sq, which):
            ms = sbuf(nc, stack, pre + "ms", [P, GROUPS])
            squared, ms_ready, r_ready, row_ready, turned, hT_ready, chained = sems(
                nc, c, pre, "squared ms_ready r_ready row_ready turned hT_ready chained")

            def on_act(act):
                for g in range(GROUPS):
                    nc.scalar.activation(sq[:, g, :], row[:, g, :], ACT.Square, accum_out=ms[:, g:g + 1]).then_inc(squared, 1)
                act.wait_ge(turned, 1)
                for k in range(CC):
                    last = nc.scalar.mul(hT[:, k, :], c.bank[k // 2][:, (k % 2) * SLOTS:(k % 2 + 1) * SLOTS], ln_w[:, which, k:k + 1])
                last.then_inc(hT_ready, 1)

            def on_dve(dve):
                dve.wait_ge(squared, GROUPS)
                nc.vector.tensor_scalar(ms[:], ms[:], 1.0 / D, 1e-6, ALU.mult, ALU.add).then_inc(ms_ready, 1)
                dve.wait_ge(r_ready, 1)
                for g in range(GROUPS):
                    last = nc.vector.tensor_scalar(sq[:, g, :], row[:, g, :], ms[:, g:g + 1], None, ALU.mult)
                last.then_inc(row_ready, 1)

            def on_pool(pool):
                pool.wait_ge(ms_ready, 1)
                nc.gpsimd.tensor_tensor(ms[:], ms[:], c.minus_half[:, 0:GROUPS], ALU.pow).then_inc(r_ready, 1)

            def on_pe(pe):
                pe.wait_ge(row_ready, 1)
                for k in range(CC):
                    for g in range(GROUPS):
                        last = nc.tensor.transpose(c.bank[k // 2][:, (k % 2) * SLOTS + g * P:(k % 2) * SLOTS + (g + 1) * P],
                                                   sq[:, g, k * P:(k + 1) * P], c.ident[:])
                last.then_inc(turned, 1)
                pe.wait_ge(hT_ready, 1)

            return on_act, on_dve, on_pool, on_pe

        with ExitStack() as stack:
            w_heads = sbuf(nc, stack, "b_w_heads", [P, CC, KVH, HEAD_COLS])
            w_o = sbuf(nc, stack, "b_w_o", [P, KVH * QH, D])
            bias = sbuf(nc, stack, "b_bias", [P, KVH, HEAD_COLS])
            causal = sbuf(nc, stack, "b_causal", [P, GROUPS * SLOTS])
            qkv = sbuf(nc, stack, "b_qkv", [P, GROUPS, HEAD_COLS])
            turn = sbuf(nc, stack, "b_turn", [P, GROUPS, QH + 1, DH])
            qk = sbuf(nc, stack, "b_qk", [P, GROUPS, QH + 1, DH])
            qT = sbuf(nc, stack, "b_qT", [P, QH, SLOTS])
            kT = sbuf(nc, stack, "b_kT", [P, SLOTS])
            prob = sbuf(nc, stack, "b_prob", [P, QH, GROUPS * SLOTS])
            probT = sbuf(nc, stack, "b_probT", [P, GROUPS, QH * SLOTS])
            oT = sbuf(nc, stack, "b_oT", [P, QH * SLOTS])
            nmax = sbuf(nc, stack, "b_nmax", [P, QH * GROUPS])
            rsum = sbuf(nc, stack, "b_rsum", [P, QH * GROUPS])
            heads_loaded, wo_loaded, bias_loaded, projected, biased_ready, qk_ready, qk_turned, qkT_ready = sems(
                nc, c, "b_", "heads_loaded wo_loaded bias_loaded projected biased_ready qk_ready qk_turned qkT_ready")
            scored, max_ready, exp_ready, prob_ready, prob_turned, probT_ready, valued, oT_ready, out_ready, added, chain_dve = sems(
                nc, c, "b_", "scored max_ready exp_ready prob_ready prob_turned probT_ready valued oT_ready out_ready added chain2")
            block = stack.enter_context(nc.Block())
            rms_act, rms_dve, rms_pool, rms_pe = rms_turned(stack, "b_r1_", picked, qkv, 0)
            SCALE = DH ** -0.5

            @block.sync
            def _(sp):
                for k in range(CC):
                    rows = slice(k * P, (k + 1) * P)
                    for src, at, cols in ((c.dram["L0_ffn_wq"], 0, QH * DH), (c.dram["L0_ffn_wk"], QH * DH, DH),
                                          (c.dram["L0_ffn_wv"], (QH + 1) * DH, DH)):
                        sp.dma_start(w_heads[:, k, :, at:at + cols],
                                     src[rows, :].rearrange("p (h n) -> p h n", n=cols)).then_inc(heads_loaded, 16)
                for src, at, cols in ((c.dram["L0_ffn_bq"], 0, QH * DH), (c.dram["L0_ffn_bk"], QH * DH, DH),
                                      (c.dram["L0_ffn_bv"], (QH + 1) * DH, DH)):
                    sp.dma_start(bias[:, :, at:at + cols],
                                 src.partition_broadcast(P).rearrange("p (h n) -> p h n", n=cols)).then_inc(bias_loaded, 16)
                sp.dma_start(causal[:], c.dram["i_causal"]).then_inc(bias_loaded, 16)
                sp.dma_start(w_o[:], c.dram["L0_ffn_wo"].rearrange("(h d) n -> d h n", d=DH)).then_inc(wo_loaded, 16)

            @block.gpsimd
            def _(pool):
                rms_pool(pool)

            @block.vector
            def _(dve):
                rms_dve(dve)
                dve.wait_ge(bias_loaded, 4 * 16)
                LINKS = 3
                with dve.Fori(0, KVH) as h:
                    chain = Chain(dve, chain_dve, h * LINKS)
                    dve.wait_ge(projected, h + 1)
                    for g in range(GROUPS):
                        last = nc.vector.tensor_tensor(qkv[:, g:g + 1, :], c.bank[g][:].unsqueeze(1),
                                                       bias[:, bass.ds(h, 1), :], ALU.add)
                    last.then_inc(biased_ready, 1)
                    dve.wait_ge(biased_ready, h + 1)
                    whole = qkv[:, :, 0:(QH + 1) * DH].rearrange("p g (n d) -> p g n d", d=HALF)
                    cos = angle[:, :, 0:1, :].broadcast_to((P, GROUPS, 2 * (QH + 1), HALF))
                    nc.vector.tensor_tensor(qk[:].rearrange("p g h (a d) -> p g (h a) d", a=2), whole, cos, ALU.mult)
                    for half, which in ((0, 2), (1, 1)):
                        other = qkv[:, :, 0:(QH + 1) * DH].rearrange("p g (h a d) -> p g h a d", a=2, d=HALF)[:, :, :, 1 - half, :]
                        sin = angle[:, :, which:which + 1, :].broadcast_to((P, GROUPS, QH + 1, HALF))
                        last = nc.vector.tensor_tensor(turn[:, :, :, half * HALF:(half + 1) * HALF], other, sin, ALU.mult)
                    chain.link(last)
                    nc.vector.tensor_tensor(qk[:], qk[:], turn[:], ALU.add).then_inc(qk_ready, 1)
                    dve.wait_ge(scored, h + 1)
                    for q in range(QH):
                        last = nc.vector.scalar_tensor_tensor(prob[:, q, :], c.bank[4 + q][:], SCALE, causal[:], ALU.mult, ALU.add)
                    chain.link(last)
                    nc.vector.reduce_max(nmax[:], prob[:].rearrange("p q (g s) -> p (q g) s", g=GROUPS), AX.X,
                                         negate=True).then_inc(max_ready, 1)
                    dve.wait_ge(exp_ready, h + 1)
                    chain.link(nc.vector.reciprocal(rsum[:], rsum[:]))
                    flat = prob[:].rearrange("p q (g s) -> p (q g) s", g=GROUPS)
                    nc.vector.tensor_tensor(flat, flat, rsum[:].unsqueeze(2).broadcast_to((P, QH * GROUPS, SLOTS)),
                                            ALU.mult).then_inc(prob_ready, 1)
                    dve.wait_ge(out_ready, h + 1)
                    for g in range(GROUPS):
                        last = nc.vector.tensor_tensor(x1[:, g, :], x1[:, g, :], c.bank[6 + g][:], ALU.add)
                    last.then_inc(added, 1)

            @block.scalar
            def _(act):
                rms_act(act)
                with act.Fori(0, KVH) as h:
                    act.wait_ge(qk_turned, h + 1)
                    nc.scalar.copy(qT[:].rearrange("p q s -> p (q s)"), c.bank[2][:])
                    nc.scalar.copy(kT[:], c.bank[3][:, 0:SLOTS]).then_inc(qkT_ready, 1)
                    act.wait_ge(max_ready, h + 1)
                    for n in range(QH * GROUPS):
                        q, g = divmod(n, GROUPS)
                        part = prob[:, q, g * SLOTS:(g + 1) * SLOTS]
                        last = nc.scalar.activation(part, part, ACT.Exp, bias=nmax[:, n:n + 1], accum_out=rsum[:, n:n + 1])
                    last.then_inc(exp_ready, 1)
                    act.wait_ge(prob_turned, h + 1)
                    for n in range(GROUPS):
                        last = nc.scalar.copy(probT[:, n, :], c.bank[n][:])
                    last.then_inc(probT_ready, 1)
                    act.wait_ge(valued, h + 1)
                    nc.scalar.copy(oT[:], c.bank[2][:]).then_inc(oT_ready, 1)

            @block.tensor
            def _(pe):
                rms_pe(pe)
                pe.wait_ge(heads_loaded, 3 * CC * 16)
                pe.wait_ge(wo_loaded, 16)
                with pe.Fori(0, KVH) as h:
                    for g in range(GROUPS):
                        for k in range(CC):
                            last = nc.tensor.matmul(c.bank[g][:], hT[:, k, g * P:(g + 1) * P], w_heads[:, k, bass.ds(h, 1), :],
                                                    start=(k == 0), stop=(k == CC - 1))
                    last.then_inc(projected, 1)
                    pe.wait_ge(qk_ready, h + 1)
                    for g in range(GROUPS):
                        for q in range(QH):
                            nc.tensor.transpose(c.bank[2][:, q * SLOTS + g * P:q * SLOTS + (g + 1) * P], qk[:, g, q, :], c.ident[:])
                        last = nc.tensor.transpose(c.bank[3][:, g * P:(g + 1) * P], qk[:, g, QH, :], c.ident[:])
                    last.then_inc(qk_turned, 1)
                    pe.wait_ge(qkT_ready, h + 1)
                    for q in range(QH):
                        for g in range(GROUPS):
                            last = nc.tensor.matmul(c.bank[4 + q][:, g * SLOTS:(g + 1) * SLOTS], qT[:, q, g * P:(g + 1) * P],
                                                    kT[:], start=True, stop=True)
                    last.then_inc(scored, 1)
                    pe.wait_ge(prob_ready, h + 1)
                    for q in range(QH):
                        for g in range(GROUPS):
                            for n in range(GROUPS):
                                last = nc.tensor.transpose(c.bank[n][:, q * SLOTS + g * P:q * SLOTS + (g + 1) * P],
                                                           prob[:, q, g * SLOTS + n * P:g * SLOTS + (n + 1) * P], c.ident[:])
                    last.then_inc(prob_turned, 1)
                    pe.wait_ge(probT_ready, h + 1)
                    for n in range(GROUPS):
                        last = nc.tensor.matmul(c.bank[2][:], qkv[:, n, (QH + 1) * DH:(QH + 2) * DH], probT[:, n, :],
                                                start=(n == 0), stop=(n == GROUPS - 1))
                    last.then_inc(valued, 1)
                    pe.wait_ge(oT_ready, h + 1)
                    pe.wait_ge(added, h)
                    for g in range(GROUPS):
                        for q in range(QH):
                            last = nc.tensor.matmul(c.bank[6 + g][:], oT[:, q * SLOTS + g * P:q * SLOTS + (g + 1) * P],
                                                    w_o[:, bass.ds(h * QH + q, 1), :], start=(q == 0), stop=(q == QH - 1))
                    last.then_inc(out_ready, 1)

        with ExitStack() as stack:
            PARTS = INNER // 512
            w_gate = sbuf(nc, stack, "b_w_gate", [P, CC, INNER])
            w_up = sbuf(nc, stack, "b_w_up", [P, CC, INNER])
            w_down = sbuf(nc, stack, "b_w_down", [P, INNER // P, D])
            act_g = sbuf(nc, stack, "b_act_g", [P, GROUPS, 512])
            mid = sbuf(nc, stack, "b_mid", [P, GROUPS, 512])
            midT = sbuf(nc, stack, "b_midT", [P, GROUPS, 512])
            gu_loaded, down_loaded, gated, silu_ready, mid_ready, mid_turned, midT_ready, out_ready, added = sems(
                nc, c, "b_", "gu_loaded down_loaded gated silu_ready mid_ready mid_turned midT_ready mlp_ready mlp_added")
            chain_dve, diff_ready, spread, landed = sems(nc, c, "b_", "chain3 diff_ready spread landed")
            block = stack.enter_context(nc.Block())
            rms_act, rms_dve, rms_pool, rms_pe = rms_turned(stack, "b_r2_", x1, mid, 1)

            @block.sync
            def _(sp):
                for dst, src in ((w_gate, c.dram["L0_ffn_w_gate"]), (w_up, c.dram["L0_ffn_w_up"])):
                    sp.dma_start(dst[:], src.rearrange("(k p) n -> p k n", p=P)).then_inc(gu_loaded, 16)
                sp.dma_start(w_down[:], c.dram["L0_ffn_w_down"].rearrange("(k p) n -> p k n", p=P)).then_inc(down_loaded, 16)

            @block.gpsimd
            def _(pool):
                rms_pool(pool)

            @block.vector
            def _(dve):
                rms_dve(dve)
                with dve.Fori(0, PARTS) as n:
                    dve.wait_ge(silu_ready, n + 1)
                    for g in range(GROUPS):
                        last = nc.vector.tensor_tensor(mid[:, g, :], act_g[:, g, :], c.bank[2 + g][:], ALU.mult)
                    last.then_inc(mid_ready, 1)
                    dve.wait_ge(out_ready, n + 1)
                    for g in range(GROUPS):
                        last = nc.vector.tensor_tensor(x1[:, g, :], x1[:, g, :], c.bank[6 + g][:], ALU.add)
                    last.then_inc(added, 1)
                chain = Chain(dve, chain_dve)
                dve.wait_ge(added, PARTS)
                chain.link(nc.vector.tensor_tensor(x1[:], x1[:], picked[:], ALU.subtract))
                for g in range(GROUPS):
                    last = nc.vector.tensor_scalar(x1[:, g, :], x1[:, g, :], gate[:, g:g + 1], None, ALU.mult)
                last.then_inc(diff_ready, 1)
                for t in range(NT):
                    dve.wait_ge(spread, t + 1)
                    nc.vector.tensor_tensor(c.X[:, t, :], c.X[:, t, :], c.bank[t % 8][:], ALU.add).then_inc(landed, 1)

            @block.scalar
            def _(act):
                rms_act(act)
                with act.Fori(0, PARTS) as n:
                    act.wait_ge(gated, n + 1)
                    for g in range(GROUPS):
                        last = nc.scalar.activation(act_g[:, g, :], c.bank[g][:], ACT.Silu)
                    last.then_inc(silu_ready, 1)
                    act.wait_ge(mid_turned, n + 1)
                    for g in range(GROUPS):
                        last = nc.scalar.copy(midT[:, g, :], c.bank[4 + g][:])
                    last.then_inc(midT_ready, 1)

            @block.tensor
            def _(pe):
                rms_pe(pe)
                pe.wait_ge(gu_loaded, 32)
                pe.wait_ge(down_loaded, 16)
                with pe.Fori(0, PARTS) as n:
                    for at, w in ((0, w_gate), (2, w_up)):
                        for g in range(GROUPS):
                            for k in range(CC):
                                last = nc.tensor.matmul(c.bank[at + g][:], hT[:, k, g * P:(g + 1) * P],
                                                        w[:, k, bass.ds(n * 512, 512)], start=(k == 0), stop=(k == CC - 1))
                    last.then_inc(gated, 1)
                    pe.wait_ge(mid_ready, n + 1)
                    for g in range(GROUPS):
                        for k in range(4):
                            last = nc.tensor.transpose(c.bank[4 + g][:, k * P:(k + 1) * P], mid[:, g, k * P:(k + 1) * P], c.ident[:])
                    last.then_inc(mid_turned, 1)
                    pe.wait_ge(midT_ready, n + 1)
                    pe.wait_ge(added, n)
                    for g in range(GROUPS):
                        for k in range(4):
                            last = nc.tensor.matmul(c.bank[6 + g][:], midT[:, g, k * P:(k + 1) * P],
                                                    w_down[:, bass.ds(n * 4 + k, 1), :], start=(k == 0), stop=(k == 3))
                    last.then_inc(out_ready, 1)
                pe.wait_ge(diff_ready, 1)
                for t in range(NT):
                    if t >= 8:
                        pe.wait_ge(landed, t - 7)
                    nc.tensor.matmul(c.bank[t % 8][:], slot_hot_T[:, t, :], x1[:, t // (NT // GROUPS), :],
                                     start=True, stop=True).then_inc(spread, 1)


def context_attention(nc, c):
    H = 16
    HD = D // H
    LAST = 16
    MAIN = S - LAST
    HPC = P // HD
    SCALE = HD ** -0.5
    with ExitStack() as stack:
        w_q = sbuf(nc, stack, "x_w_q", [P, CC, D])
        w_kv = sbuf(nc, stack, "x_w_kv", [P, KC, 2 * D])
        w_last = sbuf(nc, stack, "x_w_last", [P, KC, 2 * D])
        w_o = sbuf(nc, stack, "x_w_o", [P, CC, D])
        b_q = sbuf(nc, stack, "x_b_q", [P, D])
        b_o = sbuf(nc, stack, "x_b_o", [P, D])
        b_kv = sbuf(nc, stack, "x_b_kv", [P, 2 * D])
        b_kv_end = sbuf(nc, stack, "x_b_kv_end", [P, 2 * D])
        head_ln = sbuf(nc, stack, "x_head_ln", [P, 6])
        stats = sbuf(nc, stack, "x_stats", [P, NT, 6])
        mv = sbuf(nc, stack, "x_mv", [P, NT, 2])
        rstd = sbuf(nc, stack, "x_rstd", [P, NT])
        rows = sbuf(nc, stack, "x_rows", [P, JT, D])
        zeros = sbuf(nc, stack, "x_zeros", [P, JT, D])
        rowsT = sbuf(nc, stack, "x_rowsT", [P, CC, S])
        ctx_b = sbuf(nc, stack, "x_ctx_b", [P, KC, S])
        ctx_end = sbuf(nc, stack, "x_ctx_end", [P, KC, P])
        ctx_last = sbuf(nc, stack, "x_ctx_last", [P, KC, P])
        qk = [sbuf(nc, stack, "x_q", [P, JT, D]), sbuf(nc, stack, "x_k", [P, JT, D])]
        sq = sbuf(nc, stack, "x_sq", [P, JT, D])
        v = sbuf(nc, stack, "x_v", [P, JT, D])
        hmean = sbuf(nc, stack, "x_hmean", [P, 2, JT * H])
        hrstd = sbuf(nc, stack, "x_hrstd", [P, 2, JT * H])
        chunk = sbuf(nc, stack, "x_chunk", [P, 2, JT, P])
        qT = sbuf(nc, stack, "x_qT", [P, S])
        kT = sbuf(nc, stack, "x_kT", [P, S])
        prob = sbuf(nc, stack, "x_prob", [P, HPC, S])
        probT = sbuf(nc, stack, "x_probT", [P, HPC, S])
        shifted = sbuf(nc, stack, "x_shifted", [P, HPC, LAST])
        nmax = sbuf(nc, stack, "x_nmax", [P, 2, HPC])
        nmax_scaled = sbuf(nc, stack, "x_nmax_scaled", [P, HPC])
        rsum = sbuf(nc, stack, "x_rsum", [P, HPC])
        rsum_last = sbuf(nc, stack, "x_rsum_last", [P, HPC])
        rinv = sbuf(nc, stack, "x_rinv", [P, 2, HPC])
        mixed = sbuf(nc, stack, "x_mixed", [P, JT, D])
        loaded, var_ready, rstd_ready, rows_ready, rows_turned, rowsT_ready, ctx_ready, q_ready, kv_ready = sems(
            nc, c, "x_", "loaded var_ready rstd_ready rows_ready rows_turned rowsT_ready ctx_ready q_ready kv_ready")
        q_copied, k_copied, hvar_ready, hrstd_ready, centred, squared, chunk_ready, chunk_turned, qkT_ready = sems(
            nc, c, "x_", "q_copied k_copied hvar_ready hrstd_ready centred squared chunk_ready chunk_turned qkT_ready")
        scored, max_ready, exp_ready, last_exp, prob_ready, prob_turned, probT_act, probT_dve = sems(
            nc, c, "x_", "scored max_ready exp_ready last_exp prob_ready prob_turned probT_act probT_dve")
        valued, mixed_ready, mixed_turned, mixedT_ready, out_ready, added, dve_chain, kv_loaded, ln_loaded = sems(
            nc, c, "x_", "valued mixed_ready mixed_turned mixedT_ready out_ready added dve_chain kv_loaded ln_loaded")
        k_used, zeroed, zeros_set, zeros_stored = sems(nc, c, "x_", "k_used zeroed zeros_set zeros_stored")
        block = stack.enter_context(nc.Block())

        @block.sync
        def _(sp):
            end = slice(P - LAST, P)
            as_kv = lambda tile: tile.rearrange("p (h a d) -> p h a d", a=2, d=HD)
            for dst, src in (
                    (w_q[:], c.dram["L1_xattn_Wq"].rearrange("(k p) n -> p k n", p=P)),
                    (w_kv[:, :, 0:D], c.dram["L1_xattn_Wk"].rearrange("(k p) n -> p k n", p=P)),
                    (w_kv[:, :, D:2 * D], c.dram["L1_xattn_Wv"].rearrange("(k p) n -> p k n", p=P)),
                    (w_last[:], c.dram["L1_xattn_Wkv_dca"].rearrange("(k p) n -> p k n", p=P)),
                    (w_o[:], c.dram["L1_xattn_Wo"].rearrange("(k p) n -> p k n", p=P)),
                    (b_q[:], c.dram["L1_xattn_bq"].partition_broadcast(P)),
                    (b_o[:], c.dram["L1_xattn_bo"].partition_broadcast(P))):
                sp.dma_start(dst, src).then_inc(loaded, 16)
            for tile, n in ((b_kv, P), (b_kv_end, P - LAST)):
                sp.dma_start(tile[0:n, 0:D], c.dram["L1_xattn_bk"].partition_broadcast(n)).then_inc(kv_loaded, 16)
                sp.dma_start(tile[0:n, D:2 * D], c.dram["L1_xattn_bv"].partition_broadcast(n)).then_inc(kv_loaded, 16)
            for a in range(2):
                sp.dma_start(as_kv(b_kv_end[end, :])[:, :, a, :],
                             c.dram["L1_xattn_bkv_dca"][a * D:(a + 1) * D].partition_broadcast(LAST)
                             .rearrange("p (h d) -> p h d", d=HD)).then_inc(kv_loaded, 16)
            for n, src in enumerate((c.dram["L1_xattn_qn_w"], c.dram["L1_xattn_qn_b"], c.dram["L1_xattn_kn_w"], c.dram["L1_xattn_kn_b"],
                                     c.dram["L1_xattn_kn_dca_w"], c.dram["L1_xattn_kn_dca_b"])):
                for h in range(HPC):
                    sp.dma_start(head_ln[h * HD:(h + 1) * HD, n:n + 1],
                                 src.rearrange("(p a) -> p a", a=1)).then_inc(ln_loaded, 16)
            sp.wait_ge(zeros_set, 1)
            blank = c.dram["d_sorted"].rearrange("(n j p) d -> n p j d", p=P, j=JT)
            for n in range(ROUTED_TILES // JT):
                sp.dma_start(blank[n], zeros[:]).then_inc(zeros_stored, 16)
            sp.wait_ge(zeros_stored, 16 * (ROUTED_TILES // JT))

        @block.gpsimd
        def _(pool):
            nc.gpsimd.memset(zeros[:], 0.0).then_inc(zeros_set, 1)
            nc.gpsimd.memset(ctx_end[:, :, P - LAST:P], 0.0)
            nc.gpsimd.memset(ctx_last[:, :, 0:P - LAST], 0.0).then_inc(zeroed, 1)
            pool.wait_ge(var_ready, 1)
            nc.gpsimd.tensor_tensor(rstd[:], rstd[:], c.minus_half[:, 0:NT], ALU.pow).then_inc(rstd_ready, 1)
            with pool.Fori(0, 2 * B) as n:
                pool.wait_ge(hvar_ready, n + 1)
                one = hrstd[:, bass.ds(n % 2, 1), :]
                nc.gpsimd.tensor_tensor(one, one, c.minus_half[:, 0:JT * H].unsqueeze(1), ALU.pow).then_inc(hrstd_ready, 1)

        @block.vector
        def _(dve):
            chain = Chain(dve, dve_chain)
            norm_rows_into(nc, dve, chain, c, stats, mv, rstd, var_ready, rstd_ready, 1e-5)
            dve.wait_ge(loaded, 7 * 16)
            dve.wait_ge(kv_loaded, 6 * 16)
            HEAD_LINKS, INNER_LINKS = 6, 4 * JT
            start = chain.n
            with dve.Fori(0, B) as b:
                outer = Chain(dve, dve_chain, b * (HEAD_LINKS + CC * INNER_LINKS) + start)
                for j in range(JT):
                    t = bass.ds(b * JT + j, 1)
                    last = nc.vector.tensor_scalar(rows[:, j:j + 1, :], c.X[:, t, :], mv[:, t, 0:1], rstd[:, t],
                                                   ALU.subtract, ALU.mult)
                last.then_inc(rows_ready, 1)
                for j in range(JT):
                    t = bass.ds(b * JT + j, 1)
                    nc.vector.tensor_tensor(c.X[:, t, :], c.X[:, t, :], b_o[:].unsqueeze(1), ALU.add)
                for a, (tile, ready) in enumerate(((qk[1], kv_ready), (qk[0], q_ready))):
                    for j in range(JT):
                        dve.wait_ge(ready, b * JT + j + 1)
                        if a == 0:
                            by_head = (b_kv if j < JT - 1 else b_kv_end)[:].rearrange("p (h a d) -> p h a d", a=2, d=HD)
                            nc.vector.tensor_tensor(v[:, j, :].rearrange("p (h d) -> p h d", d=HD),
                                                    c.bank[2 * (j % 2) + 1].rearrange("p (h d) -> p h d", d=HD),
                                                    by_head[:, :, 1, :], ALU.add)
                            nc.vector.tensor_tensor(tile[:, j, :].rearrange("p (h d) -> p h d", d=HD),
                                                    c.bank[2 * (j % 2)].rearrange("p (h d) -> p h d", d=HD),
                                                    by_head[:, :, 0, :], ALU.add).then_inc(k_copied, 1)
                        else:
                            nc.vector.tensor_tensor(tile[:, j, :], c.bank[4 + j], b_q[:], ALU.add).then_inc(q_copied, 1)
                    heads = tile[:].rearrange("p j (h d) -> p (j h) d", d=HD)
                    if a == 0:
                        dve.wait_ge(k_copied, b * JT + JT)
                    else:
                        dve.wait_ge(q_copied, b * JT + JT)
                    outer.link(nc.vector.reduce_sum(hmean[:, a, :], heads, AX.X))
                    outer.link(nc.vector.tensor_scalar(hmean[:, a, :], hmean[:, a, :], 1.0 / HD, None, ALU.mult))
                    nc.vector.tensor_tensor(heads, heads, hmean[:, a, :].unsqueeze(2).broadcast_to((P, JT * H, HD)),
                                            ALU.subtract).then_inc(centred, 1)
                    dve.wait_ge(squared, 2 * b + a + 1)
                    outer.link(nc.vector.reduce_sum(hrstd[:, a, :], sq[:].rearrange("p j (h d) -> p (j h) d", d=HD), AX.X))
                    nc.vector.tensor_scalar(hrstd[:, a, :], hrstd[:, a, :], 1.0 / HD, 1e-6, ALU.mult, ALU.add).then_inc(hvar_ready, 1)
                assert outer.n == HEAD_LINKS
                with dve.Fori(0, CC) as hc:
                    step = b * CC + hc
                    chain = Chain(dve, dve_chain, b * (HEAD_LINKS + CC * INNER_LINKS) + hc * INNER_LINKS + start + HEAD_LINKS)
                    dve.wait_ge(hrstd_ready, 2 * b + 2)
                    for a in range(2):
                        by_rstd = hrstd[:, a, :].rearrange("p (j h) -> p j h", h=H)[:, :, bass.ds(hc * HPC, HPC)]
                        last = nc.vector.tensor_tensor(chunk[:, a].rearrange("p j (h d) -> p j h d", d=HD),
                                                       qk[1 - a][:, :, bass.ds(hc * P, P)].rearrange("p j (h d) -> p j h d", d=HD),
                                                       by_rstd.unsqueeze(3).broadcast_to((P, JT, HPC, HD)), ALU.mult)
                    last.then_inc(chunk_ready, 1)
                    for j in range(JT):
                        at = step * JT + j
                        dve.wait_ge(scored, at + 1)
                        nc.vector.reduce_max(nmax[:, 0, :], c.psum[:, 0:HPC, 0:MAIN], AX.X, negate=True)
                        chain.link(nc.vector.reduce_max(nmax[:, 1, :], c.psum[:, 0:HPC, MAIN:S], AX.X, negate=True))
                        nc.vector.tensor_scalar(nmax_scaled[:], nmax[:, 0, :], SCALE, None, ALU.mult)
                        nc.vector.tensor_tensor(shifted[:], c.psum[:, 0:HPC, MAIN:S],
                                                nmax[:, 1, :].unsqueeze(2).broadcast_to((P, HPC, LAST)), ALU.add).then_inc(max_ready, 1)
                        dve.wait_ge(last_exp, at + 1)
                        chain.link(nc.vector.reduce_sum(rsum_last[:], shifted[:], AX.X))
                        chain.link(nc.vector.reciprocal(rsum_last[:], rsum_last[:]))
                        dve.wait_ge(exp_ready, at + 1)
                        nc.vector.reciprocal(rinv[:, j % 2, :], rsum[:])
                        chain.link(nc.vector.tensor_tensor(rsum_last[:], rsum_last[:], rsum[:], ALU.mult))
                        nc.vector.tensor_tensor(prob[:, :, MAIN:S], shifted[:],
                                                rsum_last[:].unsqueeze(2).broadcast_to((P, HPC, LAST)), ALU.mult).then_inc(prob_ready, 1)
                        for h in (0, 2):
                            dve.wait_ge(prob_turned, at * HPC + h + 1)
                            nc.vector.tensor_copy(probT[:, h, :], c.bank[4 + h % 2]).then_inc(probT_dve, 1)
                        dve.wait_ge(valued, at + 1)
                        nc.vector.tensor_tensor(mixed[:, j, bass.ds(hc * P, P)].rearrange("p (h d) -> p h d", d=HD),
                                                c.bank[6 + j % 2][:, 0:P].rearrange("p (h d) -> p h d", d=HD),
                                                rinv[:, j % 2, :].unsqueeze(2).broadcast_to((P, HPC, HD)), ALU.mult).then_inc(mixed_ready, 1)
                    assert chain.n == INNER_LINKS
                for j in range(JT):
                    dve.wait_ge(out_ready, b * JT + j + 1)
                    t = bass.ds(b * JT + j, 1)
                    nc.vector.tensor_tensor(c.X[:, t, :], c.X[:, t, :], c.bank[4 + j].unsqueeze(1), ALU.add).then_inc(added, 1)

        @block.scalar
        def _(act):
            act.wait_ge(ln_loaded, 6 * HPC * 16)
            with act.Fori(0, B) as b:
                act.wait_ge(k_used, b)
                this = c.ctxT[:, bass.ds(b, 1), :, :].rearrange("p b k s -> p (b k) s")
                nc.scalar.copy(ctx_b[:], this)
                nc.scalar.copy(ctx_end[:, :, 0:P - LAST], this[:, :, S - P:MAIN])
                nc.scalar.copy(ctx_last[:, :, P - LAST:P], this[:, :, MAIN:S]).then_inc(ctx_ready, 1)
                act.wait_ge(rows_turned, b + 1)
                for k in range(CC):
                    last = nc.scalar.copy(rowsT[:, k, :], c.bank[k])
                last.then_inc(rowsT_ready, 1)
                for a in range(2):
                    act.wait_ge(centred, 2 * b + a + 1)
                    act.wait_ge(hvar_ready, 2 * b + a)
                    nc.scalar.activation(sq[:], qk[1 - a][:], ACT.Square).then_inc(squared, 1)
                with act.Fori(0, CC) as hc:
                    step = b * CC + hc
                    act.wait_ge(chunk_turned, step + 1)
                    nc.scalar.activation(kT[:, 0:MAIN], c.bank[0][:, 0:MAIN], ACT.Identity, scale=head_ln[:, 2:3], bias=head_ln[:, 3:4])
                    nc.scalar.activation(kT[:, MAIN:S], c.bank[0][:, MAIN:S], ACT.Identity, scale=head_ln[:, 4:5], bias=head_ln[:, 5:6])
                    nc.scalar.activation(qT[:], c.bank[1], ACT.Identity, scale=head_ln[:, 0:1], bias=head_ln[:, 1:2]).then_inc(qkT_ready, 1)
                    for j in range(JT):
                        at = step * JT + j
                        act.wait_ge(max_ready, at + 1)
                        act.wait_ge(mixed_ready, at)
                        for h in range(HPC):
                            last = nc.scalar.activation(prob[:, h, 0:MAIN], c.bank[h][:, 0:MAIN], ACT.Exp, scale=SCALE,
                                                        bias=nmax_scaled[:, h:h + 1], accum_out=rsum[:, h:h + 1])
                            if h == 0:
                                nc.scalar.activation(shifted[:], shifted[:], ACT.Exp, scale=SCALE).then_inc(last_exp, 1)
                        last.then_inc(exp_ready, 1)
                        for h in (1, 3):
                            act.wait_ge(prob_turned, at * HPC + h + 1)
                            nc.scalar.copy(probT[:, h, :], c.bank[4 + h % 2]).then_inc(probT_act, 1)
                act.wait_ge(mixed_turned, b + 1)
                for k in range(CC):
                    last = nc.scalar.copy(rowsT[:, k, :], c.bank[k])
                last.then_inc(mixedT_ready, 1)

        @block.tensor
        def _(pe):
            pe.wait_ge(loaded, 7 * 16)
            pe.wait_ge(zeroed, 1)
            with pe.Fori(0, B) as b:
                pe.wait_ge(rows_ready, b + 1)
                for k in range(CC):
                    for j in range(JT):
                        last = nc.tensor.transpose(c.bank[k][:, j * P:(j + 1) * P], rows[:, j, k * P:(k + 1) * P], c.ident[:])
                last.then_inc(rows_turned, 1)
                pe.wait_ge(rowsT_ready, b + 1)
                pe.wait_ge(added, b * JT)
                for j in range(JT):
                    for k in range(CC):
                        last = nc.tensor.matmul(c.bank[4 + j], rowsT[:, k, j * P:(j + 1) * P], w_q[:, k, :],
                                                start=(k == 0), stop=(k == CC - 1))
                    last.then_inc(q_ready, 1)
                pe.wait_ge(ctx_ready, b + 1)
                for j in range(JT):
                    if j >= 2:
                        pe.wait_ge(k_copied, b * JT + j - 1)
                    for a in range(2):
                        bank = c.bank[2 * (j % 2) + a].rearrange("p (h d) -> p h d", d=HD)
                        for k in range(KC):
                            main = w_kv[:, k, :].rearrange("p (h a d) -> p h a d", a=2, d=HD)[:, :, a, :]
                            if j < JT - 1:
                                last = nc.tensor.matmul(bank, ctx_b[:, k, j * P:(j + 1) * P], main, start=(k == 0), stop=(k == KC - 1))
                            else:
                                nc.tensor.matmul(bank, ctx_end[:, k, :], main, start=(k == 0), stop=False)
                                last = nc.tensor.matmul(bank, ctx_last[:, k, :],
                                                        w_last[:, k, a * D:(a + 1) * D].rearrange("p (h d) -> p h d", d=HD),
                                                        start=False, stop=(k == KC - 1))
                    last.then_inc(kv_ready, 1)
                    if j == JT - 1:
                        nc.tensor.nop().then_inc(k_used, 1)
                with pe.Fori(0, CC) as hc:
                    step = b * CC + hc
                    pe.wait_ge(chunk_ready, step + 1)
                    for a in range(2):
                        for j in range(JT):
                            last = nc.tensor.transpose(c.bank[a][:, j * P:(j + 1) * P], chunk[:, a, j, :], c.ident[:])
                    last.then_inc(chunk_turned, 1)
                    pe.wait_ge(qkT_ready, step + 1)

                    def scores(j):
                        for h in range(HPC):
                            part = slice(h * HD, (h + 1) * HD)
                            last = nc.tensor.matmul(c.bank[h], qT[part, j * P:(j + 1) * P], kT[part, :], start=True, stop=True)
                        last.then_inc(scored, 1)

                    def turn(j, h):
                        for n in range(JT):
                            last = nc.tensor.transpose(c.bank[4 + h % 2][:, n * P:(n + 1) * P], prob[:, h, n * P:(n + 1) * P], c.ident[:])
                        last.then_inc(prob_turned, 1)

                    def value(j, h):
                        at = step * JT + j
                        if h % 2:
                            pe.wait_ge(probT_act, at * 2 + h // 2 + 1)
                        else:
                            pe.wait_ge(probT_dve, at * 2 + h // 2 + 1)
                        for n in range(JT):
                            last = nc.tensor.matmul(c.bank[6 + j % 2][:, h * HD:(h + 1) * HD], probT[:, h, n * P:(n + 1) * P],
                                                    v[:, n, bass.ds(hc * P + h * HD, HD)], start=(n == 0), stop=(n == JT - 1))
                        return last

                    scores(0)
                    for j in range(JT):
                        pe.wait_ge(prob_ready, step * JT + j + 1)
                        if j + 1 < JT:
                            scores(j + 1)
                        turn(j, 0)
                        turn(j, 1)
                        for h in range(HPC):
                            last = value(j, h)
                            if h + 2 < HPC:
                                turn(j, h + 2)
                        last.then_inc(valued, 1)
                pe.wait_ge(mixed_ready, b * CC * JT + CC * JT)
                for k in range(CC):
                    for j in range(JT):
                        last = nc.tensor.transpose(c.bank[k][:, j * P:(j + 1) * P], mixed[:, j, k * P:(k + 1) * P], c.ident[:])
                last.then_inc(mixed_turned, 1)
                pe.wait_ge(mixedT_ready, b + 1)
                for j in range(JT):
                    for k in range(CC):
                        last = nc.tensor.matmul(c.bank[4 + j], rowsT[:, k, j * P:(j + 1) * P], w_o[:, k, :],
                                                start=(k == 0), stop=(k == CC - 1))
                    last.then_inc(out_ready, 1)


E_ = 32
TOPK = 6
EG = 4
EPG = E_ // EG
M = 352
SHARED = 2
SHARED_TILES = SHARED * NT
ROUTED_TILES = TOK * TOPK // P + E_
TILES = SHARED_TILES + ROUTED_TILES


def route_tokens(nc, c, hs, slots, y_slots, weights, tile_expert, tiles_through):
    with ExitStack() as stack:
        stats = sbuf(nc, stack, "r_stats", [P, NT, 6])
        mv = sbuf(nc, stack, "r_mv", [P, NT, 2])
        rstd = sbuf(nc, stack, "r_rstd", [P, NT])
        rows = sbuf(nc, stack, "r_rows", [P, JT, D])
        rowsT = sbuf(nc, stack, "r_rowsT", [P, CC, S])
        w_gate = sbuf(nc, stack, "r_w_gate", [P, CC, E_])
        tri = sbuf(nc, stack, "r_tri", [P, P])
        ones = sbuf(nc, stack, "r_ones", [P, P])
        iota = sbuf(nc, stack, "r_iota", [P, P])
        part = sbuf(nc, stack, "r_part", [P, 1])
        earlier = sbuf(nc, stack, "r_earlier", [P, EG, EG])
        steps = sbuf(nc, stack, "r_steps", [P, NT])
        score = sbuf(nc, stack, "r_score", [P, NT, E_])
        best = sbuf(nc, stack, "r_best", [P, NT, EG])
        pair = sbuf(nc, stack, "r_pair", [P, NT, EG, EG])
        pair2 = sbuf(nc, stack, "r_pair2", [P, NT, EG, EG])
        top = sbuf(nc, stack, "r_top", [P, NT, 8])
        index = sbuf(nc, stack, "r_index", [P, NT, 8], U32)
        indexf = sbuf(nc, stack, "r_indexf", [P, NT, 8])
        hot = sbuf(nc, stack, "r_hot", [P, TOPK, NT, E_])
        member = sbuf(nc, stack, "r_member", [P, NT, E_])
        members_before = sbuf(nc, stack, "r_members_before", [P, NT, E_])
        place = sbuf(nc, stack, "r_place", [P, NT, E_])
        work = sbuf(nc, stack, "r_work", [P, NT, E_])
        slotsf = sbuf(nc, stack, "r_slotsf", [P, NT, TOPK])
        wsum = sbuf(nc, stack, "r_wsum", [P, NT])
        count = sbuf(nc, stack, "r_count", [P, E_])
        over = sbuf(nc, stack, "r_over", [P, E_, NT])
        tiles = sbuf(nc, stack, "r_tiles", [P, E_])
        through = sbuf(nc, stack, "r_through", [P, E_])
        first_slot = sbuf(nc, stack, "r_first_slot", [P, E_])
        expert_of = sbuf(nc, stack, "r_expert_of", [P, 1])
        small = sbuf(nc, stack, "r_small", [P, E_])
        loaded, var_ready, rstd_ready, rows_ready, rows_turned, rowsT_ready, gated, taken = sems(
            nc, c, "r_", "loaded var_ready rstd_ready rows_ready rows_turned rowsT_ready gated taken")
        exped, members_ready, counted, expert_ready, expert_turned, dve_chain, hs_stored, exp_ready, ones_set, hs_ready = sems(
            nc, c, "r_", "exped members_ready counted expert_ready expert_turned dve_chain hs_stored exp_ready ones_set hs_ready")
        block = stack.enter_context(nc.Block())

        @block.sync
        def _(sp):
            for dst, src in ((w_gate[:], c.dram["L1_ffn_gate_w"].rearrange("(k p) n -> p k n", p=P)), (tri[:], c.dram["i_tri"]),
                             (iota[:], c.dram["i_iota"]), (part[:], c.dram["i_part"]), (earlier[:], c.dram["i_earlier"]), (steps[:], c.dram["i_steps"])):
                sp.dma_start(dst, src).then_inc(loaded, 16)
            sp.wait_ge(hs_ready, B)
            sp.dma_start(c.dram["d_hs"].rearrange("(t p) d -> p t d", p=P), hs[:]).then_inc(hs_stored, 16)
            sp.wait_ge(hs_stored, 16)

        @block.gpsimd
        def _(pool):
            nc.gpsimd.memset(ones[:], 1.0).then_inc(ones_set, 1)
            pool.wait_ge(var_ready, 1)
            nc.gpsimd.tensor_tensor(rstd[:], rstd[:], c.minus_half[:, 0:NT], ALU.pow).then_inc(rstd_ready, 1)

        @block.vector
        def _(dve):
            chain = Chain(dve, dve_chain)
            link = chain.link
            norm_rows_into(nc, dve, chain, c, stats, mv, rstd, var_ready, rstd_ready, 1e-5)
            with dve.Fori(0, B) as b:
                dve.wait_ge(rows_turned, b)
                for j in range(JT):
                    t = bass.ds(b * JT + j, 1)
                    last = nc.vector.tensor_scalar(rows[:, j:j + 1, :], c.X[:, t, :], mv[:, t, 0:1], rstd[:, t],
                                                   ALU.subtract, ALU.mult)
                last.then_inc(rows_ready, 1)
                for j in range(JT):
                    t = bass.ds(b * JT + j, 1)
                    last = nc.vector.tensor_scalar(hs[:, t, :], c.X[:, t, :], mv[:, t, 0:1], rstd[:, t],
                                                   ALU.subtract, ALU.mult)
                last.then_inc(hs_ready, 1)
                dve.wait_ge(gated, b + 1)
                nc.vector.tensor_scalar(score[:, bass.ds(b * JT, JT), :], c.bank[4][:, 0:JT * E_].rearrange("p (j e) -> p j e", j=JT),
                                        -1.0, None, ALU.mult).then_inc(taken, 1)
            dve.wait_ge(exp_ready, 1)
            link(nc.vector.tensor_scalar(score[:], score[:], 1.0, None, ALU.add))
            link(nc.vector.reciprocal(score[:], score[:]))
            dve.wait_ge(loaded, 6 * 16)
            link(nc.vector.reduce_max(best[:], score[:].rearrange("p t (g e) -> p t g e", g=EG), AX.X))
            shape = (P, NT, EG, EG)
            this, other = best[:].unsqueeze(3).broadcast_to(shape), best[:].unsqueeze(2).broadcast_to(shape)
            nc.vector.tensor_tensor(pair[:], other, this, ALU.is_gt)
            link(nc.vector.tensor_tensor(pair2[:], other, this, ALU.is_equal))
            link(nc.vector.tensor_tensor(pair2[:], pair2[:], earlier[:].unsqueeze(1).broadcast_to(shape), ALU.mult))
            link(nc.vector.tensor_tensor(pair[:], pair[:], pair2[:], ALU.add))
            link(nc.vector.reduce_sum(best[:], pair[:], AX.X))
            link(nc.vector.tensor_scalar(best[:], best[:], 2.0, None, ALU.is_lt))
            by_group = best[:].unsqueeze(3).broadcast_to((P, NT, EG, EPG))
            grouped = lambda tile: tile[:].rearrange("p t (g e) -> p t g e", g=EG)
            link(nc.vector.tensor_tensor(grouped(score), grouped(score), by_group, ALU.mult))
            link(nc.vector.tensor_scalar(best[:], best[:], -1.0, None, ALU.add))
            link(nc.vector.tensor_tensor(grouped(score), grouped(score), by_group, ALU.add))
            for t in range(NT):
                last = nc.vector.max(top[:, t, :], score[:, t, :])
            link(last)
            for t in range(NT):
                last = nc.vector.max_index(index[:, t, :], top[:, t, :], score[:, t, :])
            link(last)
            link(nc.vector.tensor_copy(indexf[:], index[:]))
            link(nc.vector.reduce_sum(wsum[:], top[:, :, 0:TOPK], AX.X))
            link(nc.vector.reciprocal(wsum[:], wsum[:]))
            nc.vector.tensor_tensor(weights[:], top[:, :, 0:TOPK], wsum[:].unsqueeze(2).broadcast_to((P, NT, TOPK)), ALU.mult)
            wide = (P, NT, E_)
            for k in range(TOPK):
                last = nc.vector.tensor_tensor(hot[:, k], iota[:, 0:E_].unsqueeze(1).broadcast_to(wide),
                                               indexf[:, :, k:k + 1].broadcast_to(wide), ALU.is_equal)
            link(last)
            link(nc.vector.tensor_tensor(member[:], hot[:, 0], hot[:, 1], ALU.add))
            for k in range(2, TOPK):
                link(nc.vector.tensor_tensor(member[:], member[:], hot[:, k], ALU.add))
            link(nc.vector.memset(members_before[:, 0, :], 0.0))
            for t in range(1, NT):
                link(nc.vector.tensor_tensor(members_before[:, t, :], members_before[:, t - 1, :], member[:, t - 1, :], ALU.add))
            nc.vector.tensor_tensor(small[:], members_before[:, NT - 1, :], member[:, NT - 1, :], ALU.add).then_inc(members_ready, 1)
            dve.wait_ge(counted, 1)
            nc.vector.tensor_copy(place[:].rearrange("p t e -> p (t e)"), c.bank[5])
            link(nc.vector.tensor_copy(count[:], c.bank[6][:, 0:E_]))
            link(nc.vector.tensor_tensor(over[:], count[:].unsqueeze(2).broadcast_to((P, E_, NT)),
                                         steps[:].unsqueeze(1).broadcast_to((P, E_, NT)), ALU.is_gt))
            link(nc.vector.reduce_sum(tiles[:], over[:], AX.X))
            link(nc.vector.tensor_scalar(tiles[:], tiles[:], 1.0, None, ALU.max))
            link(nc.vector.tensor_tensor_scan(through[:], ones[:, 0:E_], tiles[:], 0.0, ALU.mult, ALU.add))
            link(nc.vector.tensor_tensor(first_slot[:], through[:], tiles[:], ALU.subtract))
            link(nc.vector.tensor_scalar(first_slot[:], first_slot[:], float(P), None, ALU.mult))
            link(nc.vector.tensor_scalar(small[:], through[:], part[:, 0:1], None, ALU.is_le, ALU.add, accum_out=expert_of[:]))
            nc.vector.tensor_scalar(expert_of[:], expert_of[:], float(E_ - 1), float(SHARED), ALU.min, ALU.add).then_inc(expert_ready, 1)
            link(nc.vector.tensor_tensor(place[:], place[:], first_slot[:].unsqueeze(1).broadcast_to(wide), ALU.add))
            for k in range(TOPK):
                link(nc.vector.tensor_tensor(work[:], hot[:, k], place[:], ALU.mult))
                link(nc.vector.reduce_sum(slotsf[:, :, k], work[:], AX.X))
            nc.vector.tensor_copy(slots[:], slotsf[:])
            nc.vector.tensor_scalar(y_slots[:], slotsf[:], float(SHARED_TILES * P), None, ALU.add)
            nc.vector.tensor_scalar(tiles_through[:, SHARED:], through[0:1, :], float(SHARED_TILES), None, ALU.add)
            for s in range(SHARED):
                nc.vector.memset(tiles_through[:, s:s + 1], (s + 1) * NT)
                nc.vector.memset(tile_expert[:, s * NT:(s + 1) * NT], s)
            dve.wait_ge(expert_turned, 1)
            nc.vector.tensor_copy(tile_expert[:, SHARED_TILES:], c.bank[7][0:1, 0:ROUTED_TILES])

        @block.scalar
        def _(act):
            with act.Fori(0, B) as b:
                act.wait_ge(rows_turned, b + 1)
                for k in range(CC):
                    last = nc.scalar.copy(rowsT[:, k, :], c.bank[k])
                last.then_inc(rowsT_ready, 1)
            act.wait_ge(taken, B)
            nc.scalar.activation(score[:], score[:], ACT.Exp).then_inc(exp_ready, 1)

        @block.tensor
        def _(pe):
            pe.wait_ge(loaded, 6 * 16)
            with pe.Fori(0, B) as b:
                pe.wait_ge(rows_ready, b + 1)
                for k in range(CC):
                    for j in range(JT):
                        last = nc.tensor.transpose(c.bank[k][:, j * P:(j + 1) * P], rows[:, j, k * P:(k + 1) * P], c.ident[:])
                last.then_inc(rows_turned, 1)
                pe.wait_ge(rowsT_ready, b + 1)
                pe.wait_ge(taken, b)
                for j in range(JT):
                    for k in range(CC):
                        last = nc.tensor.matmul(c.bank[4][:, j * E_:(j + 1) * E_], rowsT[:, k, j * P:(j + 1) * P], w_gate[:, k, :],
                                                start=(k == 0), stop=(k == CC - 1))
                last.then_inc(gated, 1)
            pe.wait_ge(ones_set, 1)
            pe.wait_ge(members_ready, 1)
            nc.tensor.matmul(c.bank[5], tri[:], member[:].rearrange("p t e -> p (t e)"), start=True, stop=False)
            nc.tensor.matmul(c.bank[5], ones[:], members_before[:].rearrange("p t e -> p (t e)"), start=False, stop=True)
            nc.tensor.matmul(c.bank[6][:, 0:E_], ones[:], small[:], start=True, stop=True).then_inc(counted, 1)
            pe.wait_ge(expert_ready, 1)
            nc.tensor.transpose(c.bank[7][0:1, 0:P], expert_of[:], c.ident[:]).then_inc(expert_turned, 1)


def expert_tiles(nc, c, hs, slots, tile_expert, tiles_through):
    ME = 3
    cuts = [0, P, 2 * P, M]
    LAST_M = M - 2 * P
    with ExitStack() as stack:
        w_gu = sbuf(nc, stack, "e_w_gu", [P, 2, CC, 2 * M])
        w_d = sbuf(nc, stack, "e_w_d", [P, 2, ME, D])
        row = [sbuf(nc, stack, f"e_row{n}", [P, D]) for n in range(2)]
        rowT = [sbuf(nc, stack, f"e_rowT{n}", [P, CC, P]) for n in range(2)]
        silu = [sbuf(nc, stack, f"e_silu{n}", [P, M]) for n in range(2)]
        mid = [sbuf(nc, stack, f"e_mid{n}", [P, M]) for n in range(2)]
        midT = sbuf(nc, stack, "e_midT", [P, ME, P])
        y = [sbuf(nc, stack, f"e_y{n}", [P, D]) for n in range(2)]
        row_even, row_odd, y_even, y_odd, w_even, w_odd, scattered = sems(
            nc, c, "e_", "row_even row_odd y_even y_odd w_even w_odd scattered")
        row_loaded, y_stored, w_loaded = [row_even, row_odd], [y_even, y_odd], [w_even, w_odd]
        weights_ready, row_turned, rowT_ready, gate_done, up_done, silu_ready, mid_ready, mid_turned, midT_ready, down_done, y_copied = sems(
            nc, c, "e_", "weights_ready row_turned rowT_ready gate_done up_done silu_ready mid_ready mid_turned midT_ready down_done y_copied")
        block = stack.enter_context(nc.Block())
        G, U, XT, HT, Y = [c.bank[0], c.bank[1]], [c.bank[2], c.bank[3]], c.bank[4], c.bank[5], [c.bank[6], c.bank[7]]
        LOADS = 4

        @block.sync
        def _(sp):
            def load(par, gate, up, down):
                for dst, src in ((w_gu[:, par, :, 0:M], gate.rearrange("(k p) n -> p k n", p=P)),
                                 (w_gu[:, par, :, M:2 * M], up.rearrange("(k p) n -> p k n", p=P)),
                                 (w_d[:, par, 0:2, :], down[0:2 * P, :].rearrange("(k p) n -> p k n", p=P)),
                                 (w_d[0:LAST_M, par, 2, :], down[2 * P:M, :])):
                    sp.dma_start(dst, src).then_inc(w_loaded[par], 16)

            def routed(e, par):
                load(par, *(w[bass.ds(e, 1)].rearrange("a k n -> (a k) n") for w in (c.dram["L1_ffn_w_gate"], c.dram["L1_ffn_w_up"], c.dram["L1_ffn_w_down"])))

            for s in range(SHARED):
                part = slice(s * M, (s + 1) * M)
                load(s, c.dram["L1_ffn_sw_gate"][:, part], c.dram["L1_ffn_sw_up"][:, part], c.dram["L1_ffn_sw_down"][part, :])
            sp.wait_ge(w_loaded[0], LOADS * 16)
            sp.nop().then_inc(weights_ready, 1)
            with sp.Fori(0, E_ // 2) as n:
                for par in range(2):
                    sp.wait_ge(w_loaded[1 - par], LOADS * 16 * (n + 1 + par))
                    sp.nop().then_inc(weights_ready, 1)
                    done = sp.value_load(tiles_through[0:1, bass.ds(n * 2 + par, 1)], min_val=1, max_val=TILES)
                    sp.wait_ge(down_done, done)
                    routed(n * 2 + par, par)
            sp.wait_ge(w_loaded[1], LOADS * 16 * (E_ // 2 + 1))
            sp.nop().then_inc(weights_ready, 1)

        @block.gpsimd
        def _(pool):
            for t in range(NT):
                for k in range(TOPK):
                    nc.gpsimd.indirect_dma_start(c.dram["d_sorted"], bass.IndirectOffsetOnAxis(ap=slots[:, t, k:k + 1], axis=0),
                                                 hs[:, t, :], None).then_inc(scattered, 16)

        hs_tiles = c.dram["d_hs"].rearrange("(t p) d -> p t d", p=P)
        sorted_tiles = c.dram["d_sorted"].rearrange("(t p) d -> p t d", p=P)
        y_tiles = c.dram["d_y"].rearrange("(t p) d -> p t d", p=P)

        @block.scalar
        def _(act):
            def load(source, t, par):
                act.dma_start(row[par][:].unsqueeze(1), source[:, bass.ds(t, 1), :]).then_inc(row_loaded[par], 16)

            def silus(i, par):
                act.wait_ge(gate_done, i + 1)
                nc.scalar.activation(silu[par][:], G[par][:, 0:M], ACT.Silu).then_inc(silu_ready, 1)

            def copy_rowT(i, par):
                act.wait_ge(row_turned, i + 1)
                nc.scalar.copy(rowT[par][:], XT.rearrange("p (k n) -> p k n", k=CC)).then_inc(rowT_ready, 1)

            def store(i, par):
                act.wait_ge(y_copied, i + 1)
                act.dma_start(y_tiles[:, bass.ds(i, 1), :], y[par][:].unsqueeze(1)).then_inc(y_stored[par], 16)

            def steps(i, par, more=True, source=None, t=None, stores=True):
                silus(i, par)
                if more:
                    copy_rowT(i + 1, 1 - par)
                if source is not None:
                    load(source, t, 1 - par)
                if stores:
                    store(i - 2, par)

            load(hs_tiles, 0, 0)
            load(hs_tiles, 1, 1)
            copy_rowT(0, 0)
            load(hs_tiles, 2, 0)
            for i in range(2):
                steps(i, i, source=hs_tiles, t=i + 3, stores=False)
            with act.Fori(1, NT // 2 - 2) as n:
                for par in range(2):
                    steps(n * 2 + par, par, source=hs_tiles, t=n * 2 + par + 3)
            for i in range(NT - 4, NT):
                steps(i, i % 2, source=hs_tiles, t=(i + 3) % NT)
            with act.Fori(NT // 2, NT - 2) as n:
                for par in range(2):
                    steps(n * 2 + par, par, source=hs_tiles, t=n * 2 + par + 3 - NT)
            for i in range(SHARED_TILES - 4, SHARED_TILES):
                if i + 3 < SHARED_TILES:
                    steps(i, i % 2, source=hs_tiles, t=i + 3 - NT)
                else:
                    if i + 3 == SHARED_TILES:
                        act.wait_ge(scattered, NT * TOPK * 16)
                    steps(i, i % 2, source=sorted_tiles, t=i + 3 - SHARED_TILES)
            with act.Fori(SHARED_TILES // 2, TILES // 2 - 2) as n:
                for par in range(2):
                    steps(n * 2 + par, par, source=sorted_tiles, t=n * 2 + par + 3 - SHARED_TILES)
            for i in range(TILES - 4, TILES):
                if i + 3 < TILES:
                    steps(i, i % 2, source=sorted_tiles, t=i + 3 - SHARED_TILES)
                else:
                    steps(i, i % 2, more=(i + 1 < TILES))
            for i in range(TILES - 2, TILES):
                store(i, i % 2)
            for par in range(2):
                act.wait_ge(y_stored[par], 16 * (TILES // 2))

        @block.vector
        def _(dve):
            def copy_midT(i):
                dve.wait_ge(mid_turned, i + 1)
                nc.vector.tensor_copy(midT[:, 0:2, :], HT[:, 0:2 * P].rearrange("p (k n) -> p k n", k=2))
                nc.vector.tensor_copy(midT[0:LAST_M, 2, :], HT[0:LAST_M, 2 * P:3 * P]).then_inc(midT_ready, 1)

            def multiply(i, par):
                dve.wait_ge(silu_ready, i + 1)
                dve.wait_ge(up_done, i + 1)
                nc.vector.tensor_tensor(mid[par][:], silu[par][:], U[par][:, 0:M], ALU.mult).then_inc(mid_ready, 1)

            def copy_y(i, par, stored=None):
                dve.wait_ge(down_done, i + 1)
                if stored is not None:
                    dve.wait_ge(y_stored[par], stored)
                nc.vector.tensor_copy(y[par][:], Y[par]).then_inc(y_copied, 1)

            multiply(0, 0)
            for i in (1, 2):
                copy_midT(i - 1)
                multiply(i, i % 2)
                copy_y(i - 1, (i - 1) % 2)
            copy_midT(2)
            multiply(3, 1)
            copy_y(2, 0, 16)
            with dve.Fori(2, TILES // 2) as n:
                for par in range(2):
                    copy_midT(n * 2 + par - 1)
                    multiply(n * 2 + par, par)
                    copy_y(n * 2 + par - 1, 1 - par, 16 * (n - 1 + par))
            copy_midT(TILES - 1)
            copy_y(TILES - 1, 1, 16 * (TILES // 2 - 1))

        @block.tensor
        def _(pe):
            def turn_row(i, par, loads):
                pe.wait_ge(row_loaded[par], loads)
                for k in range(CC):
                    last = nc.tensor.transpose(XT[:, k * P:(k + 1) * P], row[par][:, k * P:(k + 1) * P], c.ident[:])
                last.then_inc(row_turned, 1)

            def turn_mid(i, par):
                pe.wait_ge(mid_ready, i + 1)
                for k in range(ME):
                    n = cuts[k + 1] - cuts[k]
                    last = nc.tensor.transpose(HT[0:n, k * P:(k + 1) * P], mid[par][:, cuts[k]:cuts[k + 1]], c.ident[:])
                last.then_inc(mid_turned, 1)

            def product(bank, par, buffer, at):
                for k in range(CC):
                    last = nc.tensor.matmul(bank[:, 0:M].unsqueeze(1), rowT[par][:, k, :],
                                            w_gu[:, bass.ds(buffer, 1), k, at:at + M],
                                            start=(k == 0), stop=(k == CC - 1))
                return last

            def down(i, par, buffer, before=None):
                pe.wait_ge(midT_ready, i + 1)
                if before is not None:
                    pe.wait_ge(y_copied, before)
                for k in range(ME):
                    n = cuts[k + 1] - cuts[k]
                    last = nc.tensor.matmul(Y[par].unsqueeze(1), midT[0:n, k, :], w_d[0:n, bass.ds(buffer, 1), k, :],
                                            start=(k == 0), stop=(k == ME - 1))
                last.then_inc(down_done, 1)

            def expert(i):
                return pe.value_load(tile_expert[0:1, bass.ds(i, 1)], min_val=0, max_val=E_ + SHARED - 1)

            def tile(i, par, old, more=True, loads=None, used=None, before=None):
                e = expert(i)
                pe.wait_ge(rowT_ready, i + 1)
                pe.wait_ge(weights_ready, e + 1)
                if used is not None:
                    pe.wait_ge(mid_ready, used)
                buffer = e % 2
                product(G[par], par, buffer, 0).then_inc(gate_done, 1)
                if old is not None:
                    turn_mid(i - 1, 1 - par)
                if more:
                    turn_row(i + 1, 1 - par, loads)
                product(U[par], par, buffer, M).then_inc(up_done, 1)
                if old is not None:
                    down(i - 1, 1 - par, old, before)
                return buffer

            turn_row(0, 0, 16)
            tile(0, 0, None, loads=16)
            tile(1, 1, 0, loads=32)
            tile(2, 0, 0, loads=32, used=1)
            tile(3, 1, 0, loads=48, used=2, before=1)
            with pe.Fori(2, TILES // 2 - 1) as n:
                tile(n * 2, 0, expert(n * 2 - 1) % 2, loads=16 * (n + 1), used=n * 2 - 1, before=n * 2 - 2)
                tile(n * 2 + 1, 1, expert(n * 2) % 2, loads=16 * (n + 2), used=n * 2, before=n * 2 - 1)
            i = TILES - 2
            tile(i, 0, expert(i - 1) % 2, loads=16 * (TILES // 2), used=i - 1, before=i - 2)
            tile(i + 1, 1, expert(i) % 2, more=False, used=i, before=i - 1)
            turn_mid(i + 1, 1)
            down(i + 1, 1, expert(i + 1) % 2, i)


def combine(nc, c, y_slots, weights):
    SETS = 2
    with ExitStack() as stack:
        part = sbuf(nc, stack, "m_part", [P, SETS, TOPK + SHARED, D])
        shared_even, shared_odd, routed_even, routed_odd, added, stored, dve_chain = sems(
            nc, c, "m_", "shared_even shared_odd routed_even routed_odd added stored dve_chain")
        shared_in, routed_in = [shared_even, shared_odd], [routed_even, routed_odd]
        block = stack.enter_context(nc.Block())
        y_tiles = c.dram["d_y"].rearrange("(t p) d -> p t d", p=P)

        @block.sync
        def _(sp):
            for t in range(NT):
                if t >= SETS:
                    sp.wait_ge(added, t - SETS + 1)
                for s in range(SHARED):
                    sp.dma_start(part[:, t % SETS, TOPK + s, :], y_tiles[:, s * NT + t, :]).then_inc(shared_in[t % SETS], 16)
                if t >= 1:
                    sp.wait_ge(added, t)
                    sp.dma_start(c.out.rearrange("b (j p) d -> p (b j) d", p=P)[:, t - 1, :], c.X[:, t - 1, :]).then_inc(stored, 16)
            sp.wait_ge(added, NT)
            sp.dma_start(c.out.rearrange("b (j p) d -> p (b j) d", p=P)[:, NT - 1, :], c.X[:, NT - 1, :]).then_inc(stored, 16)
            sp.wait_ge(stored, 16 * NT)

        @block.gpsimd
        def _(pool):
            for t in range(NT):
                if t >= SETS:
                    pool.wait_ge(added, t - SETS + 1)
                for k in range(TOPK):
                    nc.gpsimd.indirect_dma_start(part[:, t % SETS, k, :], None, c.dram["d_y"],
                                                 bass.IndirectOffsetOnAxis(ap=y_slots[:, t, k:k + 1], axis=0)).then_inc(routed_in[t % SETS], 16)

        @block.vector
        def _(dve):
            chain = Chain(dve, dve_chain)
            for t in range(NT):
                dve.wait_ge(shared_in[t % SETS], SHARED * 16 * (t // SETS + 1))
                for s in range(SHARED):
                    chain.link(nc.vector.tensor_tensor(c.X[:, t, :], c.X[:, t, :], part[:, t % SETS, TOPK + s, :], ALU.add))
                dve.wait_ge(routed_in[t % SETS], TOPK * 16 * (t // SETS + 1))
                for k in range(TOPK):
                    last = nc.vector.scalar_tensor_tensor(c.X[:, t, :], part[:, t % SETS, k, :], weights[:, t, k:k + 1],
                                                          c.X[:, t, :], ALU.mult, ALU.add)
                    if k < TOPK - 1:
                        chain.link(last)
                last.then_inc(added, 1)


def routed_ffn(nc, c):
    with ExitStack() as stack:
        slots = sbuf(nc, stack, "f_slots", [P, NT, TOPK], U32)
        y_slots = sbuf(nc, stack, "f_y_slots", [P, NT, TOPK], U32)
        weights = sbuf(nc, stack, "f_weights", [P, NT, TOPK])
        tile_expert = sbuf(nc, stack, "f_tile_expert", [1, TILES], I32)
        tiles_through = sbuf(nc, stack, "f_tiles_through", [1, E_ + SHARED], I32)
        with ExitStack() as inner:
            hs = sbuf(nc, inner, "f_hs", [P, NT, D])
            route_tokens(nc, c, hs, slots, y_slots, weights, tile_expert, tiles_through)
            expert_tiles(nc, c, hs, slots, tile_expert, tiles_through)
        combine(nc, c, y_slots, weights)


def store_rows(nc, c):
    with ExitStack() as stack:
        stored, = sems(nc, c, "s_", "stored")
        block = stack.enter_context(nc.Block())

        @block.sync
        def _(sp):
            sp.dma_start(c.out.rearrange("b (j p) d -> p (b j) d", p=P), c.X[:]).then_inc(stored, 16)
            sp.wait_ge(stored, 16)


def build(nc, aps, out):
    c = Core()
    c.dram = aps
    c.out = out
    c.of_stage = []
    with ExitStack() as stack:
        c.X = sbuf(nc, stack, "X", [P, NT, D])
        c.ctxT = sbuf(nc, stack, "ctxT", [P, B, KC, S])
        c.ident = sbuf(nc, stack, "ident", [P, P])
        c.minus_half = sbuf(nc, stack, "minus_half", [P, 64])
        c.psum = stack.enter_context(nc.psum_tensor("psum", [P, 8, 512], F32))
        c.bank = [c.psum[:, n, :] for n in range(8)]
        half_set, = sems(nc, c, "g_", "half_set")
        with nc.Block() as block:
            @block.gpsimd
            def _(pool):
                nc.gpsimd.memset(c.minus_half[:], -0.5).then_inc(half_set, 1)
                pool.wait_ge(half_set, 1)
        load_constants(nc, c)
        end_stage(nc, c)
        if LAST_STAGE >= 1:
            map_attention(nc, c)
            end_stage(nc, c)
        if LAST_STAGE >= 2:
            token_choice_ffn(nc, c)
            end_stage(nc, c)
        if LAST_STAGE >= 3:
            context_attention(nc, c)
            end_stage(nc, c)
        if LAST_STAGE >= 4:
            routed_ffn(nc, c)
        else:
            store_rows(nc, c)


def shape_tables():
    s, p = np.arange(S), np.arange(P)
    inv_freq = (np.float32(1.0) / np.float32(10000.0) ** (np.arange(0, 128, 2, dtype=np.float32) / np.float32(128))).astype(np.float32)
    ang = (s.astype(np.float32)[:, None] * inv_freq).astype(np.float32)
    slots = np.arange(2 * P)
    causal = np.stack([slots[None, :] <= (g * P + p)[:, None] for g in range(2)], 1)
    f = np.float32
    return {
        "i_ident": np.eye(P, dtype=f),
        "i_tri": (p[:, None] < p[None, :]).astype(f),
        "i_before": np.stack([s[None, :] < (j * P + p)[:, None] for j in range(JT)], 1).astype(f),
        "i_iota": np.broadcast_to(p.astype(f), (P, P)).copy(),
        "i_slot_base": np.broadcast_to(((np.arange(NT) // JT % 2) * (S // 8) + 1).astype(f), (P, NT)).copy(),
        "i_rope": np.concatenate([np.cos(ang), np.sin(ang)], 1).astype(f),
        "i_part": p.astype(f)[:, None].copy(),
        "i_earlier": np.broadcast_to(np.tri(EG, EG, -1, dtype=f), (P, EG, EG)).copy(),
        "i_steps": np.broadcast_to((np.arange(NT) * P).astype(f), (P, NT)).copy(),
        "i_causal": np.where(causal, f(0), f(-1e30)).reshape(P, 4 * P).astype(f),
    }


def kernel(**inputs):
    import concourse.bacc as _bacc
    from concourse.bass_utils import run_bass_kernel_spmd as _run

    nc = _bacc.Bacc("TRN2", target_bir_lowering=False, num_devices=1)
    arrays, aps = {}, {}
    for name, a in {**inputs, **shape_tables()}.items():
        a = np.ascontiguousarray(a)
        arrays[f"in_{name}"] = a
        aps[name] = nc.dram_tensor(f"in_{name}", a.shape, mybir.dt.from_np(a.dtype), kind="ExternalInput").ap()
    aps["d_scores"] = nc.dram_tensor("d_scores", (NT, P), F32).ap()
    aps["d_hs"] = nc.dram_tensor("d_hs", (TOK, D), F32).ap()
    aps["d_sorted"] = nc.dram_tensor("d_sorted", (ROUTED_TILES * P, D), F32).ap()
    aps["d_y"] = nc.dram_tensor("d_y", (TILES * P, D), F32).ap()
    out = nc.dram_tensor("out", (B, S, D), F32, kind="ExternalOutput").ap()
    build(nc, aps, out)
    r = _run(nc, [arrays], core_ids=[0])
    return r.results[0]["out"]
```

```python
from contextlib import ExitStack

import numpy as np

import concourse.bass as bass
from concourse import mybir

F32 = mybir.dt.float32
F32R = mybir.dt.float32r
I32 = mybir.dt.int32
U32 = mybir.dt.uint32
ALU = mybir.AluOpType
ACT = mybir.ActivationFunctionType
AX = mybir.AxisListType

P = 128
B, S, D = 4, 512, 512
TOK = B * S
NT = TOK // P
JT = S // P
CC = D // P
CTX = 256
KC = CTX // P
LAST_STAGE = 99


class Core:
    pass


def sbuf(nc, stack, name, shape, dt=F32):
    return stack.enter_context(nc.sbuf_tensor(name, shape, dt))


def sems(nc, c, prefix, names):
    made = [nc.alloc_semaphore(prefix + n) for n in names.split()]
    c.of_stage += made
    return made


def end_stage(nc, c):
    with nc.Block() as block:
        @block.gpsimd
        def _(pool):
            nc.clear_and_free_semaphores(c.of_stage)
    c.of_stage = []


class Chain:

    def __init__(self, eng, sem, base=0):
        self.eng, self.sem, self.n, self.base = eng, sem, 0, base

    def link(self, ins):
        self.n += 1
        ins.then_inc(self.sem, 1)
        self.eng.wait_ge(self.sem, self.base + self.n)

    def after_loop(self, times):
        self.n += times
        self.eng.wait_ge(self.sem, self.base + self.n)


def load_constants(nc, c):
    with ExitStack() as stack:
        ctx_rows = sbuf(nc, stack, "ctx_rows", [P, 2, JT, CTX])
        x_loaded, const_loaded, ctx_even, ctx_odd, turned, copied = sems(
            nc, c, "c_", "x_loaded const_loaded ctx_even ctx_odd turned copied")
        ctx_loaded = [ctx_even, ctx_odd]
        block = stack.enter_context(nc.Block())

        @block.sync
        def _(sp):
            sp.dma_start(c.ident[:], c.dram["i_ident"]).then_inc(const_loaded, 16)
            for b in range(B):
                if b >= 2:
                    sp.wait_ge(turned, b - 1)
                sp.dma_start(ctx_rows[:, b % 2], c.dram["ctx_1024"][b].rearrange("(j p) d -> p j d", p=P)).then_inc(
                    ctx_loaded[b % 2], 16)
            sp.dma_start(c.X[:], c.dram["x"].rearrange("b (j p) d -> p (b j) d", p=P)).then_inc(x_loaded, 16)
            sp.wait_ge(x_loaded, 16)

        @block.tensor
        def _(pe):
            pe.wait_ge(const_loaded, 16)
            for b in range(B):
                pe.wait_ge(ctx_loaded[b % 2], 16 * (b // 2 + 1))
                if b >= 2:
                    pe.wait_ge(copied, b - 1)
                for k in range(KC):
                    for j in range(JT):
                        last = nc.tensor.transpose(c.bank[2 * (b % 2) + k][:, j * P:(j + 1) * P],
                                                   ctx_rows[:, b % 2, j, k * P:(k + 1) * P], c.ident[:])
                last.then_inc(turned, 1)

        @block.scalar
        def _(act):
            for b in range(B):
                act.wait_ge(turned, b + 1)
                for k in range(KC):
                    last = nc.scalar.copy(c.ctxT[:, b, k, :], c.bank[2 * (b % 2) + k][:])
                last.then_inc(copied, 1)


def map_attention(nc, c):
    with ExitStack() as stack:
        wq = sbuf(nc, stack, "a_wq", [P, 2, CTX])
        wT = sbuf(nc, stack, "a_wT", [P, 2, KC, P])
        bias = sbuf(nc, stack, "a_bias", [P, 2])
        stats = sbuf(nc, stack, "a_stats", [P, JT, 6])
        mv = sbuf(nc, stack, "a_mv", [P, JT, 2])
        rstd = sbuf(nc, stack, "a_rstd", [P, JT])
        xln = sbuf(nc, stack, "a_xln", [P, JT, D])
        xlnT = sbuf(nc, stack, "a_xlnT", [P, CC, S])
        qkT = sbuf(nc, stack, "a_qkT", [P, 2, S])
        prob = sbuf(nc, stack, "a_prob", [P, JT, S])
        attT = sbuf(nc, stack, "a_attT", [P, CC, S])
        nmax = sbuf(nc, stack, "a_nmax", [P, JT])
        rsum = sbuf(nc, stack, "a_rsum", [P, JT])
        rinv = sbuf(nc, stack, "a_rinv", [P, JT])
        w_loaded, w_turned, w_copied = sems(nc, c, "a_", "w_loaded w_turned w_copied")
        var_ready, rstd_ready, xln_ready, xln_turned, xlnT_ready = sems(
            nc, c, "a_", "var_ready rstd_ready xln_ready xln_turned xlnT_ready")
        qk_ready, qkT_ready, energy_ready, max_ready, exp_ready, prob_ready = sems(
            nc, c, "a_", "qk_ready qkT_ready energy_ready max_ready exp_ready prob_ready")
        prob_turned, attT_ready, mixed, added, dve_chain = sems(
            nc, c, "a_", "prob_turned attT_ready mixed added dve_chain")
        block = stack.enter_context(nc.Block())
        energy_bank = [6, 7, 4, 5]

        @block.sync
        def _(sp):
            sp.dma_start(wq[:, 0], c.dram["L0_xattn_Wq"]).then_inc(w_loaded, 16)
            sp.dma_start(wq[:, 1], c.dram["L0_xattn_Wk"]).then_inc(w_loaded, 16)
            sp.dma_start(bias[:, 0:1], c.dram["L0_xattn_bq"].rearrange("(p a) -> p a", a=1)).then_inc(w_loaded, 16)
            sp.dma_start(bias[:, 1:2], c.dram["L0_xattn_bk"].rearrange("(p a) -> p a", a=1)).then_inc(w_loaded, 16)

        @block.gpsimd
        def _(pool):
            with pool.Fori(0, B) as b:
                pool.wait_ge(var_ready, b + 1)
                nc.gpsimd.tensor_tensor(rstd[:], rstd[:], c.minus_half[:, 0:JT], ALU.pow).then_inc(rstd_ready, 1)

        @block.vector
        def _(dve):
            LINKS = 3
            with dve.Fori(0, B) as b:
                chain = Chain(dve, dve_chain, b * LINKS)
                for j in range(JT):
                    last = nc.vector.bn_stats(stats[:, j, :], c.X[:, bass.ds(b * JT + j, 1), :])
                chain.link(last)
                nc.vector.tensor_copy(rinv[:, 0:1], stats[:, 0, 0:1])
                for j in range(JT):
                    last = nc.vector.bn_aggr(mv[:, j, :], stats[:, j, :])
                chain.link(last)
                nc.vector.tensor_scalar(rstd[:], mv[:, :, 1], 1e-5, None, ALU.add).then_inc(var_ready, 1)
                dve.wait_ge(rstd_ready, b + 1)
                for j in range(JT):
                    last = nc.vector.tensor_scalar(xln[:, j, :], c.X[:, bass.ds(b * JT + j, 1), :],
                                                   mv[:, j, 0:1], rstd[:, j:j + 1], ALU.subtract, ALU.mult)
                last.then_inc(xln_ready, 1)
                for m in range(JT):
                    dve.wait_ge(energy_ready, b * JT + m + 1)
                    nc.vector.reduce_max(nmax[:, m:m + 1], c.bank[energy_bank[m]][:], AX.X,
                                         negate=True).then_inc(max_ready, 1)
                dve.wait_ge(exp_ready, b * JT + JT)
                chain.link(nc.vector.reciprocal(rinv[:], rsum[:]))
                for m in range(JT):
                    last = nc.vector.tensor_scalar(prob[:, m, :], prob[:, m, :], rinv[:, m:m + 1], None, ALU.mult)
                last.then_inc(prob_ready, 1)
                for j in range(JT):
                    dve.wait_ge(mixed, b * JT + j + 1)
                    row = c.X[:, bass.ds(b * JT + j, 1), :]
                    nc.vector.tensor_tensor(row, row, c.bank[4 + j][:].unsqueeze(1), ALU.add).then_inc(added, 1)

        @block.scalar
        def _(act):
            act.wait_ge(w_turned, 1)
            for s in range(2):
                last = nc.scalar.copy(wT[:, s], c.bank[s][:, 0:CTX].rearrange("p (k d) -> p k d", k=KC))
            last.then_inc(w_copied, 1)
            with act.Fori(0, B) as b:
                act.wait_ge(qk_ready, b + 1)
                for s in range(2):
                    last = nc.scalar.activation(qkT[:, s, :], c.bank[4 + s][:], ACT.Identity, bias=bias[:, s:s + 1])
                last.then_inc(qkT_ready, 1)
                act.wait_ge(xln_turned, b + 1)
                for k in range(CC):
                    last = nc.scalar.copy(xlnT[:, k, :], c.bank[k][:])
                last.then_inc(xlnT_ready, 1)
                for m in range(JT):
                    act.wait_ge(max_ready, b * JT + m + 1)
                    nc.scalar.activation(prob[:, m, :], c.bank[energy_bank[m]][:], ACT.Exp, bias=nmax[:, m:m + 1],
                                         accum_out=rsum[:, m:m + 1]).then_inc(exp_ready, 1)
                act.wait_ge(prob_turned, b + 1)
                for k in range(CC):
                    last = nc.scalar.copy(attT[:, k, :], c.bank[k][:])
                last.then_inc(attT_ready, 1)

        @block.tensor
        def _(pe):
            pe.wait_ge(w_loaded, 64)
            for s in range(2):
                for k in range(KC):
                    last = nc.tensor.transpose(c.bank[s][:, k * P:(k + 1) * P], wq[:, s, k * P:(k + 1) * P], c.ident[:])
            last.then_inc(w_turned, 1)
            pe.wait_ge(w_copied, 1)
            with pe.Fori(0, B) as b:
                pe.wait_ge(added, b * JT)
                for s in range(2):
                    for k in range(KC):
                        last = nc.tensor.matmul(c.bank[4 + s][:], wT[:, s, k, :], c.ctxT[:, bass.ds(b, 1), k, :],
                                                start=(k == 0), stop=(k == KC - 1))
                last.then_inc(qk_ready, 1)
                pe.wait_ge(xln_ready, b + 1)
                for k in range(CC):
                    for j in range(JT):
                        last = nc.tensor.transpose(c.bank[k][:, j * P:(j + 1) * P], xln[:, j, k * P:(k + 1) * P],
                                                   c.ident[:])
                last.then_inc(xln_turned, 1)
                pe.wait_ge(qkT_ready, b + 1)
                for m in range(JT):
                    nc.tensor.matmul(c.bank[energy_bank[m]][:], qkT[:, 0, m * P:(m + 1) * P], qkT[:, 1, :],
                                     start=True, stop=True).then_inc(energy_ready, 1)
                pe.wait_ge(xlnT_ready, b + 1)
                pe.wait_ge(prob_ready, b + 1)
                for k in range(CC):
                    for m in range(JT):
                        last = nc.tensor.transpose(c.bank[k][:, m * P:(m + 1) * P], prob[:, m, k * P:(k + 1) * P],
                                                   c.ident[:])
                last.then_inc(prob_turned, 1)
                pe.wait_ge(attT_ready, b + 1)
                for j in range(JT):
                    for k in range(CC):
                        last = nc.tensor.matmul(c.bank[4 + j][:], xlnT[:, k, j * P:(j + 1) * P], attT[:, k, :],
                                                start=(k == 0), stop=(k == CC - 1))
                    last.then_inc(mixed, 1)


def norm_rows_into(nc, dve, chain, c, stats, mv, rstd, var_ready, rstd_ready, eps):
    with dve.Fori(0, B) as b:
        for j in range(JT):
            t = bass.ds(b * JT + j, 1)
            last = nc.vector.bn_stats(stats[:, t, :], c.X[:, t, :])
        last.then_inc(chain.sem, 1)
    chain.after_loop(B)
    for t in range(NT):
        last = nc.vector.bn_aggr(mv[:, t, :], stats[:, t, :])
    chain.link(last)
    nc.vector.tensor_scalar(rstd[:], mv[:, :, 1], eps, None, ALU.add).then_inc(var_ready, 1)
    dve.wait_ge(rstd_ready, 1)


def token_choice_ffn(nc, c):
    CAP = S // 8
    GROUPS = B * CAP // P
    DH = 128
    HALF = DH // 2
    KVH = 8
    QH = 2
    HEAD_COLS = (QH + 2) * DH
    SLOTS = GROUPS * P
    INNER = 2048
    with ExitStack() as kept:
        slot_hot_T = sbuf(nc, kept, "b_slot_hot_T", [P, NT, P])
        picked = sbuf(nc, kept, "b_picked", [P, GROUPS, D])
        x1 = sbuf(nc, kept, "b_x1", [P, GROUPS, D])
        angle = sbuf(nc, kept, "b_angle", [P, GROUPS, 3, HALF])
        gate = sbuf(nc, kept, "b_gate", [P, GROUPS])
        hT = sbuf(nc, kept, "b_hT", [P, CC, SLOTS])
        ln_w = sbuf(nc, kept, "b_ln_w", [P, 2, CC])
        heads_held = kept.enter_context(ExitStack())
        w_heads = sbuf(nc, heads_held, "b_w_heads", [P, CC, KVH, HEAD_COLS])
        heads_loaded, = sems(nc, c, "b_", "heads_loaded")

        with ExitStack() as stack:
            hs = sbuf(nc, stack, "b_hs", [P, NT, D])
            stats = sbuf(nc, stack, "b_stats", [P, NT, 6])
            mv = sbuf(nc, stack, "b_mv", [P, NT, 2])
            rstd = sbuf(nc, stack, "b_rstd", [P, NT])
            w_router = sbuf(nc, stack, "b_w_router", [P, D])
            score = sbuf(nc, stack, "b_score", [P, NT])
            score_T = sbuf(nc, stack, "b_score_T", [NT, P])
            scores_of_batch = sbuf(nc, stack, "b_scores_of_batch", [P, B, S])
            before = sbuf(nc, stack, "b_before", [P, JT, S])
            tri = sbuf(nc, stack, "b_tri", [P, P])
            ones = sbuf(nc, stack, "b_ones", [P, P])
            iota = sbuf(nc, stack, "b_iota", [P, P])
            slot_base = sbuf(nc, stack, "b_slot_base", [P, NT])
            rope = sbuf(nc, stack, "b_rope", [P, JT, DH])
            above = sbuf(nc, stack, "b_above", [P, NT])
            equal = sbuf(nc, stack, "b_equal", [P, NT])
            chosen = sbuf(nc, stack, "b_chosen", [P, NT])
            chosen_before = sbuf(nc, stack, "b_chosen_before", [P, NT])
            slot = sbuf(nc, stack, "b_slot", [P, NT])
            slot_hot = sbuf(nc, stack, "b_slot_hot", [P, NT, P])
            loaded, var_ready, rstd_ready, score_ready, score_turned, score_T_ready, score_stored, scores_spread = sems(
                nc, c, "b_", "loaded var_ready rstd_ready score_ready score_turned score_T_ready score_stored scores_spread")
            chosen_ready, slot_counted, hot_ready, gathered, hot_turned, chain_dve, gate_ready, gate_exp = sems(
                nc, c, "b_", "chosen_ready slot_counted hot_ready gathered hot_turned chain_dve gate_ready gate_exp")
            block = stack.enter_context(nc.Block())

            @block.sync
            def _(sp):
                for dst, src in ((w_router[:], c.dram["L0_ffn_w_router"].partition_broadcast(P)), (before[:], c.dram["i_before"]),
                                 (tri[:], c.dram["i_tri"]), (iota[:], c.dram["i_iota"]), (slot_base[:], c.dram["i_slot_base"]),
                                 (rope[:], c.dram["i_rope"].rearrange("(j p) d -> p j d", p=P)),
                                 (ln_w[:, 0], c.dram["L0_ffn_ln1_w"].rearrange("(k p) -> p k", p=P)),
                                 (ln_w[:, 1], c.dram["L0_ffn_ln2_w"].rearrange("(k p) -> p k", p=P))):
                    sp.dma_start(dst, src, allow_slow_non_contiguous=True).then_inc(loaded, 16)
                sp.wait_ge(score_T_ready, 1)
                sp.dma_start(c.dram["d_scores"], score_T[:]).then_inc(score_stored, 16)
                sp.wait_ge(score_stored, 16)
                sp.dma_start(scores_of_batch[:], c.dram["d_scores"].rearrange("(b j) p -> (b j p)", b=B).partition_broadcast(P)
                             .rearrange("q (b s) -> q b s", b=B)).then_inc(scores_spread, 16)

            @block.gpsimd
            def _(pool):
                nc.gpsimd.memset(ones[:], 1.0)
                pool.wait_ge(var_ready, 1)
                nc.gpsimd.tensor_tensor(rstd[:], rstd[:], c.minus_half[:, 0:NT], ALU.pow).then_inc(rstd_ready, 1)

            @block.vector
            def _(dve):
                chain = Chain(dve, chain_dve)
                dve.wait_ge(loaded, 8 * 16)
                norm_rows_into(nc, dve, chain, c, stats, mv, rstd, var_ready, rstd_ready, 1e-5)
                first = chain.n
                with dve.Fori(0, B) as b:
                    tiles = [bass.ds(b * JT + j, 1) for j in range(JT)]
                    for t in tiles:
                        last = nc.vector.tensor_scalar(hs[:, t, :], c.X[:, t, :], mv[:, t, 0:1], rstd[:, t],
                                                       ALU.subtract, ALU.mult)
                    last.then_inc(chain_dve, 1)
                    dve.wait_ge(chain_dve, b + first + 1)
                    for j, t in enumerate(tiles):
                        nc.vector.scalar_tensor_tensor(c.bank[4 + j][:].unsqueeze(1), hs[:, t, :], 1.0,
                                                       w_router[:].unsqueeze(1), ALU.mult, ALU.mult,
                                                       accum_out=score[:, t])
                        last = nc.vector.tensor_tensor(c.X[:, t, :], c.X[:, t, :], hs[:, t, :], ALU.add)
                    last.then_inc(score_ready, 1)
                chain.n += B
                dve.wait_ge(score_turned, 1)
                nc.vector.tensor_copy(score_T[:], c.bank[0][0:NT, 0:P]).then_inc(score_T_ready, 1)
                dve.wait_ge(score_T_ready, 1)
                dve.wait_ge(scores_spread, 16)
                first = chain.n
                with dve.Fori(0, B) as b:
                    dve.wait_ge(chain_dve, b + first)
                    of_batch = scores_of_batch[:, bass.ds(b, 1), :]
                    for j in range(JT):
                        t = bass.ds(b * JT + j, 1)
                        nc.vector.tensor_scalar(c.bank[j][:].unsqueeze(1), of_batch, score[:, t], None, ALU.is_gt,
                                                ALU.add, accum_out=above[:, t])
                        last = nc.vector.scalar_tensor_tensor(c.bank[4 + j][:].unsqueeze(1), of_batch, score[:, t],
                                                              before[:, j:j + 1, :], ALU.is_equal, ALU.mult,
                                                              accum_out=equal[:, t])
                    last.then_inc(chain_dve, 1)
                chain.after_loop(B)
                chain.link(nc.vector.tensor_tensor(above[:], above[:], equal[:], ALU.add))
                chain.link(nc.vector.tensor_scalar(chosen[:], above[:], float(CAP), None, ALU.is_lt))
                of = lambda tile, j: tile[:].rearrange("p (b j) -> p b j", j=JT)[:, :, j]
                chain.link(nc.vector.memset(chosen_before[:], 0.0))
                for j in range(1, JT):
                    last = nc.vector.tensor_tensor(of(chosen_before, j), of(chosen_before, j - 1), of(chosen, j - 1), ALU.add)
                    if j < JT - 1:
                        chain.link(last)
                last.then_inc(chosen_ready, 1)
                dve.wait_ge(slot_counted, 1)
                chain.link(nc.vector.tensor_tensor(slot[:], c.bank[1][:, 0:NT], slot_base[:], ALU.add))
                chain.link(nc.vector.tensor_tensor(slot[:], slot[:], chosen[:], ALU.mult))
                chain.link(nc.vector.tensor_scalar(slot[:], slot[:], -1.0, None, ALU.add))
                nc.vector.tensor_tensor(slot_hot[:], iota[:].unsqueeze(1).broadcast_to((P, NT, P)),
                                        slot[:].unsqueeze(2).broadcast_to((P, NT, P)), ALU.is_equal).then_inc(hot_ready, 1)
                dve.wait_ge(gathered, 1)
                for g in range(GROUPS):
                    last = nc.vector.tensor_copy(gate[:, g:g + 1], c.bank[2 + g][:, DH:DH + 1])
                last.then_inc(gate_ready, 1)
                for g in range(GROUPS):
                    nc.vector.tensor_copy(picked[:, g, :], c.bank[g][:])
                    nc.vector.tensor_copy(x1[:, g, :], c.bank[g][:])
                    nc.vector.tensor_copy(angle[:, g, 0:2, :], c.bank[2 + g][:, 0:DH].rearrange("p (a d) -> p a d", a=2))
                    nc.vector.tensor_scalar(angle[:, g, 2, :], c.bank[2 + g][:, HALF:DH], -1.0, None, ALU.mult)
                dve.wait_ge(gate_exp, 1)
                chain.link(nc.vector.tensor_scalar(gate[:], gate[:], 1.0, None, ALU.add))
                nc.vector.reciprocal(gate[:], gate[:])

            @block.scalar
            def _(act):
                for k in range(CC):
                    if k == CC // 2:
                        act.wait_ge(scores_spread, 16)
                    rows = slice(k * P, (k + 1) * P)
                    for src, at, cols in ((c.dram["L0_ffn_wq"], 0, QH * DH), (c.dram["L0_ffn_wk"], QH * DH, DH),
                                          (c.dram["L0_ffn_wv"], (QH + 1) * DH, DH)):
                        act.dma_start(w_heads[:, k, :, at:at + cols],
                                     src[rows, :].rearrange("p (h n) -> p h n", n=cols)).then_inc(heads_loaded, 16)
                act.wait_ge(gate_ready, 1)
                nc.scalar.activation(gate[:], gate[:], ACT.Exp, scale=-1.0).then_inc(gate_exp, 1)
                act.wait_ge(hot_turned, 1)
                for q in range(4):
                    nc.scalar.copy(slot_hot_T[:, 4 * q:4 * q + 4, :], c.bank[4 + q][:].rearrange("p (t s) -> p t s", t=4))

            @block.tensor
            def _(pe):
                pe.wait_ge(score_ready, B)
                nc.tensor.transpose(c.bank[0][0:NT, 0:P], score[:], c.ident[:]).then_inc(score_turned, 1)
                pe.wait_ge(chosen_ready, 1)
                nc.tensor.matmul(c.bank[1][:, 0:NT], tri[:], chosen[:], start=True, stop=False)
                nc.tensor.matmul(c.bank[1][:, 0:NT], ones[:], chosen_before[:], start=False, stop=True).then_inc(slot_counted, 1)
                pe.wait_ge(hot_ready, 1)
                per = NT // GROUPS
                for g in range(GROUPS):
                    for n in range(per):
                        t = g * per + n
                        nc.tensor.matmul(c.bank[g][:], slot_hot[:, t, :], hs[:, t, :], start=(n == 0), stop=(n == per - 1))
                    for n in range(per):
                        t = g * per + n
                        nc.tensor.matmul(c.bank[2 + g][:, 0:DH], slot_hot[:, t, :], rope[:, t % JT, :],
                                         start=(n == 0), stop=(n == per - 1))
                    for n in range(per):
                        t = g * per + n
                        last = nc.tensor.matmul(c.bank[2 + g][:, DH:DH + 1], slot_hot[:, t, :], score[:, t:t + 1],
                                                start=(n == 0), stop=(n == per - 1))
                last.then_inc(gathered, 1)
                for t in range(NT):
                    last = nc.tensor.transpose(c.bank[4 + t // 4][:, (t % 4) * P:(t % 4 + 1) * P], slot_hot[:, t, :], c.ident[:])
                last.then_inc(hot_turned, 1)

        def rms_turned(stack, pre, row, sq, which):
            ms = sbuf(nc, stack, pre + "ms", [P, GROUPS])
            squared, ms_ready, r_ready, row_ready, turned, hT_ready, chained = sems(
                nc, c, pre, "squared ms_ready r_ready row_ready turned hT_ready chained")

            def on_act(act):
                for g in range(GROUPS):
                    nc.scalar.activation(sq[:, g, :], row[:, g, :], ACT.Square, accum_out=ms[:, g:g + 1]).then_inc(squared, 1)
                act.wait_ge(turned, 1)
                for k in range(CC):
                    last = nc.scalar.mul(hT[:, k, :], c.bank[k // 2][:, (k % 2) * SLOTS:(k % 2 + 1) * SLOTS], ln_w[:, which, k:k + 1])
                last.then_inc(hT_ready, 1)

            def on_dve(dve):
                dve.wait_ge(squared, GROUPS)
                nc.vector.tensor_scalar(ms[:], ms[:], 1.0 / D, 1e-6, ALU.mult, ALU.add).then_inc(ms_ready, 1)
                dve.wait_ge(r_ready, 1)
                for g in range(GROUPS):
                    last = nc.vector.tensor_scalar(sq[:, g, :], row[:, g, :], ms[:, g:g + 1], None, ALU.mult)
                last.then_inc(row_ready, 1)

            def on_pool(pool):
                pool.wait_ge(ms_ready, 1)
                nc.gpsimd.tensor_tensor(ms[:], ms[:], c.minus_half[:, 0:GROUPS], ALU.pow).then_inc(r_ready, 1)

            def on_pe(pe):
                pe.wait_ge(row_ready, 1)
                for k in range(CC):
                    for g in range(GROUPS):
                        last = nc.tensor.transpose(c.bank[k // 2][:, (k % 2) * SLOTS + g * P:(k % 2) * SLOTS + (g + 1) * P],
                                                   sq[:, g, k * P:(k + 1) * P], c.ident[:])
                last.then_inc(turned, 1)
                pe.wait_ge(hT_ready, 1)

            return on_act, on_dve, on_pool, on_pe

        with ExitStack() as stack:
            w_o = sbuf(nc, stack, "b_w_o", [P, 2, QH, D])
            bias = sbuf(nc, stack, "b_bias", [P, KVH, HEAD_COLS])
            causal = sbuf(nc, stack, "b_causal", [P, GROUPS * SLOTS])
            qkv = sbuf(nc, stack, "b_qkv", [P, 2, GROUPS, HEAD_COLS])
            turn = sbuf(nc, stack, "b_turn", [P, GROUPS, QH + 1, DH])
            qk = sbuf(nc, stack, "b_qk", [P, GROUPS, QH + 1, DH])
            qT = sbuf(nc, stack, "b_qT", [P, QH, SLOTS])
            kT = sbuf(nc, stack, "b_kT", [P, SLOTS])
            prob = sbuf(nc, stack, "b_prob", [P, QH, GROUPS * SLOTS])
            probT = sbuf(nc, stack, "b_probT", [P, GROUPS, QH * SLOTS])
            oT = sbuf(nc, stack, "b_oT", [P, QH * SLOTS])
            nmax = sbuf(nc, stack, "b_nmax", [P, QH * GROUPS])
            rsum = sbuf(nc, stack, "b_rsum", [P, QH * GROUPS])
            wo_even, wo_odd, bias_loaded, projected, biased_ready, qk_ready, qk_turned, qkT_ready = sems(
                nc, c, "b_", "wo_even wo_odd bias_loaded projected biased_ready qk_ready qk_turned qkT_ready")
            scored, max_ready, exp_ready, prob_ready, prob_turned, probT_ready, valued, oT_ready, out_ready, added = sems(
                nc, c, "b_", "scored max_ready exp_ready prob_ready prob_turned probT_ready valued oT_ready out_ready added")
            wo_loaded = [wo_even, wo_odd]
            turn_ready, masked, inverted = sems(nc, c, "b_", "turn_ready masked inverted")
            block = stack.enter_context(nc.Block())
            rms_act, rms_dve, rms_pool, rms_pe = rms_turned(stack, "b_r1_", picked, qkv[:, 0], 0)
            SCALE = DH ** -0.5

            @block.sync
            def _(sp):
                for src, at, cols in ((c.dram["L0_ffn_bq"], 0, QH * DH), (c.dram["L0_ffn_bk"], QH * DH, DH),
                                      (c.dram["L0_ffn_bv"], (QH + 1) * DH, DH)):
                    sp.dma_start(bias[:, :, at:at + cols],
                                 src.partition_broadcast(P).rearrange("p (h n) -> p h n", n=cols)).then_inc(bias_loaded, 16)
                sp.dma_start(causal[:], c.dram["i_causal"]).then_inc(bias_loaded, 16)
                for h in range(KVH):
                    if h >= 2:
                        sp.wait_ge(out_ready, h - 1)
                    sp.dma_start(w_o[:, h % 2], c.dram["L0_ffn_wo"][h * QH * DH:(h + 1) * QH * DH, :].rearrange(
                        "(q d) n -> d q n", d=DH)).then_inc(wo_loaded[h % 2], 16)

            @block.gpsimd
            def _(pool):
                rms_pool(pool)

            @block.vector
            def _(dve):
                rms_dve(dve)
                dve.wait_ge(bias_loaded, 4 * 16)

                def rotate(h, par):
                    dve.wait_ge(projected, h + 1)
                    for g in range(GROUPS):
                        last = nc.vector.tensor_tensor(qkv[:, par, g, :].unsqueeze(1), c.bank[g][:].unsqueeze(1),
                                                       bias[:, bass.ds(h, 1), :], ALU.add)
                    last.then_inc(biased_ready, 1)
                    dve.wait_ge(biased_ready, h + 1)
                    rows = qkv[:, par, :, 0:(QH + 1) * DH]
                    cos = angle[:, :, 0:1, :].broadcast_to((P, GROUPS, 2 * (QH + 1), HALF))
                    nc.vector.tensor_tensor(qk[:].rearrange("p g h (a d) -> p g (h a) d", a=2),
                                            rows.rearrange("p g (n d) -> p g n d", d=HALF), cos, ALU.mult)
                    for half, which in ((0, 2), (1, 1)):
                        other = rows.rearrange("p g (h a d) -> p g h a d", a=2, d=HALF)[:, :, :, 1 - half, :]
                        sin = angle[:, :, which:which + 1, :].broadcast_to((P, GROUPS, QH + 1, HALF))
                        last = nc.vector.tensor_tensor(turn[:, :, :, half * HALF:(half + 1) * HALF], other, sin, ALU.mult)
                    last.then_inc(turn_ready, 1)
                    dve.wait_ge(turn_ready, h + 1)
                    nc.vector.tensor_tensor(qk[:], qk[:], turn[:], ALU.add).then_inc(qk_ready, 1)

                def add_out(h):
                    dve.wait_ge(out_ready, h + 1)
                    for g in range(GROUPS):
                        last = nc.vector.tensor_tensor(x1[:, g, :], x1[:, g, :], c.bank[6 + g][:], ALU.add)
                    last.then_inc(added, 1)

                def a_head(h, par, first=False, last_head=False):
                    dve.wait_ge(scored, h + 1)
                    for q in range(QH):
                        last = nc.vector.scalar_tensor_tensor(prob[:, q, :], c.bank[4 + q][:], SCALE, causal[:], ALU.mult, ALU.add)
                    last.then_inc(masked, 1)
                    dve.wait_ge(masked, h + 1)
                    nc.vector.reduce_max(nmax[:], prob[:].rearrange("p q (g s) -> p (q g) s", g=GROUPS), AX.X,
                                         negate=True).then_inc(max_ready, 1)
                    dve.wait_ge(exp_ready, h + 1)
                    nc.vector.reciprocal(rsum[:], rsum[:]).then_inc(inverted, 1)
                    dve.wait_ge(inverted, h + 1)
                    flat = prob[:].rearrange("p q (g s) -> p (q g) s", g=GROUPS)
                    nc.vector.tensor_tensor(flat, flat, rsum[:].unsqueeze(2).broadcast_to((P, QH * GROUPS, SLOTS)),
                                            ALU.mult).then_inc(prob_ready, 1)
                    if not last_head:
                        rotate(h + 1, 1 - par)
                    if not first:
                        add_out(h - 1)

                rotate(0, 0)
                a_head(0, 0, first=True)
                a_head(1, 1)
                with dve.Fori(1, KVH // 2 - 1) as n:
                    for par in range(2):
                        a_head(n * 2 + par, par)
                a_head(KVH - 2, 0)
                a_head(KVH - 1, 1, last_head=True)
                add_out(KVH - 1)

            @block.scalar
            def _(act):
                rms_act(act)
                with act.Fori(0, KVH) as h:
                    act.wait_ge(qk_turned, h + 1)
                    nc.scalar.copy(qT[:].rearrange("p q s -> p (q s)"), c.bank[2][:])
                    nc.scalar.copy(kT[:], c.bank[3][:, 0:SLOTS]).then_inc(qkT_ready, 1)
                    act.wait_ge(max_ready, h + 1)
                    for n in range(QH * GROUPS):
                        q, g = divmod(n, GROUPS)
                        part = prob[:, q, g * SLOTS:(g + 1) * SLOTS]
                        last = nc.scalar.activation(part, part, ACT.Exp, bias=nmax[:, n:n + 1], accum_out=rsum[:, n:n + 1])
                    last.then_inc(exp_ready, 1)
                    act.wait_ge(prob_turned, h + 1)
                    for n in range(GROUPS):
                        last = nc.scalar.copy(probT[:, n, :], c.bank[4 + n][:])
                    last.then_inc(probT_ready, 1)
                    act.wait_ge(valued, h + 1)
                    nc.scalar.copy(oT[:], c.bank[2][:]).then_inc(oT_ready, 1)

            @block.tensor
            def _(pe):
                rms_pe(pe)
                pe.wait_ge(heads_loaded, 3 * CC * 16)

                def project(h, first=False):
                    if not first:
                        pe.wait_ge(biased_ready, h)
                    for g in range(GROUPS):
                        for k in range(CC):
                            last = nc.tensor.matmul(c.bank[g][:], hT[:, k, g * P:(g + 1) * P], w_heads[:, k, bass.ds(h, 1), :],
                                                    start=(k == 0), stop=(k == CC - 1))
                    last.then_inc(projected, 1)

                def out(h, par, loads, first=False):
                    pe.wait_ge(oT_ready, h + 1)
                    pe.wait_ge(wo_loaded[par], loads * 16)
                    if not first:
                        pe.wait_ge(added, h)
                    for g in range(GROUPS):
                        for q in range(QH):
                            last = nc.tensor.matmul(c.bank[6 + g][:], oT[:, q * SLOTS + g * P:q * SLOTS + (g + 1) * P],
                                                    w_o[:, par, q, :], start=(q == 0), stop=(q == QH - 1))
                    last.then_inc(out_ready, 1)

                def a_head(h, par, loads=1, first=False, second=False, last_head=False):
                    pe.wait_ge(qk_ready, h + 1)
                    if not first:
                        pe.wait_ge(oT_ready, h)
                    for g in range(GROUPS):
                        for q in range(QH):
                            nc.tensor.transpose(c.bank[2][:, q * SLOTS + g * P:q * SLOTS + (g + 1) * P], qk[:, g, q, :], c.ident[:])
                        last = nc.tensor.transpose(c.bank[3][:, g * P:(g + 1) * P], qk[:, g, QH, :], c.ident[:])
                    last.then_inc(qk_turned, 1)
                    pe.wait_ge(qkT_ready, h + 1)
                    for q in range(QH):
                        for g in range(GROUPS):
                            last = nc.tensor.matmul(c.bank[4 + q][:, g * SLOTS:(g + 1) * SLOTS], qT[:, q, g * P:(g + 1) * P],
                                                    kT[:], start=True, stop=True)
                    last.then_inc(scored, 1)
                    if not last_head:
                        project(h + 1)
                    if not first:
                        out(h - 1, 1 - par, loads, second)
                    pe.wait_ge(prob_ready, h + 1)
                    for q in range(QH):
                        for g in range(GROUPS):
                            for n in range(GROUPS):
                                last = nc.tensor.transpose(c.bank[4 + n][:, q * SLOTS + g * P:q * SLOTS + (g + 1) * P],
                                                           prob[:, q, g * SLOTS + n * P:g * SLOTS + (n + 1) * P], c.ident[:])
                    last.then_inc(prob_turned, 1)
                    pe.wait_ge(probT_ready, h + 1)
                    for n in range(GROUPS):
                        last = nc.tensor.matmul(c.bank[2][:], qkv[:, par, n, (QH + 1) * DH:(QH + 2) * DH], probT[:, n, :],
                                                start=(n == 0), stop=(n == GROUPS - 1))
                    last.then_inc(valued, 1)

                project(0, first=True)
                a_head(0, 0, first=True)
                a_head(1, 1, second=True)
                with pe.Fori(1, KVH // 2 - 1) as n:
                    a_head(n * 2, 0, n)
                    a_head(n * 2 + 1, 1, n + 1)
                a_head(KVH - 2, 0, KVH // 2 - 1)
                a_head(KVH - 1, 1, KVH // 2, last_head=True)
                out(KVH - 1, 1, KVH // 2)
        heads_held.close()

        with ExitStack() as stack:
            PARTS = INNER // 512
            w_gate = sbuf(nc, stack, "b_w_gate", [P, CC, INNER])
            w_up = sbuf(nc, stack, "b_w_up", [P, CC, INNER])
            w_down = sbuf(nc, stack, "b_w_down", [P, INNER // P, D])
            act_g = sbuf(nc, stack, "b_act_g", [P, GROUPS, 512])
            mid = sbuf(nc, stack, "b_mid", [P, GROUPS, 512])
            midT = sbuf(nc, stack, "b_midT", [P, GROUPS, 512])
            part_loaded = sems(nc, c, "b_", " ".join(f"part{n}_loaded" for n in range(PARTS)))
            gated, upped, silu_ready, mid_ready, mid_turned, midT_ready, out_ready = sems(
                nc, c, "b_", "gated upped silu_ready mid_ready mid_turned midT_ready mlp_ready")
            chain_dve, diff_ready, spread, landed = sems(nc, c, "b_", "chain3 diff_ready spread landed")
            block = stack.enter_context(nc.Block())
            rms_act, rms_dve, rms_pool, rms_pe = rms_turned(stack, "b_r2_", x1, mid, 1)

            @block.sync
            def _(sp):
                for n in range(PARTS):
                    cols = slice(n * 512, (n + 1) * 512)
                    for dst, src in ((w_gate, c.dram["L0_ffn_w_gate"]), (w_up, c.dram["L0_ffn_w_up"])):
                        sp.dma_start(dst[:, :, cols], src.rearrange("(k p) n -> p k n", p=P)[:, :, cols]).then_inc(part_loaded[n], 16)
                    sp.dma_start(w_down[:, n * 4:(n + 1) * 4, :], c.dram["L0_ffn_w_down"].rearrange("(k p) n -> p k n", p=P)[
                        :, n * 4:(n + 1) * 4, :]).then_inc(part_loaded[n], 16)

            @block.gpsimd
            def _(pool):
                rms_pool(pool)

            @block.vector
            def _(dve):
                rms_dve(dve)
                with dve.Fori(0, PARTS) as n:
                    dve.wait_ge(silu_ready, n + 1)
                    dve.wait_ge(upped, n + 1)
                    for g in range(GROUPS):
                        last = nc.vector.tensor_tensor(mid[:, g, :], act_g[:, g, :], c.bank[2 + g][:], ALU.mult)
                    last.then_inc(mid_ready, 1)
                chain = Chain(dve, chain_dve)
                dve.wait_ge(out_ready, 1)
                for g in range(GROUPS):
                    last = nc.vector.tensor_tensor(x1[:, g, :], x1[:, g, :], c.bank[6 + g][:], ALU.add)
                chain.link(last)
                chain.link(nc.vector.tensor_tensor(x1[:], x1[:], picked[:], ALU.subtract))
                for g in range(GROUPS):
                    last = nc.vector.tensor_scalar(x1[:, g, :], x1[:, g, :], gate[:, g:g + 1], None, ALU.mult)
                last.then_inc(diff_ready, 1)
                for t in range(NT):
                    dve.wait_ge(spread, t + 1)
                    nc.vector.tensor_tensor(c.X[:, t, :], c.X[:, t, :], c.bank[t % 8][:], ALU.add).then_inc(landed, 1)

            @block.scalar
            def _(act):
                rms_act(act)
                with act.Fori(0, PARTS) as n:
                    act.wait_ge(gated, n + 1)
                    act.wait_ge(mid_ready, n)
                    for g in range(GROUPS):
                        last = nc.scalar.activation(act_g[:, g, :], c.bank[g][:], ACT.Silu)
                    last.then_inc(silu_ready, 1)
                    act.wait_ge(mid_turned, n + 1)
                    for g in range(GROUPS):
                        last = nc.scalar.copy(midT[:, g, :], c.bank[4 + g][:])
                    last.then_inc(midT_ready, 1)

            @block.tensor
            def _(pe):
                rms_pe(pe)

                def product(at, w, n):
                    for g in range(GROUPS):
                        for k in range(CC):
                            last = nc.tensor.matmul(c.bank[at + g][:], hT[:, k, g * P:(g + 1) * P],
                                                    w[:, k, n * 512:(n + 1) * 512], start=(k == 0), stop=(k == CC - 1))
                    return last

                def turn_mid(n):
                    pe.wait_ge(mid_ready, n + 1)
                    for g in range(GROUPS):
                        for k in range(4):
                            last = nc.tensor.transpose(c.bank[4 + g][:, k * P:(k + 1) * P], mid[:, g, k * P:(k + 1) * P], c.ident[:])
                    last.then_inc(mid_turned, 1)

                def down(n):
                    pe.wait_ge(midT_ready, n + 1)
                    for g in range(GROUPS):
                        for k in range(4):
                            last = nc.tensor.matmul(c.bank[6 + g][:], midT[:, g, k * P:(k + 1) * P], w_down[:, n * 4 + k, :],
                                                    start=(n == 0 and k == 0), stop=(n == PARTS - 1 and k == 3))
                    return last

                for n in range(PARTS):
                    pe.wait_ge(part_loaded[n], 3 * 16)
                    if n >= 1:
                        pe.wait_ge(silu_ready, n)
                    product(0, w_gate, n).then_inc(gated, 1)
                    if n >= 1:
                        turn_mid(n - 1)
                    product(2, w_up, n).then_inc(upped, 1)
                    if n >= 1:
                        down(n - 1)
                turn_mid(PARTS - 1)
                down(PARTS - 1).then_inc(out_ready, 1)
                pe.wait_ge(diff_ready, 1)
                for t in range(NT):
                    if t >= 8:
                        pe.wait_ge(landed, t - 7)
                    nc.tensor.matmul(c.bank[t % 8][:], slot_hot_T[:, t, :], x1[:, t // (NT // GROUPS), :],
                                     start=True, stop=True).then_inc(spread, 1)


X_H = 16
X_HD = D // X_H
X_LAST = 16


def project_heads(nc, c):
    H, HD, LAST = X_H, X_HD, X_LAST
    MAIN = S - LAST
    SCALE = HD ** -0.5
    with ExitStack() as stack:
        w_q = sbuf(nc, stack, "x_w_q", [P, CC, D])
        w_kv = sbuf(nc, stack, "x_w_kv", [P, KC, 2 * D])
        w_last = sbuf(nc, stack, "x_w_last", [P, KC, 2 * D])
        b_q = sbuf(nc, stack, "x_b_q", [P, D])
        b_o = sbuf(nc, stack, "x_b_o", [P, D])
        b_kv = sbuf(nc, stack, "x_b_kv", [P, 2 * D])
        b_kv_end = sbuf(nc, stack, "x_b_kv_end", [P, 2 * D])
        head_mean = sbuf(nc, stack, "x_head_mean", [P, H])
        affine = sbuf(nc, stack, "x_affine", [P, 3, 2, HD])
        stats = sbuf(nc, stack, "x_stats", [P, NT, 6])
        mv = sbuf(nc, stack, "x_mv", [P, NT, 2])
        rstd = sbuf(nc, stack, "x_rstd", [P, NT])
        rows = sbuf(nc, stack, "x_rows", [P, JT, D])
        squares = sbuf(nc, stack, "x_squares", [P, JT, D])
        rowsT = sbuf(nc, stack, "x_rowsT", [P, CC, S])
        ctx_b = sbuf(nc, stack, "x_ctx_b", [P, KC, S])
        ctx_end = sbuf(nc, stack, "x_ctx_end", [P, KC, P])
        ctx_last = sbuf(nc, stack, "x_ctx_last", [P, KC, P])
        q = sbuf(nc, stack, "x_q", [P, 2, JT, D])
        k = sbuf(nc, stack, "x_k", [P, 2, JT, D])
        v = sbuf(nc, stack, "x_v", [P, 2, JT, D])
        hrstd = sbuf(nc, stack, "x_hrstd", [P, 2, JT * H])
        loaded, kv_loaded, affine_loaded, var_ready, rstd_ready, rows_ready, rows_turned, rowsT_ready, ctx_ready = sems(
            nc, c, "x_", "loaded kv_loaded affine_loaded var_ready rstd_ready rows_ready rows_turned rowsT_ready ctx_ready")
        weights_ready, q_done, kv_done, q_copied, k_copied, hvar_ready, hrstd_ready, squared, dve_chain = sems(
            nc, c, "x_", "weights_ready q_done kv_done q_copied k_copied hvar_ready hrstd_ready squared dve_chain")
        q_scaled, k_scaled, k_used, zeroed, stored_even, stored_odd = sems(
            nc, c, "x_", "q_scaled k_scaled k_used zeroed stored_even stored_odd")
        stored = [stored_even, stored_odd]
        block = stack.enter_context(nc.Block())

        def by_head(ap, d=HD):
            return ap.rearrange("p (h d) -> p h d", d=d)

        def keys_of(ap):
            return ap.rearrange("p (h a d) -> p h a d", a=2, d=HD)[:, :, 0, :]

        @block.sync
        def _(sp):
            end = slice(P - LAST, P)
            as_kv = lambda tile: tile.rearrange("p (h a d) -> p h a d", a=2, d=HD)
            for dst, src in (
                    (w_q[:], c.dram["L1_xattn_Wq"].rearrange("(k p) n -> p k n", p=P)),
                    (w_kv[:, :, 0:D], c.dram["L1_xattn_Wk"].rearrange("(k p) n -> p k n", p=P)),
                    (w_kv[:, :, D:2 * D], c.dram["L1_xattn_Wv"].rearrange("(k p) n -> p k n", p=P)),
                    (w_last[:], c.dram["L1_xattn_Wkv_dca"].rearrange("(k p) n -> p k n", p=P)),
                    (b_q[:], c.dram["L1_xattn_bq"].partition_broadcast(P)),
                    (b_o[:], c.dram["L1_xattn_bo"].partition_broadcast(P))):
                sp.dma_start(dst, src).then_inc(loaded, 16)
            for tile, n in ((b_kv, P), (b_kv_end, P - LAST)):
                sp.dma_start(tile[0:n, 0:D], c.dram["L1_xattn_bk"].partition_broadcast(n)).then_inc(kv_loaded, 16)
                sp.dma_start(tile[0:n, D:2 * D], c.dram["L1_xattn_bv"].partition_broadcast(n)).then_inc(kv_loaded, 16)
            for a in range(2):
                sp.dma_start(as_kv(b_kv_end[end, :])[:, :, a, :],
                             c.dram["L1_xattn_bkv_dca"][a * D:(a + 1) * D].partition_broadcast(LAST)
                             .rearrange("p (h d) -> p h d", d=HD)).then_inc(kv_loaded, 16)
            for n, at, rows_, name in ((0, 0, slice(0, P), "qn_w"), (0, 1, slice(0, P), "qn_b"),
                                       (1, 0, slice(0, P), "kn_w"), (1, 1, slice(0, P), "kn_b"),
                                       (2, 0, slice(0, P - LAST), "kn_w"), (2, 1, slice(0, P - LAST), "kn_b"),
                                       (2, 0, end, "kn_dca_w"), (2, 1, end, "kn_dca_b")):
                sp.dma_start(affine[rows_, n, at, :], c.dram["L1_xattn_" + name].partition_broadcast(
                    rows_.stop - rows_.start)).then_inc(affine_loaded, 16)
            for b in range(B):
                for tile, name, ready in ((v, "d_xv", k_copied), (q, "d_xq", q_scaled), (k, "d_xk", k_scaled)):
                    sp.wait_ge(ready, (b + 1) * (JT if ready is k_copied else 1))
                    sp.dma_start(c.dram[name][b].rearrange("(j p) d -> p j d", p=P), tile[:, b % 2]).then_inc(stored[b % 2], 16)
            for par in range(2):
                sp.wait_ge(stored[par], 16 * 3 * B // 2)

        @block.gpsimd
        def _(pool):
            nc.gpsimd.memset(ctx_end[:, :, P - LAST:P], 0.0)
            nc.gpsimd.memset(ctx_last[:, :, 0:P - LAST], 0.0).then_inc(zeroed, 1)
            pool.wait_ge(var_ready, 1)
            nc.gpsimd.tensor_tensor(rstd[:], rstd[:], c.minus_half[:, 0:NT], ALU.pow).then_inc(rstd_ready, 1)
            with pool.Fori(0, B) as b:
                for a in range(2):
                    pool.wait_ge(hvar_ready, b * 2 + a + 1)
                    nc.gpsimd.tensor_tensor(hrstd[:, a, :], hrstd[:, a, :], c.minus_half[:, 0:JT * H],
                                            ALU.pow).then_inc(hrstd_ready, 1)

        @block.vector
        def _(dve):
            chain = Chain(dve, dve_chain)
            norm_rows_into(nc, dve, chain, c, stats, mv, rstd, var_ready, rstd_ready, 1e-5)

            def write_rows(b):
                for j in range(JT):
                    t = b * JT + j
                    last = nc.vector.tensor_scalar(rows[:, j, :], c.X[:, t, :], mv[:, t, 0:1], rstd[:, t:t + 1],
                                                   ALU.subtract, ALU.mult)
                last.then_inc(rows_ready, 1)

            def sum_squares(b, a):
                dve.wait_ge(squared, b * 2 + a + 1)
                chain.link(nc.vector.reduce_sum(hrstd[:, a, :], squares[:].rearrange("p j (h d) -> p (j h) d", d=HD), AX.X))
                nc.vector.tensor_scalar(hrstd[:, a, :], hrstd[:, a, :], 1.0 / HD, 1e-6, ALU.mult, ALU.add).then_inc(hvar_ready, 1)

            def finish(b, a, tile, scaled):
                dve.wait_ge(hrstd_ready, b * 2 + a + 1)
                heads = tile.rearrange("p j (h d) -> p (j h) d", d=HD)
                chain.link(nc.vector.tensor_tensor(heads, heads, hrstd[:, a, :].unsqueeze(2).broadcast_to((P, JT * H, HD)), ALU.mult))
                for at, op in enumerate((ALU.mult, ALU.add)):
                    if a == 0:
                        last = nc.vector.tensor_tensor(heads, heads, affine[:, 0, at, :].unsqueeze(1).broadcast_to((P, JT * H, HD)), op)
                    else:
                        most = tile[:, 0:JT - 1, :].rearrange("p j (h d) -> p (j h) d", d=HD)
                        nc.vector.tensor_tensor(most, most, affine[:, 1, at, :].unsqueeze(1).broadcast_to((P, (JT - 1) * H, HD)), op)
                        end = by_head(tile[:, JT - 1, :])
                        last = nc.vector.tensor_tensor(end, end, affine[:, 2, at, :].unsqueeze(1).broadcast_to((P, H, HD)), op)
                    if at == 0:
                        chain.link(last)
                    else:
                        last.then_inc(scaled, 1)

            write_rows(0)
            dve.wait_ge(loaded, 6 * 16)
            dve.wait_ge(kv_loaded, 6 * 16)
            for tile in [by_head(w_q[:, n, :]) for n in range(CC)] + [keys_of(w_kv[:, n, :]) for n in range(KC)] + [
                    by_head(w_last[:, n, 0:D]) for n in range(KC)] + [by_head(b_q[:]), keys_of(b_kv[:]), keys_of(b_kv_end[:])]:
                mean = head_mean[:]
                chain.link(nc.vector.reduce_sum(mean, tile, AX.X))
                chain.link(nc.vector.tensor_scalar(mean, mean, 1.0 / HD, None, ALU.mult))
                chain.link(nc.vector.tensor_tensor(tile, tile, mean.unsqueeze(2).broadcast_to((P, H, HD)), ALU.subtract))
            dve.wait_ge(affine_loaded, 8 * 16)
            chain.link(nc.vector.tensor_scalar(affine[:, 0], affine[:, 0], SCALE, None, ALU.mult))
            nc.vector.tensor_copy(head_mean[:, 0:1], affine[:, 0, 0, 0:1]).then_inc(weights_ready, 1)
            for b in range(B):
                par = b % 2
                if b >= 2:
                    dve.wait_ge(stored[par], 16 * 3)
                for j in range(JT):
                    dve.wait_ge(q_done, b * JT + j + 1)
                    nc.vector.tensor_tensor(q[:, par, j, :], c.bank[4 + j], b_q[:], ALU.add).then_inc(q_copied, 1)
                for j in range(JT):
                    t = b * JT + j
                    nc.vector.tensor_tensor(c.X[:, t, :], c.X[:, t, :], b_o[:], ALU.add)
                sum_squares(b, 0)
                for j in range(JT):
                    dve.wait_ge(kv_done, b * JT + j + 1)
                    bias = (b_kv if j < JT - 1 else b_kv_end)[:].rearrange("p (h a d) -> p h a d", a=2, d=HD)
                    nc.vector.tensor_tensor(by_head(v[:, par, j, :]), by_head(c.bank[2 * (j % 2) + 1]), bias[:, :, 1, :], ALU.add)
                    nc.vector.tensor_tensor(by_head(k[:, par, j, :]), by_head(c.bank[2 * (j % 2)]),
                                            bias[:, :, 0, :], ALU.add).then_inc(k_copied, 1)
                if b + 1 < B:
                    dve.wait_ge(rows_turned, b + 1)
                    write_rows(b + 1)
                sum_squares(b, 1)
                finish(b, 0, q[:, par], q_scaled)
                finish(b, 1, k[:, par], k_scaled)

        @block.scalar
        def _(act):
            for b in range(B):
                if b >= 1:
                    act.wait_ge(k_used, b)
                nc.scalar.copy(ctx_b[:], c.ctxT[:, b])
                nc.scalar.copy(ctx_end[:, :, 0:P - LAST], c.ctxT[:, b, :, S - P:MAIN])
                nc.scalar.copy(ctx_last[:, :, P - LAST:P], c.ctxT[:, b, :, MAIN:S]).then_inc(ctx_ready, 1)
                act.wait_ge(rows_turned, b + 1)
                for n in range(CC):
                    last = nc.scalar.copy(rowsT[:, n, :], c.bank[n])
                last.then_inc(rowsT_ready, 1)
                for a, (tile, copied) in enumerate(((q, q_copied), (k, k_copied))):
                    act.wait_ge(copied, b * JT + JT)
                    if b > 0 or a > 0:
                        act.wait_ge(hvar_ready, b * 2 + a)
                    nc.scalar.activation(squares[:], tile[:, b % 2], ACT.Square).then_inc(squared, 1)

        @block.tensor
        def _(pe):
            pe.wait_ge(zeroed, 1)
            for b in range(B):
                pe.wait_ge(rows_ready, b + 1)
                if b >= 1:
                    pe.wait_ge(k_copied, b * JT)
                for n in range(CC):
                    for j in range(JT):
                        last = nc.tensor.transpose(c.bank[n][:, j * P:(j + 1) * P], rows[:, j, n * P:(n + 1) * P], c.ident[:])
                last.then_inc(rows_turned, 1)
                pe.wait_ge(rowsT_ready, b + 1)
                if b == 0:
                    pe.wait_ge(weights_ready, 1)
                if b >= 1:
                    pe.wait_ge(q_copied, b * JT)
                for j in range(JT):
                    for n in range(CC):
                        last = nc.tensor.matmul(c.bank[4 + j], rowsT[:, n, j * P:(j + 1) * P], w_q[:, n, :],
                                                start=(n == 0), stop=(n == CC - 1))
                    last.then_inc(q_done, 1)
                pe.wait_ge(ctx_ready, b + 1)
                for j in range(JT):
                    if j >= 2:
                        pe.wait_ge(k_copied, b * JT + j - 1)
                    for a in range(2):
                        bank = by_head(c.bank[2 * (j % 2) + a])
                        for n in range(KC):
                            main = w_kv[:, n, :].rearrange("p (h a d) -> p h a d", a=2, d=HD)[:, :, a, :]
                            if j < JT - 1:
                                last = nc.tensor.matmul(bank, ctx_b[:, n, j * P:(j + 1) * P], main, start=(n == 0), stop=(n == KC - 1))
                            else:
                                nc.tensor.matmul(bank, ctx_end[:, n, :], main, start=(n == 0), stop=False)
                                last = nc.tensor.matmul(bank, ctx_last[:, n, :], by_head(w_last[:, n, a * D:(a + 1) * D]),
                                                        start=False, stop=(n == KC - 1))
                    last.then_inc(kv_done, 1)
                    if j == JT - 1:
                        nc.tensor.nop().then_inc(k_used, 1)


def context_attention(nc, c):
    H, HD, LAST = X_H, X_HD, X_LAST
    MAIN = S - LAST
    HPG = P // HD
    GROUPS = B * H // HPG
    PAIRS = HPG * JT // 2
    PARTS = 2 * HPG
    RING = 4
    with ExitStack() as stack:
        w_o = sbuf(nc, stack, "y_w_o", [P, CC, D])
        zeros = sbuf(nc, stack, "y_zeros", [P, JT, D])
        qk = [sbuf(nc, stack, "y_q", [P, 2, JT, P]), sbuf(nc, stack, "y_k", [P, 2, JT, P])]
        mixedT = sbuf(nc, stack, "y_mixedT", [P, GROUPS, S])
        part = sbuf(nc, stack, "y_part", [P, 2, JT, 4, HD], F32R)
        stacked = [sbuf(nc, stack, "y_q_stacked", [P, HPG, S], F32R), sbuf(nc, stack, "y_k_stacked", [P, HPG, S], F32R)]
        ident_r = sbuf(nc, stack, "y_ident_r", [P, P], F32R)
        group_v = sbuf(nc, stack, "y_group_v", [P, JT, P])
        prob = sbuf(nc, stack, "y_prob", [P, RING, 2, S])
        probT = sbuf(nc, stack, "y_probT", [P, HPG, JT, S])
        last_part = sbuf(nc, stack, "y_last_part", [P, RING, 2, LAST])
        nmax = sbuf(nc, stack, "y_nmax", [P, RING, 2, 2])
        rsum = sbuf(nc, stack, "y_rsum", [P, RING, 2, 2])
        rinv = sbuf(nc, stack, "y_rinv", [P, RING, 2, 2])
        w_loaded, loaded_even, loaded_odd, v_loaded, hi_ready, part_ready, part_turned, q_stacked, k_stacked = sems(
            nc, c, "y_", "w_loaded loaded_even loaded_odd v_loaded hi_ready part_ready part_turned q_stacked k_stacked")
        scored, max_found, max_ready, exp_ready, summed, rinv_ready, prob_ready, prob_turned, probT_act, probT_dve = sems(
            nc, c, "y_", "scored max_found max_ready exp_ready summed rinv_ready prob_ready prob_turned probT_act probT_dve")
        valued, mixedT_ready, ident_ready, out_ready, added, zeros_set, zeros_stored = sems(
            nc, c, "y_", "valued mixedT_ready ident_ready out_ready added zeros_set zeros_stored")
        loaded = [loaded_even, loaded_odd]
        stacked_ready = [q_stacked, k_stacked]
        block = stack.enter_context(nc.Block())
        SCORES, PROB_T, PART_T, VALUES = 0, 4, 6, 7

        @block.sync
        def _(sp):
            def of_group(name, group):
                b, hc = group // (H // HPG), group % (H // HPG)
                return c.dram[name][b, :, hc * P:(hc + 1) * P].rearrange("(j p) d -> p j d", p=P)

            def load(group):
                for kind, name in enumerate(("d_xq", "d_xk")):
                    sp.dma_start(qk[kind][:, group % 2], of_group(name, group)).then_inc(loaded[group % 2], 16)

            blank = c.dram["d_sorted"].rearrange("(n j p) d -> n p j d", p=P, j=JT)
            blanks = ROUTED_TILES // JT
            for group in range(2):
                load(group)
            sp.dma_start(group_v[:], of_group("d_xv", 0)).then_inc(v_loaded, 16)
            sp.dma_start(w_o[:], c.dram["L1_xattn_Wo"].rearrange("(k p) n -> p k n", p=P)).then_inc(w_loaded, 16)
            sp.wait_ge(zeros_set, 1)
            for group in range(1, GROUPS):
                if group + 1 < GROUPS:
                    sp.wait_ge(part_ready, PARTS * group)
                    load(group + 1)
                sp.wait_ge(valued, group)
                sp.dma_start(group_v[:], of_group("d_xv", group)).then_inc(v_loaded, 16)
                for n in range(blanks * (group - 1) // (GROUPS - 1), blanks * group // (GROUPS - 1)):
                    sp.dma_start(blank[n], zeros[:]).then_inc(zeros_stored, 16)
            sp.wait_ge(zeros_stored, 16 * blanks)

        @block.gpsimd
        def _(pool):
            nc.gpsimd.memset(zeros[:], 0.0).then_inc(zeros_set, 1)
            with pool.Fori(0, GROUPS * PAIRS // RING) as n:
                for r in range(RING):
                    pool.wait_ge(rinv_ready, n * RING + r + 1)
                    nc.gpsimd.tensor_tensor(prob[:, r, :, MAIN:S], last_part[:, r],
                                            rinv[:, r, 1, :].unsqueeze(2).broadcast_to((P, 2, LAST)), ALU.mult)
                    nc.gpsimd.tensor_tensor(prob[:, r, :, 0:MAIN], prob[:, r, :, 0:MAIN],
                                            rinv[:, r, 0, :].unsqueeze(2).broadcast_to((P, 2, MAIN)),
                                            ALU.mult).then_inc(prob_ready, 1)

        @block.vector
        def _(dve):
            nc.vector.tensor_copy(ident_r[:], c.ident[:]).then_inc(ident_ready, 1)

            def write_part(group, i):
                kind, ring, h = i % 2, i % 2, i // 2
                source = qk[kind][:, bass.ds(group % 2, 1), :, h * HD:(h + 1) * HD].rearrange("p a j d -> p (a j) d")
                if kind == 0:
                    hi, lo = part[:, ring, :, 0:2, :], part[:, ring, :, 2:4, :]
                else:
                    hi, lo = part[:, ring, :, 0:4:2, :], part[:, ring, :, 1:4:2, :]
                wide = source.unsqueeze(2).broadcast_to((P, JT, 2, HD))
                nc.vector.tensor_copy(hi, wide).then_inc(hi_ready, 1)
                dve.wait_ge(hi_ready, group * PARTS + i + 1)
                nc.vector.tensor_tensor(lo, wide, hi.bitcast(F32), ALU.subtract).then_inc(part_ready, 1)

            def find_max(group, pair, first=False):
                dve.wait_ge(scored, group * PAIRS + pair + 1)
                r = pair % RING
                if pair >= RING or not first:
                    dve.wait_ge(prob_ready, group * PAIRS + pair - RING + 1)
                banks = c.psum[:, SCORES + 2 * (pair % 2):SCORES + 2 * (pair % 2) + 2, :]
                nc.vector.reduce_max(nmax[:, r, 1, :], banks[:, :, MAIN:S], AX.X, negate=True)
                nc.vector.reduce_max(nmax[:, r, 0, :], banks[:, :, 0:MAIN], AX.X, negate=True).then_inc(max_found, 1)
                dve.wait_ge(max_found, group * PAIRS + pair + 1)
                nc.vector.tensor_tensor(last_part[:, r], banks[:, :, MAIN:S],
                                        nmax[:, r, 1, :].unsqueeze(2).broadcast_to((P, 2, LAST)), ALU.add).then_inc(max_ready, 1)

            def invert_sums(group, pair):
                dve.wait_ge(exp_ready, group * PAIRS + pair + 1)
                r = pair % RING
                nc.vector.reduce_sum(rsum[:, r, 1, :], last_part[:, r], AX.X).then_inc(summed, 1)
                dve.wait_ge(summed, group * PAIRS + pair + 1)
                nc.vector.reciprocal(rinv[:, r], rsum[:, r]).then_inc(rinv_ready, 1)

            def copy_probT(group, pair):
                h, j = pair // 2 % HPG, pair % 2 * 2 + 1
                dve.wait_ge(prob_turned, (group * PAIRS + pair) * 2 + 2)
                nc.vector.tensor_copy(probT[:, h, :, j * P:(j + 1) * P],
                                      c.bank[PROB_T + 1].rearrange("p (n q) -> p n q", q=P)).then_inc(probT_dve, 1)

            def copy_values(group):
                dve.wait_ge(valued, group + 1)
                nc.vector.tensor_copy(mixedT[:, bass.ds(group, 1), :], c.bank[VALUES].unsqueeze(1)).then_inc(mixedT_ready, 1)

            def a_group(group, parity=None, first=False, more=True):
                for s in range(PAIRS):
                    if s + 1 < PAIRS or more:
                        find_max(group, s + 1, first)
                    if more:
                        if s == 0:
                            dve.wait_ge(loaded[parity], LOADS * ((group + 1) // 2 + 1))
                        dve.wait_ge(part_turned, (group + 1) * PARTS + s - 1)
                        write_part(group + 1, s)
                    if s >= 3 or not first:
                        copy_probT(group, s - 3)
                    invert_sums(group, s)
                    if s == 4 and not first:
                        copy_values(group - 1)

            LOADS = 2 * 16
            dve.wait_ge(loaded[0], LOADS)
            for i in range(PARTS):
                if i >= 2:
                    dve.wait_ge(part_turned, i - 1)
                write_part(0, i)
            find_max(0, 0, True)
            a_group(0, 1, first=True)
            with dve.Fori(0, (GROUPS - 2) // 2) as n:
                for par in range(2):
                    a_group(n * 2 + 1 + par, par)
            final = GROUPS - 1
            a_group(final, more=False)
            for pair in range(PAIRS - 3, PAIRS):
                copy_probT(final, pair)
            copy_values(final)
            for t in range(NT):
                dve.wait_ge(out_ready, t + 1)
                nc.vector.tensor_tensor(c.X[:, t, :], c.X[:, t, :], c.bank[t % 8], ALU.add).then_inc(added, 1)

        @block.scalar
        def _(act):
            def copy_part(group, i):
                act.wait_ge(part_turned, group * PARTS + i + 1)
                nc.scalar.copy(stacked[i % 2][:, i // 2 % HPG, :], c.bank[PART_T]).then_inc(stacked_ready[i % 2], 1)

            def exponentials(group, pair):
                act.wait_ge(max_ready, group * PAIRS + pair + 1)
                r = pair % RING
                nc.scalar.activation(last_part[:, r], last_part[:, r], ACT.Exp)
                for n in range(2):
                    last = nc.scalar.activation(prob[:, r, n, 0:MAIN], c.bank[SCORES + 2 * (pair % 2) + n][:, 0:MAIN], ACT.Exp,
                                                bias=nmax[:, r, 0, n:n + 1], accum_out=rsum[:, r, 0, n:n + 1])
                last.then_inc(exp_ready, 1)

            def copy_probT(group, pair):
                h, j = pair // 2 % HPG, pair % 2 * 2
                act.wait_ge(prob_turned, (group * PAIRS + pair) * 2 + 1)
                nc.scalar.copy(probT[:, h, :, j * P:(j + 1) * P],
                               c.bank[PROB_T].rearrange("p (n q) -> p n q", q=P)).then_inc(probT_act, 1)

            def a_group(group, first=False, more=True):
                for s in range(PAIRS):
                    if s >= RING or not first:
                        act.wait_ge(prob_turned, (group * PAIRS + s - RING) * 2 + 2)
                    exponentials(group, s)
                    if s >= 3 or not first:
                        copy_probT(group, s - 3)
                    if (s > 0 and more) or (s == 0 and not first):
                        copy_part(group + (1 if s > 0 else 0), (s - 1) % PARTS)

            for i in range(PARTS):
                copy_part(0, i)
            a_group(0, first=True)
            with act.Fori(1, GROUPS - 1) as group:
                a_group(group)
            final = GROUPS - 1
            a_group(final, more=False)
            for pair in range(PAIRS - 3, PAIRS):
                copy_probT(final, pair)

        @block.tensor
        def _(pe):
            def turn_part(group, i, first=False):
                pe.wait_ge(part_ready, group * PARTS + i + 1)
                if i >= 1:
                    pe.wait_ge(stacked_ready[(i + 1) % 2], group * HPG + (i - 1) // 2 + 1)
                elif not first:
                    pe.wait_ge(k_stacked, group * HPG)
                for j in range(JT):
                    last = nc.tensor.transpose(c.bank[PART_T][:, j * P:(j + 1) * P].bitcast(F32R),
                                               part[:, i % 2, j].rearrange("p r d -> p (r d)"), ident_r[:])
                last.then_inc(part_turned, 1)

            def scores(group, pair):
                h = pair // 2 % HPG
                if pair % 2 == 0:
                    for ready in stacked_ready:
                        pe.wait_ge(ready, group * HPG + pair // 2 + 1)
                for n in range(2):
                    j = pair % 2 * 2 + n
                    last = nc.tensor.matmul(c.bank[SCORES + j], stacked[0][:, h, j * P:(j + 1) * P], stacked[1][:, h, :],
                                            start=True, stop=True)
                last.then_inc(scored, 1)

            def turn(group, pair, bank_used=True):
                pe.wait_ge(prob_ready, group * PAIRS + pair + 1)
                for n, copied in enumerate((probT_act, probT_dve)):
                    if bank_used:
                        pe.wait_ge(copied, group * PAIRS + pair)
                    for k in range(JT):
                        last = nc.tensor.transpose(c.bank[PROB_T + n][:, k * P:(k + 1) * P],
                                                   prob[:, pair % RING, n, k * P:(k + 1) * P], c.ident[:])
                    last.then_inc(prob_turned, 1)

            def values(group, first=False):
                pe.wait_ge(probT_act, group * PAIRS + PAIRS)
                pe.wait_ge(probT_dve, group * PAIRS + PAIRS)
                pe.wait_ge(v_loaded, group * 16 + 16)
                if not first:
                    pe.wait_ge(mixedT_ready, group)
                for n in range(JT):
                    for h in range(HPG):
                        last = nc.tensor.matmul(c.bank[VALUES][h * HD:(h + 1) * HD, :], group_v[:, n, h * HD:(h + 1) * HD],
                                                probT[:, h, n, :], start=(n == 0), stop=(n == JT - 1),
                                                tile_position=(0, h * HD))
                last.then_inc(valued, 1)

            def a_group(group, first=False, second=False, more=True):
                for s in range(PAIRS):
                    if (s > 0 and more) or (s == 0 and not first):
                        turn_part(group + (1 if s > 0 else 0), (s - 1) % PARTS)
                    if s == 2 and not first:
                        values(group - 1, second)
                    if s + 2 < PAIRS or more:
                        pe.wait_ge(exp_ready, group * PAIRS + s + 1)
                        scores(group, s + 2)
                    if s >= 2 or not first:
                        turn(group, s - 2, bank_used=(s > 2 or not first))

            pe.wait_ge(ident_ready, 1)
            for i in range(PARTS):
                turn_part(0, i, first=True)
            for pair in range(2):
                scores(0, pair)
            a_group(0, first=True)
            a_group(1, second=True)
            with pe.Fori(2, GROUPS - 1) as group:
                a_group(group)
            final = GROUPS - 1
            a_group(final, more=False)
            for pair in range(PAIRS - 2, PAIRS):
                turn(final, pair)
            values(final)
            pe.wait_ge(w_loaded, 16)
            pe.wait_ge(mixedT_ready, GROUPS)
            pe.wait_ge(probT_act, GROUPS * PAIRS)
            for t in range(NT):
                if t >= 8:
                    pe.wait_ge(added, t - 7)
                for n in range(CC):
                    j = t % JT
                    last = nc.tensor.matmul(c.bank[t % 8], mixedT[:, t // JT * CC + n, j * P:(j + 1) * P], w_o[:, n, :],
                                            start=(n == 0), stop=(n == CC - 1))
                last.then_inc(out_ready, 1)


E_ = 32
TOPK = 6
EG = 4
EPG = E_ // EG
M = 352
SHARED = 2
SHARED_TILES = SHARED * NT
ROUTED_TILES = TOK * TOPK // P + E_
TILES = SHARED_TILES + ROUTED_TILES


def route_tokens(nc, c, hs, slots, y_slots, weights, tile_expert, tiles_through):
    with ExitStack() as stack:
        stats = sbuf(nc, stack, "r_stats", [P, NT, 6])
        mv = sbuf(nc, stack, "r_mv", [P, NT, 2])
        rstd = sbuf(nc, stack, "r_rstd", [P, NT])
        rows = sbuf(nc, stack, "r_rows", [P, JT, D])
        rowsT = sbuf(nc, stack, "r_rowsT", [P, CC, S])
        w_gate = sbuf(nc, stack, "r_w_gate", [P, CC, E_])
        tri = sbuf(nc, stack, "r_tri", [P, P])
        ones = sbuf(nc, stack, "r_ones", [P, P])
        iota = sbuf(nc, stack, "r_iota", [P, P])
        part = sbuf(nc, stack, "r_part", [P, 1])
        earlier = sbuf(nc, stack, "r_earlier", [P, EG, EG])
        steps = sbuf(nc, stack, "r_steps", [P, NT])
        score = sbuf(nc, stack, "r_score", [P, NT, E_])
        best = sbuf(nc, stack, "r_best", [P, NT, EG])
        pair = sbuf(nc, stack, "r_pair", [P, NT, EG, EG])
        pair2 = sbuf(nc, stack, "r_pair2", [P, NT, EG, EG])
        top = sbuf(nc, stack, "r_top", [P, NT, 8])
        index = sbuf(nc, stack, "r_index", [P, NT, 8], U32)
        indexf = sbuf(nc, stack, "r_indexf", [P, NT, 8])
        hot = sbuf(nc, stack, "r_hot", [P, TOPK, NT, E_])
        member = sbuf(nc, stack, "r_member", [P, NT, E_])
        members_before = sbuf(nc, stack, "r_members_before", [P, NT, E_])
        place = sbuf(nc, stack, "r_place", [P, NT, E_])
        work = sbuf(nc, stack, "r_work", [P, NT, E_])
        slotsf = sbuf(nc, stack, "r_slotsf", [P, NT, TOPK])
        wsum = sbuf(nc, stack, "r_wsum", [P, NT])
        count = sbuf(nc, stack, "r_count", [P, E_])
        over = sbuf(nc, stack, "r_over", [P, E_, NT])
        tiles = sbuf(nc, stack, "r_tiles", [P, E_])
        through = sbuf(nc, stack, "r_through", [P, E_])
        first_slot = sbuf(nc, stack, "r_first_slot", [P, E_])
        expert_of = sbuf(nc, stack, "r_expert_of", [P, 1])
        small = sbuf(nc, stack, "r_small", [P, E_])
        loaded, var_ready, rstd_ready, rows_ready, rows_turned, rowsT_ready, gated, taken = sems(
            nc, c, "r_", "loaded var_ready rstd_ready rows_ready rows_turned rowsT_ready gated taken")
        exped, members_ready, counted, expert_ready, expert_turned, dve_chain, hs_stored, exp_ready, ones_set, hs_ready = sems(
            nc, c, "r_", "exped members_ready counted expert_ready expert_turned dve_chain hs_stored exp_ready ones_set hs_ready")
        block = stack.enter_context(nc.Block())

        @block.sync
        def _(sp):
            for dst, src in ((w_gate[:], c.dram["L1_ffn_gate_w"].rearrange("(k p) n -> p k n", p=P)), (tri[:], c.dram["i_tri"]),
                             (iota[:], c.dram["i_iota"]), (part[:], c.dram["i_part"]), (earlier[:], c.dram["i_earlier"]), (steps[:], c.dram["i_steps"])):
                sp.dma_start(dst, src).then_inc(loaded, 16)
            sp.wait_ge(hs_ready, B)
            sp.dma_start(c.dram["d_hs"].rearrange("(t p) d -> p t d", p=P), hs[:]).then_inc(hs_stored, 16)
            sp.wait_ge(hs_stored, 16)

        @block.gpsimd
        def _(pool):
            nc.gpsimd.memset(ones[:], 1.0).then_inc(ones_set, 1)
            pool.wait_ge(var_ready, 1)
            nc.gpsimd.tensor_tensor(rstd[:], rstd[:], c.minus_half[:, 0:NT], ALU.pow).then_inc(rstd_ready, 1)

        @block.vector
        def _(dve):
            chain = Chain(dve, dve_chain)
            link = chain.link
            norm_rows_into(nc, dve, chain, c, stats, mv, rstd, var_ready, rstd_ready, 1e-5)
            with dve.Fori(0, B) as b:
                dve.wait_ge(rows_turned, b)
                for j in range(JT):
                    t = bass.ds(b * JT + j, 1)
                    last = nc.vector.tensor_scalar(rows[:, j:j + 1, :], c.X[:, t, :], mv[:, t, 0:1], rstd[:, t],
                                                   ALU.subtract, ALU.mult)
                last.then_inc(rows_ready, 1)
                for j in range(JT):
                    t = bass.ds(b * JT + j, 1)
                    last = nc.vector.tensor_scalar(hs[:, t, :], c.X[:, t, :], mv[:, t, 0:1], rstd[:, t],
                                                   ALU.subtract, ALU.mult)
                last.then_inc(hs_ready, 1)
                dve.wait_ge(gated, b + 1)
                nc.vector.tensor_scalar(score[:, bass.ds(b * JT, JT), :], c.bank[4][:, 0:JT * E_].rearrange("p (j e) -> p j e", j=JT),
                                        -1.0, None, ALU.mult).then_inc(taken, 1)
            dve.wait_ge(exp_ready, 1)
            link(nc.vector.tensor_scalar(score[:], score[:], 1.0, None, ALU.add))
            link(nc.vector.reciprocal(score[:], score[:]))
            dve.wait_ge(loaded, 6 * 16)
            link(nc.vector.reduce_max(best[:], score[:].rearrange("p t (g e) -> p t g e", g=EG), AX.X))
            shape = (P, NT, EG, EG)
            this, other = best[:].unsqueeze(3).broadcast_to(shape), best[:].unsqueeze(2).broadcast_to(shape)
            nc.vector.tensor_tensor(pair[:], other, this, ALU.is_gt)
            link(nc.vector.tensor_tensor(pair2[:], other, this, ALU.is_equal))
            link(nc.vector.tensor_tensor(pair2[:], pair2[:], earlier[:].unsqueeze(1).broadcast_to(shape), ALU.mult))
            link(nc.vector.tensor_tensor(pair[:], pair[:], pair2[:], ALU.add))
            link(nc.vector.reduce_sum(best[:], pair[:], AX.X))
            link(nc.vector.tensor_scalar(best[:], best[:], 2.0, None, ALU.is_lt))
            by_group = best[:].unsqueeze(3).broadcast_to((P, NT, EG, EPG))
            grouped = lambda tile: tile[:].rearrange("p t (g e) -> p t g e", g=EG)
            link(nc.vector.tensor_tensor(grouped(score), grouped(score), by_group, ALU.mult))
            link(nc.vector.tensor_scalar(best[:], best[:], -1.0, None, ALU.add))
            link(nc.vector.tensor_tensor(grouped(score), grouped(score), by_group, ALU.add))
            for t in range(NT):
                last = nc.vector.max(top[:, t, :], score[:, t, :])
            link(last)
            for t in range(NT):
                last = nc.vector.max_index(index[:, t, :], top[:, t, :], score[:, t, :])
            link(last)
            link(nc.vector.tensor_copy(indexf[:], index[:]))
            link(nc.vector.reduce_sum(wsum[:], top[:, :, 0:TOPK], AX.X))
            link(nc.vector.reciprocal(wsum[:], wsum[:]))
            nc.vector.tensor_tensor(weights[:], top[:, :, 0:TOPK], wsum[:].unsqueeze(2).broadcast_to((P, NT, TOPK)), ALU.mult)
            wide = (P, NT, E_)
            for k in range(TOPK):
                last = nc.vector.tensor_tensor(hot[:, k], iota[:, 0:E_].unsqueeze(1).broadcast_to(wide),
                                               indexf[:, :, k:k + 1].broadcast_to(wide), ALU.is_equal)
            link(last)
            link(nc.vector.tensor_tensor(member[:], hot[:, 0], hot[:, 1], ALU.add))
            for k in range(2, TOPK):
                link(nc.vector.tensor_tensor(member[:], member[:], hot[:, k], ALU.add))
            link(nc.vector.memset(members_before[:, 0, :], 0.0))
            for t in range(1, NT):
                link(nc.vector.tensor_tensor(members_before[:, t, :], members_before[:, t - 1, :], member[:, t - 1, :], ALU.add))
            nc.vector.tensor_tensor(small[:], members_before[:, NT - 1, :], member[:, NT - 1, :], ALU.add).then_inc(members_ready, 1)
            dve.wait_ge(counted, 1)
            nc.vector.tensor_copy(place[:].rearrange("p t e -> p (t e)"), c.bank[5])
            link(nc.vector.tensor_copy(count[:], c.bank[6][:, 0:E_]))
            link(nc.vector.tensor_tensor(over[:], count[:].unsqueeze(2).broadcast_to((P, E_, NT)),
                                         steps[:].unsqueeze(1).broadcast_to((P, E_, NT)), ALU.is_gt))
            link(nc.vector.reduce_sum(tiles[:], over[:], AX.X))
            link(nc.vector.tensor_scalar(tiles[:], tiles[:], 1.0, None, ALU.max))
            link(nc.vector.tensor_tensor_scan(through[:], ones[:, 0:E_], tiles[:], 0.0, ALU.mult, ALU.add))
            link(nc.vector.tensor_tensor(first_slot[:], through[:], tiles[:], ALU.subtract))
            link(nc.vector.tensor_scalar(first_slot[:], first_slot[:], float(P), None, ALU.mult))
            link(nc.vector.tensor_scalar(small[:], through[:], part[:, 0:1], None, ALU.is_le, ALU.add, accum_out=expert_of[:]))
            nc.vector.tensor_scalar(expert_of[:], expert_of[:], float(E_ - 1), float(SHARED), ALU.min, ALU.add).then_inc(expert_ready, 1)
            link(nc.vector.tensor_tensor(place[:], place[:], first_slot[:].unsqueeze(1).broadcast_to(wide), ALU.add))
            for k in range(TOPK):
                link(nc.vector.tensor_tensor(work[:], hot[:, k], place[:], ALU.mult))
                link(nc.vector.reduce_sum(slotsf[:, :, k], work[:], AX.X))
            nc.vector.tensor_copy(slots[:], slotsf[:])
            nc.vector.tensor_scalar(y_slots[:], slotsf[:], float(SHARED_TILES * P), None, ALU.add)
            nc.vector.tensor_scalar(tiles_through[:, SHARED:], through[0:1, :], float(SHARED_TILES), None, ALU.add)
            for s in range(SHARED):
                nc.vector.memset(tiles_through[:, s:s + 1], (s + 1) * NT)
                nc.vector.memset(tile_expert[:, s * NT:(s + 1) * NT], s)
            dve.wait_ge(expert_turned, 1)
            nc.vector.tensor_copy(tile_expert[:, SHARED_TILES:], c.bank[7][0:1, 0:ROUTED_TILES])

        @block.scalar
        def _(act):
            with act.Fori(0, B) as b:
                act.wait_ge(rows_turned, b + 1)
                for k in range(CC):
                    last = nc.scalar.copy(rowsT[:, k, :], c.bank[k])
                last.then_inc(rowsT_ready, 1)
            act.wait_ge(taken, B)
            nc.scalar.activation(score[:], score[:], ACT.Exp).then_inc(exp_ready, 1)

        @block.tensor
        def _(pe):
            pe.wait_ge(loaded, 6 * 16)
            with pe.Fori(0, B) as b:
                pe.wait_ge(rows_ready, b + 1)
                for k in range(CC):
                    for j in range(JT):
                        last = nc.tensor.transpose(c.bank[k][:, j * P:(j + 1) * P], rows[:, j, k * P:(k + 1) * P], c.ident[:])
                last.then_inc(rows_turned, 1)
                pe.wait_ge(rowsT_ready, b + 1)
                pe.wait_ge(taken, b)
                for j in range(JT):
                    for k in range(CC):
                        last = nc.tensor.matmul(c.bank[4][:, j * E_:(j + 1) * E_], rowsT[:, k, j * P:(j + 1) * P], w_gate[:, k, :],
                                                start=(k == 0), stop=(k == CC - 1))
                last.then_inc(gated, 1)
            pe.wait_ge(ones_set, 1)
            pe.wait_ge(members_ready, 1)
            nc.tensor.matmul(c.bank[5], tri[:], member[:].rearrange("p t e -> p (t e)"), start=True, stop=False)
            nc.tensor.matmul(c.bank[5], ones[:], members_before[:].rearrange("p t e -> p (t e)"), start=False, stop=True)
            nc.tensor.matmul(c.bank[6][:, 0:E_], ones[:], small[:], start=True, stop=True).then_inc(counted, 1)
            pe.wait_ge(expert_ready, 1)
            nc.tensor.transpose(c.bank[7][0:1, 0:P], expert_of[:], c.ident[:]).then_inc(expert_turned, 1)


def expert_tiles(nc, c, hs, slots, tile_expert, tiles_through):
    ME = 3
    cuts = [0, P, 2 * P, M]
    LAST_M = M - 2 * P
    with ExitStack() as stack:
        ones = sbuf(nc, stack, "e_ones", [P, 1])
        gu_in = sbuf(nc, stack, "e_gu_in", [P, CC, 2 * M])
        d_in = sbuf(nc, stack, "e_d_in", [P, ME, D])
        gu_high, gu_low = [sbuf(nc, stack, f"e_gu_{part}", [P, 2, CC, 2 * M], F32R) for part in ("high", "low")]
        d_high, d_low = [sbuf(nc, stack, f"e_d_{part}", [P, 2, ME, D], F32R) for part in ("high", "low")]
        row = [sbuf(nc, stack, f"e_row{n}", [P, D]) for n in range(2)]
        rowT_high = [sbuf(nc, stack, f"e_rowT_high{n}", [P, CC, P], F32R) for n in range(2)]
        rowT_low = [sbuf(nc, stack, f"e_rowT_low{n}", [P, CC, P], F32R) for n in range(2)]
        silu = [sbuf(nc, stack, f"e_silu{n}", [P, M]) for n in range(2)]
        mid = [sbuf(nc, stack, f"e_mid{n}", [P, M]) for n in range(2)]
        midT_high = sbuf(nc, stack, "e_midT_high", [P, ME, P], F32R)
        midT_low = sbuf(nc, stack, "e_midT_low", [P, ME, P], F32R)
        y = [sbuf(nc, stack, f"e_y{n}", [P, D]) for n in range(2)]
        row_even, row_odd, y_even, y_odd, scattered = sems(nc, c, "e_", "row_even row_odd y_even y_odd scattered")
        row_loaded, y_stored = [row_even, row_odd], [y_even, y_odd]
        gate_loaded, up_loaded, down_loaded, arrivals_seen, ones_set, high_ready, gate_split, up_split, down_split = sems(
            nc, c, "e_", "gate_loaded up_loaded down_loaded arrivals_seen ones_set high_ready gate_split up_split down_split")
        row_turned, rowT_high_ready, rowT_low_ready, gate_done, up_done, silu_ready, mid_ready, mid_turned = sems(
            nc, c, "e_", "row_turned rowT_high_ready rowT_low_ready gate_done up_done silu_ready mid_ready mid_turned")
        midT_high_ready, midT_low_ready, down_done, y_copied = sems(
            nc, c, "e_", "midT_high_ready midT_low_ready down_done y_copied")
        block = stack.enter_context(nc.Block())
        G, U, XT, HT, Y = [c.bank[0], c.bank[1]], [c.bank[2], c.bank[3]], c.bank[4], c.bank[5], [c.bank[6], c.bank[7]]

        @block.sync
        def _(sp):
            def load(n, gate, up, down, again=True):
                if again:
                    sp.wait_ge(gate_split, n)
                sp.dma_start(gu_in[:, :, 0:M], gate.rearrange("(k p) n -> p k n", p=P)).then_inc(gate_loaded, 16)
                if again:
                    sp.wait_ge(up_split, n)
                sp.dma_start(gu_in[:, :, M:2 * M], up.rearrange("(k p) n -> p k n", p=P)).then_inc(up_loaded, 16)
                if again:
                    sp.wait_ge(down_split, n)
                sp.dma_start(d_in[:, 0:2, :], down[0:2 * P, :].rearrange("(k p) n -> p k n", p=P)).then_inc(down_loaded, 16)
                sp.dma_start(d_in[0:LAST_M, 2, :], down[2 * P:M, :]).then_inc(down_loaded, 16)

            for s in range(SHARED):
                part = slice(s * M, (s + 1) * M)
                load(s, c.dram["L1_ffn_sw_gate"][:, part], c.dram["L1_ffn_sw_up"][:, part],
                     c.dram["L1_ffn_sw_down"][part, :], again=(s > 0))
            with sp.Fori(0, E_) as e:
                load(e + SHARED, *(c.dram[w][bass.ds(e, 1)].rearrange("a k n -> (a k) n")
                                   for w in ("L1_ffn_w_gate", "L1_ffn_w_up", "L1_ffn_w_down")))

        @block.gpsimd
        def _(pool):
            def arrived(sem, n):
                pool.wait_ge(sem, n)
                pool.nop().then_inc(arrivals_seen, 1)

            def split(n, par, reused=True):
                if reused:
                    done = pool.value_load(tiles_through[0:1, bass.ds(n - 2, 1)], min_val=1, max_val=TILES)
                    pool.wait_ge(up_done, done)
                arrived(gate_loaded, 16 * (n + 1))
                nc.gpsimd.tensor_tensor(gu_high[:, par, :, 0:M], gu_in[:, :, 0:M], ones[:].unsqueeze(2).broadcast_to((P, CC, M)), ALU.mult).then_inc(high_ready, 1)
                arrived(up_loaded, 16 * (n + 1))
                nc.gpsimd.tensor_tensor(gu_high[:, par, :, M:2 * M], gu_in[:, :, M:2 * M], ones[:].unsqueeze(2).broadcast_to((P, CC, M)), ALU.mult).then_inc(high_ready, 1)
                pool.wait_ge(high_ready, 3 * n + 1)
                nc.gpsimd.tensor_tensor(gu_low[:, par, :, 0:M], gu_in[:, :, 0:M], gu_high[:, par, :, 0:M].bitcast(F32),
                                        ALU.subtract).then_inc(gate_split, 1)
                pool.wait_ge(high_ready, 3 * n + 2)
                nc.gpsimd.tensor_tensor(gu_low[:, par, :, M:2 * M], gu_in[:, :, M:2 * M],
                                        gu_high[:, par, :, M:2 * M].bitcast(F32), ALU.subtract).then_inc(up_split, 1)
                if reused:
                    pool.wait_ge(down_done, done)
                arrived(down_loaded, 32 * (n + 1))
                nc.gpsimd.tensor_tensor(d_high[:, par, 0:2, :], d_in[:, 0:2, :], ones[:].unsqueeze(2).broadcast_to((P, 2, D)), ALU.mult)
                nc.gpsimd.tensor_tensor(d_high[0:LAST_M, par, 2, :], d_in[0:LAST_M, 2, :], ones[0:LAST_M].broadcast_to((LAST_M, D)), ALU.mult).then_inc(high_ready, 1)
                pool.wait_ge(high_ready, 3 * n + 3)
                nc.gpsimd.tensor_tensor(d_low[:, par, 0:2, :], d_in[:, 0:2, :], d_high[:, par, 0:2, :].bitcast(F32), ALU.subtract)
                nc.gpsimd.tensor_tensor(d_low[0:LAST_M, par, 2, :], d_in[0:LAST_M, 2, :],
                                        d_high[0:LAST_M, par, 2, :].bitcast(F32), ALU.subtract).then_inc(down_split, 1)

            nc.gpsimd.memset(ones[:], 1.0).then_inc(ones_set, 1)
            pool.wait_ge(ones_set, 1)
            for s in range(SHARED):
                split(s, s, reused=False)
            for t in range(NT):
                for k in range(TOPK):
                    nc.gpsimd.indirect_dma_start(c.dram["d_sorted"], bass.IndirectOffsetOnAxis(ap=slots[:, t, k:k + 1], axis=0),
                                                 hs[:, t, :], None).then_inc(scattered, 16)
            with pool.Fori(1, E_ // 2 + 1) as n:
                for par in range(2):
                    split(n * 2 + par, par)

        hs_tiles = c.dram["d_hs"].rearrange("(t p) d -> p t d", p=P)
        sorted_tiles = c.dram["d_sorted"].rearrange("(t p) d -> p t d", p=P)
        y_tiles = c.dram["d_y"].rearrange("(t p) d -> p t d", p=P)

        @block.scalar
        def _(act):
            def load(source, t, par):
                act.dma_start(row[par][:].unsqueeze(1), source[:, bass.ds(t, 1), :]).then_inc(row_loaded[par], 16)

            def silus(i, par):
                act.wait_ge(gate_done, i + 1)
                nc.scalar.activation(silu[par][:], G[par][:, 0:M], ACT.Silu).then_inc(silu_ready, 1)

            def copy_rowT(i, par):
                act.wait_ge(row_turned, i + 1)
                nc.scalar.copy(rowT_high[par][:], XT.rearrange("p (k n) -> p k n", k=CC)).then_inc(rowT_high_ready, 1)

            def copy_midT(i):
                act.wait_ge(mid_turned, i + 1)
                nc.scalar.copy(midT_high[:, 0:2, :], HT[:, 0:2 * P].rearrange("p (k n) -> p k n", k=2))
                nc.scalar.copy(midT_high[0:LAST_M, 2, :], HT[0:LAST_M, 2 * P:3 * P]).then_inc(midT_high_ready, 1)

            def store(i, par):
                act.wait_ge(y_copied, i + 1)
                act.dma_start(y_tiles[:, bass.ds(i, 1), :], y[par][:].unsqueeze(1)).then_inc(y_stored[par], 16)

            def steps(i, par, more=True, source=None, t=None, stores=True, old=True):
                silus(i, par)
                if old:
                    copy_midT(i - 1)
                if more:
                    copy_rowT(i + 1, 1 - par)
                if source is not None:
                    load(source, t, 1 - par)
                if stores:
                    store(i - 2, par)

            load(hs_tiles, 0, 0)
            load(hs_tiles, 1, 1)
            copy_rowT(0, 0)
            load(hs_tiles, 2, 0)
            for i in range(2):
                steps(i, i, source=hs_tiles, t=i + 3, stores=False, old=(i > 0))
            with act.Fori(1, NT // 2 - 2) as n:
                for par in range(2):
                    steps(n * 2 + par, par, source=hs_tiles, t=n * 2 + par + 3)
            for i in range(NT - 4, NT):
                steps(i, i % 2, source=hs_tiles, t=(i + 3) % NT)
            with act.Fori(NT // 2, NT - 2) as n:
                for par in range(2):
                    steps(n * 2 + par, par, source=hs_tiles, t=n * 2 + par + 3 - NT)
            for i in range(SHARED_TILES - 4, SHARED_TILES):
                if i + 3 < SHARED_TILES:
                    steps(i, i % 2, source=hs_tiles, t=i + 3 - NT)
                else:
                    if i + 3 == SHARED_TILES:
                        act.wait_ge(scattered, NT * TOPK * 16)
                    steps(i, i % 2, source=sorted_tiles, t=i + 3 - SHARED_TILES)
            with act.Fori(SHARED_TILES // 2, TILES // 2 - 2) as n:
                for par in range(2):
                    steps(n * 2 + par, par, source=sorted_tiles, t=n * 2 + par + 3 - SHARED_TILES)
            for i in range(TILES - 4, TILES):
                if i + 3 < TILES:
                    steps(i, i % 2, source=sorted_tiles, t=i + 3 - SHARED_TILES)
                else:
                    steps(i, i % 2, more=(i + 1 < TILES))
            copy_midT(TILES - 1)
            for i in range(TILES - 2, TILES):
                store(i, i % 2)
            for par in range(2):
                act.wait_ge(y_stored[par], 16 * (TILES // 2))

        @block.vector
        def _(dve):
            def low_rowT(i, par):
                dve.wait_ge(rowT_high_ready, i + 1)
                nc.vector.tensor_tensor(rowT_low[par][:], XT.rearrange("p (k n) -> p k n", k=CC),
                                        rowT_high[par][:].bitcast(F32), ALU.subtract).then_inc(rowT_low_ready, 1)

            def low_midT(i):
                dve.wait_ge(midT_high_ready, i + 1)
                nc.vector.tensor_tensor(midT_low[:, 0:2, :], HT[:, 0:2 * P].rearrange("p (k n) -> p k n", k=2),
                                        midT_high[:, 0:2, :].bitcast(F32), ALU.subtract)
                nc.vector.tensor_tensor(midT_low[0:LAST_M, 2, :], HT[0:LAST_M, 2 * P:3 * P],
                                        midT_high[0:LAST_M, 2, :].bitcast(F32), ALU.subtract).then_inc(midT_low_ready, 1)

            def multiply(i, par):
                dve.wait_ge(silu_ready, i + 1)
                dve.wait_ge(up_done, i + 1)
                nc.vector.tensor_tensor(mid[par][:], silu[par][:], U[par][:, 0:M], ALU.mult).then_inc(mid_ready, 1)

            def copy_y(i, par, stored=None):
                dve.wait_ge(down_done, i + 1)
                if stored is not None:
                    dve.wait_ge(y_stored[par], stored)
                nc.vector.tensor_copy(y[par][:], Y[par]).then_inc(y_copied, 1)

            low_rowT(0, 0)
            low_rowT(1, 1)
            multiply(0, 0)
            for i in (1, 2):
                low_midT(i - 1)
                low_rowT(i + 1, (i + 1) % 2)
                multiply(i, i % 2)
                copy_y(i - 1, (i - 1) % 2)
            low_midT(2)
            low_rowT(4, 0)
            multiply(3, 1)
            copy_y(2, 0, 16)
            with dve.Fori(2, TILES // 2 - 1) as n:
                for par in range(2):
                    low_midT(n * 2 + par - 1)
                    low_rowT(n * 2 + par + 1, 1 - par)
                    multiply(n * 2 + par, par)
                    copy_y(n * 2 + par - 1, 1 - par, 16 * (n - 1 + par))
            for i in (TILES - 2, TILES - 1):
                low_midT(i - 1)
                if i + 1 < TILES:
                    low_rowT(i + 1, 1)
                multiply(i, i % 2)
                copy_y(i - 1, (i - 1) % 2, 16 * ((i - 1) // 2))
            low_midT(TILES - 1)
            copy_y(TILES - 1, 1, 16 * (TILES // 2 - 1))

        @block.tensor
        def _(pe):
            def turn_row(i, par, loads):
                pe.wait_ge(row_loaded[par], loads)
                for k in range(CC):
                    last = nc.tensor.transpose(XT[:, k * P:(k + 1) * P], row[par][:, k * P:(k + 1) * P], c.ident[:])
                last.then_inc(row_turned, 1)

            def turn_mid(i, par):
                pe.wait_ge(mid_ready, i + 1)
                for k in range(ME):
                    n = cuts[k + 1] - cuts[k]
                    last = nc.tensor.transpose(HT[0:n, k * P:(k + 1) * P], mid[par][:, cuts[k]:cuts[k + 1]], c.ident[:])
                last.then_inc(mid_turned, 1)

            def product(bank, par, buffer, at, low_parts=None):
                for k in range(CC):
                    for part, w in enumerate((gu_high, gu_low)):
                        nc.tensor.matmul(bank[:, 0:M].unsqueeze(1), rowT_high[par][:, k, :],
                                         w[:, bass.ds(buffer, 1), k, at:at + M], start=(k == 0 and part == 0), stop=False)
                if low_parts is not None:
                    pe.wait_ge(rowT_low_ready, low_parts)
                for k in range(CC):
                    last = nc.tensor.matmul(bank[:, 0:M].unsqueeze(1), rowT_low[par][:, k, :],
                                            gu_high[:, bass.ds(buffer, 1), k, at:at + M],
                                            start=False, stop=(k == CC - 1))
                return last

            def down(i, par, e, before=None):
                buffer = e % 2
                pe.wait_ge(midT_high_ready, i + 1)
                pe.wait_ge(down_split, e + 1)
                if before is not None:
                    pe.wait_ge(y_copied, before)
                for k in range(ME):
                    n = cuts[k + 1] - cuts[k]
                    for part, w in enumerate((d_high, d_low)):
                        nc.tensor.matmul(Y[par].unsqueeze(1), midT_high[0:n, k, :], w[0:n, bass.ds(buffer, 1), k, :],
                                         start=(k == 0 and part == 0), stop=False)
                pe.wait_ge(midT_low_ready, i + 1)
                for k in range(ME):
                    n = cuts[k + 1] - cuts[k]
                    last = nc.tensor.matmul(Y[par].unsqueeze(1), midT_low[0:n, k, :], d_high[0:n, bass.ds(buffer, 1), k, :],
                                            start=False, stop=(k == ME - 1))
                last.then_inc(down_done, 1)

            def expert(i):
                return pe.value_load(tile_expert[0:1, bass.ds(i, 1)], min_val=0, max_val=E_ + SHARED - 1)

            def tile(i, par, old, more=True, loads=None, used=None, before=None):
                e = expert(i)
                pe.wait_ge(rowT_high_ready, i + 1)
                pe.wait_ge(gate_split, e + 1)
                if used is not None:
                    pe.wait_ge(mid_ready, used)
                buffer = e % 2
                product(G[par], par, buffer, 0, i + 1).then_inc(gate_done, 1)
                if old is not None:
                    turn_mid(i - 1, 1 - par)
                if more:
                    turn_row(i + 1, 1 - par, loads)
                pe.wait_ge(up_split, e + 1)
                product(U[par], par, buffer, M).then_inc(up_done, 1)
                if old is not None:
                    down(i - 1, 1 - par, old, before)

            turn_row(0, 0, 16)
            tile(0, 0, None, loads=16)
            tile(1, 1, 0, loads=32)
            tile(2, 0, 0, loads=32, used=1)
            tile(3, 1, 0, loads=48, used=2, before=1)
            with pe.Fori(2, TILES // 2 - 1) as n:
                tile(n * 2, 0, expert(n * 2 - 1), loads=16 * (n + 1), used=n * 2 - 1, before=n * 2 - 2)
                tile(n * 2 + 1, 1, expert(n * 2), loads=16 * (n + 2), used=n * 2, before=n * 2 - 1)
            i = TILES - 2
            tile(i, 0, expert(i - 1), loads=16 * (TILES // 2), used=i - 1, before=i - 2)
            tile(i + 1, 1, expert(i), more=False, used=i, before=i - 1)
            turn_mid(i + 1, 1)
            down(i + 1, 1, expert(i + 1), i)


def combine(nc, c, y_slots, weights):
    SETS = 2
    with ExitStack() as stack:
        part = sbuf(nc, stack, "m_part", [P, SETS, TOPK + SHARED, D])
        shared_even, shared_odd, routed_even, routed_odd, added, stored, dve_chain = sems(
            nc, c, "m_", "shared_even shared_odd routed_even routed_odd added stored dve_chain")
        shared_in, routed_in = [shared_even, shared_odd], [routed_even, routed_odd]
        block = stack.enter_context(nc.Block())
        y_tiles = c.dram["d_y"].rearrange("(t p) d -> p t d", p=P)

        @block.sync
        def _(sp):
            for t in range(NT):
                if t >= SETS:
                    sp.wait_ge(added, t - SETS + 1)
                for s in range(SHARED):
                    sp.dma_start(part[:, t % SETS, TOPK + s, :], y_tiles[:, s * NT + t, :]).then_inc(shared_in[t % SETS], 16)
                if t >= 1:
                    sp.wait_ge(added, t)
                    sp.dma_start(c.out.rearrange("b (j p) d -> p (b j) d", p=P)[:, t - 1, :], c.X[:, t - 1, :]).then_inc(stored, 16)
            sp.wait_ge(added, NT)
            sp.dma_start(c.out.rearrange("b (j p) d -> p (b j) d", p=P)[:, NT - 1, :], c.X[:, NT - 1, :]).then_inc(stored, 16)
            sp.wait_ge(stored, 16 * NT)

        @block.gpsimd
        def _(pool):
            for t in range(NT):
                if t >= SETS:
                    pool.wait_ge(added, t - SETS + 1)
                for k in range(TOPK):
                    nc.gpsimd.indirect_dma_start(part[:, t % SETS, k, :], None, c.dram["d_y"],
                                                 bass.IndirectOffsetOnAxis(ap=y_slots[:, t, k:k + 1], axis=0)).then_inc(routed_in[t % SETS], 16)

        @block.vector
        def _(dve):
            chain = Chain(dve, dve_chain)
            for t in range(NT):
                dve.wait_ge(shared_in[t % SETS], SHARED * 16 * (t // SETS + 1))
                for s in range(SHARED):
                    chain.link(nc.vector.tensor_tensor(c.X[:, t, :], c.X[:, t, :], part[:, t % SETS, TOPK + s, :], ALU.add))
                dve.wait_ge(routed_in[t % SETS], TOPK * 16 * (t // SETS + 1))
                for k in range(TOPK):
                    last = nc.vector.scalar_tensor_tensor(c.X[:, t, :], part[:, t % SETS, k, :], weights[:, t, k:k + 1],
                                                          c.X[:, t, :], ALU.mult, ALU.add)
                    if k < TOPK - 1:
                        chain.link(last)
                last.then_inc(added, 1)


def routed_ffn(nc, c):
    with ExitStack() as stack:
        slots = sbuf(nc, stack, "f_slots", [P, NT, TOPK], U32)
        y_slots = sbuf(nc, stack, "f_y_slots", [P, NT, TOPK], U32)
        weights = sbuf(nc, stack, "f_weights", [P, NT, TOPK])
        tile_expert = sbuf(nc, stack, "f_tile_expert", [1, TILES], I32)
        tiles_through = sbuf(nc, stack, "f_tiles_through", [1, E_ + SHARED], I32)
        with ExitStack() as inner:
            hs = sbuf(nc, inner, "f_hs", [P, NT, D])
            route_tokens(nc, c, hs, slots, y_slots, weights, tile_expert, tiles_through)
            expert_tiles(nc, c, hs, slots, tile_expert, tiles_through)
        combine(nc, c, y_slots, weights)


def store_rows(nc, c):
    with ExitStack() as stack:
        stored, = sems(nc, c, "s_", "stored")
        block = stack.enter_context(nc.Block())

        @block.sync
        def _(sp):
            sp.dma_start(c.out.rearrange("b (j p) d -> p (b j) d", p=P), c.X[:]).then_inc(stored, 16)
            sp.wait_ge(stored, 16)


def build(nc, aps, out):
    c = Core()
    c.dram = aps
    c.out = out
    c.of_stage = []
    with ExitStack() as stack:
        c.X = sbuf(nc, stack, "X", [P, NT, D])
        c.ctxT = sbuf(nc, stack, "ctxT", [P, B, KC, S])
        c.ident = sbuf(nc, stack, "ident", [P, P])
        c.minus_half = sbuf(nc, stack, "minus_half", [P, 64])
        c.psum = stack.enter_context(nc.psum_tensor("psum", [P, 8, 512], F32))
        c.bank = [c.psum[:, n, :] for n in range(8)]
        half_set, = sems(nc, c, "g_", "half_set")
        with nc.Block() as block:
            @block.gpsimd
            def _(pool):
                nc.gpsimd.memset(c.minus_half[:], -0.5).then_inc(half_set, 1)
                pool.wait_ge(half_set, 1)
        load_constants(nc, c)
        end_stage(nc, c)
        if LAST_STAGE >= 1:
            map_attention(nc, c)
            end_stage(nc, c)
        if LAST_STAGE >= 2:
            token_choice_ffn(nc, c)
            end_stage(nc, c)
        if LAST_STAGE >= 3:
            project_heads(nc, c)
            end_stage(nc, c)
            context_attention(nc, c)
            end_stage(nc, c)
        if LAST_STAGE >= 4:
            routed_ffn(nc, c)
        else:
            store_rows(nc, c)


def shape_tables():
    s, p = np.arange(S), np.arange(P)
    inv_freq = (np.float32(1.0) / np.float32(10000.0) ** (np.arange(0, 128, 2, dtype=np.float32) / np.float32(128))).astype(np.float32)
    ang = (s.astype(np.float32)[:, None] * inv_freq).astype(np.float32)
    slots = np.arange(2 * P)
    causal = np.stack([slots[None, :] <= (g * P + p)[:, None] for g in range(2)], 1)
    f = np.float32
    return {
        "i_ident": np.eye(P, dtype=f),
        "i_tri": (p[:, None] < p[None, :]).astype(f),
        "i_before": np.stack([s[None, :] < (j * P + p)[:, None] for j in range(JT)], 1).astype(f),
        "i_iota": np.broadcast_to(p.astype(f), (P, P)).copy(),
        "i_slot_base": np.broadcast_to(((np.arange(NT) // JT % 2) * (S // 8) + 1).astype(f), (P, NT)).copy(),
        "i_rope": np.concatenate([np.cos(ang), np.sin(ang)], 1).astype(f),
        "i_part": p.astype(f)[:, None].copy(),
        "i_earlier": np.broadcast_to(np.tri(EG, EG, -1, dtype=f), (P, EG, EG)).copy(),
        "i_steps": np.broadcast_to((np.arange(NT) * P).astype(f), (P, NT)).copy(),
        "i_causal": np.where(causal, f(0), f(-1e30)).reshape(P, 4 * P).astype(f),
    }


def kernel(**inputs):
    import concourse.bacc as _bacc
    from concourse.bass_utils import run_bass_kernel_spmd as _run

    nc = _bacc.Bacc("TRN2", target_bir_lowering=False, num_devices=1)
    arrays, aps = {}, {}
    for name, a in {**inputs, **shape_tables()}.items():
        a = np.ascontiguousarray(a)
        arrays[f"in_{name}"] = a
        aps[name] = nc.dram_tensor(f"in_{name}", a.shape, mybir.dt.from_np(a.dtype), kind="ExternalInput").ap()
    aps["d_scores"] = nc.dram_tensor("d_scores", (NT, P), F32).ap()
    for name in ("d_xq", "d_xk", "d_xv"):
        aps[name] = nc.dram_tensor(name, (B, S, D), F32).ap()
    aps["d_hs"] = nc.dram_tensor("d_hs", (TOK, D), F32).ap()
    aps["d_sorted"] = nc.dram_tensor("d_sorted", (ROUTED_TILES * P, D), F32).ap()
    aps["d_y"] = nc.dram_tensor("d_y", (TILES * P, D), F32).ap()
    out = nc.dram_tensor("out", (B, S, D), F32, kind="ExternalOutput").ap()
    build(nc, aps, out)
    r = _run(nc, [arrays], core_ids=[0])
    return r.results[0]["out"]
```

```python
from contextlib import ExitStack

import numpy as np

import concourse.bass as bass
from concourse import mybir

F32 = mybir.dt.float32
F32R = mybir.dt.float32r
I32 = mybir.dt.int32
U32 = mybir.dt.uint32
ALU = mybir.AluOpType
ACT = mybir.ActivationFunctionType
AX = mybir.AxisListType

P = 128
B, S, D = 4, 512, 512
TOK = B * S
NT = TOK // P
JT = S // P
CC = D // P
CTX = 256
KC = CTX // P


class Core:
    pass


def sbuf(nc, stack, name, shape, dt=F32):
    return stack.enter_context(nc.sbuf_tensor(name, shape, dt))


def sems(nc, c, prefix, names):
    made = [nc.alloc_semaphore(prefix + n) for n in names.split()]
    c.of_stage += made
    return made


def end_stage(nc, c):
    with nc.Block() as block:
        @block.gpsimd
        def _(pool):
            nc.clear_and_free_semaphores(c.of_stage)
    c.of_stage = []


class Chain:

    def __init__(self, eng, sem, base=0):
        self.eng, self.sem, self.n, self.base = eng, sem, 0, base

    def link(self, ins):
        self.n += 1
        ins.then_inc(self.sem, 1)
        self.eng.wait_ge(self.sem, self.base + self.n)

    def after_loop(self, times):
        self.n += times
        self.eng.wait_ge(self.sem, self.base + self.n)


def load_constants(nc, c):
    with ExitStack() as stack:
        ctx_rows = sbuf(nc, stack, "ctx_rows", [P, 2, JT, CTX])
        const_loaded, ctx_even, ctx_odd, turned, copied = sems(
            nc, c, "c_", "const_loaded ctx_even ctx_odd turned copied")
        ctx_loaded = [ctx_even, ctx_odd]
        block = stack.enter_context(nc.Block())

        @block.sync
        def _(sp):
            sp.dma_start(c.ident[:], c.dram["i_ident"]).then_inc(const_loaded, 16)
            for b in range(B):
                if b >= 2:
                    sp.wait_ge(turned, b - 1)
                sp.dma_start(ctx_rows[:, b % 2], c.dram["ctx_1024"][b].rearrange("(j p) d -> p j d", p=P)).then_inc(
                    ctx_loaded[b % 2], 16)

        @block.tensor
        def _(pe):
            pe.wait_ge(const_loaded, 16)
            for b in range(B):
                pe.wait_ge(ctx_loaded[b % 2], 16 * (b // 2 + 1))
                if b >= 2:
                    pe.wait_ge(copied, b - 1)
                for k in range(KC):
                    for j in range(JT):
                        last = nc.tensor.transpose(c.bank[2 * (b % 2) + k][:, j * P:(j + 1) * P],
                                                   ctx_rows[:, b % 2, j, k * P:(k + 1) * P], c.ident[:])
                last.then_inc(turned, 1)

        @block.scalar
        def _(act):
            for b in range(B):
                act.wait_ge(turned, b + 1)
                for k in range(KC):
                    last = nc.scalar.copy(c.ctxT[:, b, k, :], c.bank[2 * (b % 2) + k][:])
                last.then_inc(copied, 1)


def map_attention(nc, c):
    with ExitStack() as stack:
        wq = sbuf(nc, stack, "a_wq", [P, 2, CTX])
        wT = sbuf(nc, stack, "a_wT", [P, 2, KC, P])
        bias = sbuf(nc, stack, "a_bias", [P, 2])
        stats = sbuf(nc, stack, "a_stats", [P, JT, 6])
        mv = sbuf(nc, stack, "a_mv", [P, JT, 2])
        rstd = sbuf(nc, stack, "a_rstd", [P, JT])
        xln = sbuf(nc, stack, "a_xln", [P, JT, D])
        xlnT = sbuf(nc, stack, "a_xlnT", [P, CC, S])
        qkT = sbuf(nc, stack, "a_qkT", [P, 2, S])
        prob = sbuf(nc, stack, "a_prob", [P, JT, S])
        attT = sbuf(nc, stack, "a_attT", [P, 2, CC, S])
        nmax = sbuf(nc, stack, "a_nmax", [P, JT])
        rsum = sbuf(nc, stack, "a_rsum", [P, JT])
        rinv = sbuf(nc, stack, "a_rinv", [P, JT])
        w_loaded, w_turned, w_copied = sems(nc, c, "a_", "w_loaded w_turned w_copied")
        x_loaded = sems(nc, c, "a_", " ".join(f"x_loaded{b}" for b in range(B)))
        var_ready, rstd_ready, xln_ready, xln_turned, xlnT_ready = sems(
            nc, c, "a_", "var_ready rstd_ready xln_ready xln_turned xlnT_ready")
        qk_ready, qkT_ready, energy_ready, max_ready, exp_ready, prob_ready = sems(
            nc, c, "a_", "qk_ready qkT_ready energy_ready max_ready exp_ready prob_ready")
        prob_turned, attT_ready, mixed, added, dve_chain = sems(
            nc, c, "a_", "prob_turned attT_ready mixed added dve_chain")
        block = stack.enter_context(nc.Block())
        QK, ENERGY, ATT_T = [0, 1], [0, 1, 2, 3], [0, 1, 2, 3]
        XLN_T, MIX = [2, 3, 4, 5], [4, 5, 6, 7]

        @block.sync
        def _(sp):
            sp.dma_start(wq[:, 0], c.dram["L0_xattn_Wq"]).then_inc(w_loaded, 16)
            sp.dma_start(wq[:, 1], c.dram["L0_xattn_Wk"]).then_inc(w_loaded, 16)
            sp.dma_start(bias[:, 0:1], c.dram["L0_xattn_bq"].rearrange("(p a) -> p a", a=1)).then_inc(w_loaded, 16)
            sp.dma_start(bias[:, 1:2], c.dram["L0_xattn_bk"].rearrange("(p a) -> p a", a=1)).then_inc(w_loaded, 16)
            for b in range(B):
                sp.dma_start(c.X[:, b * JT:(b + 1) * JT, :], c.dram["x"][b].rearrange("(j p) d -> p j d", p=P)).then_inc(x_loaded[b], 16)

        @block.gpsimd
        def _(pool):
            for b in range(B):
                pool.wait_ge(var_ready, b + 1)
                nc.gpsimd.tensor_tensor(rstd[:], rstd[:], c.minus_half[:, 0:JT], ALU.pow).then_inc(rstd_ready, 1)

        @block.vector
        def _(dve):
            chain = Chain(dve, dve_chain)

            def softmax(b):
                for m in range(JT):
                    dve.wait_ge(energy_ready, b * JT + m + 1)
                    nc.vector.reduce_max(nmax[:, m:m + 1], c.bank[ENERGY[m]][:], AX.X, negate=True).then_inc(max_ready, 1)
                dve.wait_ge(exp_ready, (b + 1) * JT)
                chain.link(nc.vector.reciprocal(rinv[:], rsum[:]))
                for m in range(JT):
                    last = nc.vector.tensor_scalar(prob[:, m, :], prob[:, m, :], rinv[:, m:m + 1], None, ALU.mult)
                last.then_inc(prob_ready, 1)

            def norm(b):
                dve.wait_ge(x_loaded[b], 16)
                for j in range(JT):
                    last = nc.vector.bn_stats(stats[:, j, :], c.X[:, b * JT + j, :])
                chain.link(last)
                for j in range(JT):
                    last = nc.vector.bn_aggr(mv[:, j, :], stats[:, j, :])
                chain.link(last)
                nc.vector.tensor_scalar(rstd[:], mv[:, :, 1], 1e-5, None, ALU.add).then_inc(var_ready, 1)
                dve.wait_ge(rstd_ready, b + 1)
                if b >= 1:
                    dve.wait_ge(xln_turned, b)
                for j in range(JT):
                    last = nc.vector.tensor_scalar(xln[:, j, :], c.X[:, b * JT + j, :], mv[:, j, 0:1], rstd[:, j:j + 1],
                                                   ALU.subtract, ALU.mult)
                last.then_inc(xln_ready, 1)

            def add(b, j):
                dve.wait_ge(mixed, b * JT + j + 1)
                row = c.X[:, b * JT + j, :]
                nc.vector.tensor_tensor(row, row, c.bank[MIX[j]][:], ALU.add).then_inc(added, 1)
                if b > 0 or j > 0:
                    row_stats(nc, dve, c, b * JT + j - 1, added, b * JT + j)

            softmax(0)
            norm(0)
            for b in range(B):
                if b + 1 < B:
                    softmax(b + 1)
                add(b, 0)
                add(b, 1)
                if b + 1 < B:
                    norm(b + 1)
                add(b, 2)
                add(b, 3)
            row_stats(nc, dve, c, NT - 1, added, NT)

        @block.scalar
        def _(act):
            def copy_qk(b):
                act.wait_ge(qk_ready, b + 1)
                for s in range(2):
                    last = nc.scalar.activation(qkT[:, s, :], c.bank[QK[s]][:], ACT.Identity, bias=bias[:, s:s + 1])
                last.then_inc(qkT_ready, 1)

            def exponentials(b):
                for m in range(JT):
                    act.wait_ge(max_ready, b * JT + m + 1)
                    nc.scalar.activation(prob[:, m, :], c.bank[ENERGY[m]][:], ACT.Exp, bias=nmax[:, m:m + 1],
                                         accum_out=rsum[:, m:m + 1]).then_inc(exp_ready, 1)

            def copy_att(b):
                act.wait_ge(prob_turned, b + 1)
                for k in range(CC):
                    last = nc.scalar.copy(attT[:, b % 2, k, :], c.bank[ATT_T[k]][:])
                last.then_inc(attT_ready, 1)

            def copy_xln(b):
                act.wait_ge(xln_turned, b + 1)
                for k in range(CC):
                    last = nc.scalar.copy(xlnT[:, k, :], c.bank[XLN_T[k]][:])
                last.then_inc(xlnT_ready, 1)

            act.wait_ge(w_turned, 1)
            for s in range(2):
                last = nc.scalar.copy(wT[:, s], c.bank[s][:, 0:CTX].rearrange("p (k d) -> p k d", k=KC))
            last.then_inc(w_copied, 1)
            copy_qk(0)
            exponentials(0)
            copy_att(0)
            copy_qk(1)
            copy_xln(0)
            for b in range(B - 1):
                exponentials(b + 1)
                copy_att(b + 1)
                if b + 2 < B:
                    copy_qk(b + 2)
                copy_xln(b + 1)

        @block.tensor
        def _(pe):
            def project(b):
                if b >= 1:
                    pe.wait_ge(attT_ready, b)
                for s in range(2):
                    for k in range(KC):
                        last = nc.tensor.matmul(c.bank[QK[s]][:], wT[:, s, k, :], c.ctxT[:, b, k, :],
                                                start=(k == 0), stop=(k == KC - 1))
                last.then_inc(qk_ready, 1)

            def energies(b):
                pe.wait_ge(qkT_ready, b + 1)
                if b >= 1:
                    pe.wait_ge(xlnT_ready, b)
                for m in range(JT):
                    nc.tensor.matmul(c.bank[ENERGY[m]][:], qkT[:, 0, m * P:(m + 1) * P], qkT[:, 1, :],
                                     start=True, stop=True).then_inc(energy_ready, 1)

            def turn_prob(b):
                pe.wait_ge(prob_ready, b + 1)
                for k in range(CC):
                    for m in range(JT):
                        last = nc.tensor.transpose(c.bank[ATT_T[k]][:, m * P:(m + 1) * P], prob[:, m, k * P:(k + 1) * P],
                                                   c.ident[:])
                last.then_inc(prob_turned, 1)

            def turn_xln(b):
                pe.wait_ge(xln_ready, b + 1)
                pe.wait_ge(attT_ready, b + 1)
                if b >= 1:
                    pe.wait_ge(added, (b - 1) * JT + 2)
                for k in range(CC):
                    for j in range(JT):
                        last = nc.tensor.transpose(c.bank[XLN_T[k]][:, j * P:(j + 1) * P], xln[:, j, k * P:(k + 1) * P],
                                                   c.ident[:])
                last.then_inc(xln_turned, 1)

            def mix(b, tiles):
                pe.wait_ge(xlnT_ready, b + 1)
                for j in tiles:
                    if b >= 1:
                        pe.wait_ge(added, (b - 1) * JT + j + 1)
                    for k in range(CC):
                        last = nc.tensor.matmul(c.bank[MIX[j]][:], xlnT[:, k, j * P:(j + 1) * P], attT[:, b % 2, k, :],
                                                start=(k == 0), stop=(k == CC - 1))
                    last.then_inc(mixed, 1)

            pe.wait_ge(w_loaded, 64)
            for s in range(2):
                for k in range(KC):
                    last = nc.tensor.transpose(c.bank[s][:, k * P:(k + 1) * P], wq[:, s, k * P:(k + 1) * P], c.ident[:])
            last.then_inc(w_turned, 1)
            pe.wait_ge(w_copied, 1)
            project(0)
            energies(0)
            turn_prob(0)
            project(1)
            turn_xln(0)
            for b in range(B):
                if b + 1 < B:
                    energies(b + 1)
                mix(b, (0, 1))
                if b + 1 < B:
                    turn_prob(b + 1)
                mix(b, (2, 3))
                if b + 2 < B:
                    project(b + 2)
                if b + 1 < B:
                    turn_xln(b + 1)


def row_stats(nc, dve, c, t, added, count):
    dve.wait_ge(added, count)
    nc.vector.bn_stats(c.stats[:, t, :], c.X[:, t, :])


def norm_rows_into(nc, dve, chain, c, mv, rstd, var_ready, rstd_ready, eps):
    for t in range(NT):
        last = nc.vector.bn_aggr(mv[:, t, :], c.stats[:, t, :])
    chain.link(last)
    nc.vector.tensor_scalar(rstd[:], mv[:, :, 1], eps, None, ALU.add).then_inc(var_ready, 1)
    dve.wait_ge(rstd_ready, 1)


def token_choice_ffn(nc, c):
    CAP = S // 8
    GROUPS = B * CAP // P
    DH = 128
    HALF = DH // 2
    KVH = 8
    QH = 2
    HEAD_COLS = (QH + 2) * DH
    SLOTS = GROUPS * P
    INNER = 2048
    with ExitStack() as kept:
        slot_hot_T = sbuf(nc, kept, "b_slot_hot_T", [P, NT, P])
        picked = sbuf(nc, kept, "b_picked", [P, GROUPS, D])
        x1 = sbuf(nc, kept, "b_x1", [P, GROUPS, D])
        angle = sbuf(nc, kept, "b_angle", [P, GROUPS, 3, HALF])
        gate = sbuf(nc, kept, "b_gate", [P, GROUPS])
        hT = sbuf(nc, kept, "b_hT", [P, CC, SLOTS])
        ln_w = sbuf(nc, kept, "b_ln_w", [P, 2, CC])
        heads_held = kept.enter_context(ExitStack())
        w_heads = sbuf(nc, heads_held, "b_w_heads", [P, CC, KVH, HEAD_COLS])
        heads_loaded, = sems(nc, c, "b_", "heads_loaded")

        with ExitStack() as stack:
            hs = sbuf(nc, stack, "b_hs", [P, NT, D])
            mv = sbuf(nc, stack, "b_mv", [P, NT, 2])
            rstd = sbuf(nc, stack, "b_rstd", [P, NT])
            w_router = sbuf(nc, stack, "b_w_router", [P, D])
            score = sbuf(nc, stack, "b_score", [P, NT])
            score_T = sbuf(nc, stack, "b_score_T", [NT, P])
            scores_of_batch = sbuf(nc, stack, "b_scores_of_batch", [P, B, S])
            before = sbuf(nc, stack, "b_before", [P, JT, S])
            tri = sbuf(nc, stack, "b_tri", [P, P])
            ones = sbuf(nc, stack, "b_ones", [P, P])
            iota = sbuf(nc, stack, "b_iota", [P, P])
            slot_base = sbuf(nc, stack, "b_slot_base", [P, NT])
            rope = sbuf(nc, stack, "b_rope", [P, JT, DH])
            above = sbuf(nc, stack, "b_above", [P, NT])
            equal = sbuf(nc, stack, "b_equal", [P, NT])
            chosen = sbuf(nc, stack, "b_chosen", [P, NT])
            chosen_before = sbuf(nc, stack, "b_chosen_before", [P, NT])
            slot = sbuf(nc, stack, "b_slot", [P, NT])
            slot_hot = sbuf(nc, stack, "b_slot_hot", [P, NT, P])
            router_loaded, loaded, var_ready, rstd_ready, score_ready, score_turned, score_T_ready, score_stored, scores_spread = sems(
                nc, c, "b_", "router_loaded loaded var_ready rstd_ready score_ready score_turned score_T_ready score_stored scores_spread")
            chosen_ready, slot_counted, hot_ready, gathered, hot_turned, chain_dve, gate_ready, gate_exp = sems(
                nc, c, "b_", "chosen_ready slot_counted hot_ready gathered hot_turned chain_dve gate_ready gate_exp")
            block = stack.enter_context(nc.Block())

            @block.sync
            def _(sp):
                sp.dma_start(w_router[:], c.dram["L0_ffn_w_router"].partition_broadcast(P)).then_inc(router_loaded, 16)
                for dst, src in ((before[:], c.dram["i_before"]),
                                 (tri[:], c.dram["i_tri"]), (iota[:], c.dram["i_iota"]), (slot_base[:], c.dram["i_slot_base"]),
                                 (rope[:], c.dram["i_rope"].rearrange("(j p) d -> p j d", p=P)),
                                 (ln_w[:, 0], c.dram["L0_ffn_ln1_w"].rearrange("(k p) -> p k", p=P)),
                                 (ln_w[:, 1], c.dram["L0_ffn_ln2_w"].rearrange("(k p) -> p k", p=P))):
                    sp.dma_start(dst, src, allow_slow_non_contiguous=True).then_inc(loaded, 16)
                sp.wait_ge(score_T_ready, 1)
                sp.dma_start(c.dram["d_scores"], score_T[:]).then_inc(score_stored, 16)
                sp.wait_ge(score_stored, 16)
                sp.dma_start(scores_of_batch[:], c.dram["d_scores"].rearrange("(b j) p -> (b j p)", b=B).partition_broadcast(P)
                             .rearrange("q (b s) -> q b s", b=B)).then_inc(scores_spread, 16)

            @block.gpsimd
            def _(pool):
                nc.gpsimd.memset(ones[:], 1.0)
                pool.wait_ge(var_ready, 1)
                nc.gpsimd.tensor_tensor(rstd[:], rstd[:], c.minus_half[:, 0:NT], ALU.pow).then_inc(rstd_ready, 1)

            @block.vector
            def _(dve):
                chain = Chain(dve, chain_dve)
                norm_rows_into(nc, dve, chain, c, mv, rstd, var_ready, rstd_ready, 1e-5)
                dve.wait_ge(router_loaded, 16)
                first = chain.n
                with dve.Fori(0, B) as b:
                    tiles = [bass.ds(b * JT + j, 1) for j in range(JT)]
                    for t in tiles:
                        last = nc.vector.tensor_scalar(hs[:, t, :], c.X[:, t, :], mv[:, t, 0:1], rstd[:, t],
                                                       ALU.subtract, ALU.mult)
                    last.then_inc(chain_dve, 1)
                    dve.wait_ge(chain_dve, b + first + 1)
                    for j, t in enumerate(tiles):
                        last = nc.vector.scalar_tensor_tensor(c.bank[4 + j][:].unsqueeze(1), hs[:, t, :], 1.0,
                                                              w_router[:].unsqueeze(1), ALU.mult, ALU.mult,
                                                              accum_out=score[:, t])
                    last.then_inc(score_ready, 1)
                chain.n += B
                dve.wait_ge(score_turned, 1)
                nc.vector.tensor_copy(score_T[:], c.bank[0][0:NT, 0:P]).then_inc(score_T_ready, 1)
                with dve.Fori(0, B) as b:
                    for j in range(JT):
                        t = bass.ds(b * JT + j, 1)
                        nc.vector.tensor_tensor(c.X[:, t, :], c.X[:, t, :], hs[:, t, :], ALU.add)
                dve.wait_ge(loaded, 7 * 16)
                dve.wait_ge(score_T_ready, 1)
                dve.wait_ge(scores_spread, 16)
                first = chain.n
                with dve.Fori(0, B) as b:
                    dve.wait_ge(chain_dve, b + first)
                    of_batch = scores_of_batch[:, bass.ds(b, 1), :]
                    for j in range(JT):
                        t = bass.ds(b * JT + j, 1)
                        nc.vector.tensor_scalar(c.bank[j][:].unsqueeze(1), of_batch, score[:, t], None, ALU.is_gt,
                                                ALU.add, accum_out=above[:, t])
                        last = nc.vector.scalar_tensor_tensor(c.bank[4 + j][:].unsqueeze(1), of_batch, score[:, t],
                                                              before[:, j:j + 1, :], ALU.is_equal, ALU.mult,
                                                              accum_out=equal[:, t])
                    last.then_inc(chain_dve, 1)
                chain.after_loop(B)
                chain.link(nc.vector.tensor_tensor(above[:], above[:], equal[:], ALU.add))
                chain.link(nc.vector.tensor_scalar(chosen[:], above[:], float(CAP), None, ALU.is_lt))
                of = lambda tile, j: tile[:].rearrange("p (b j) -> p b j", j=JT)[:, :, j]
                chain.link(nc.vector.memset(chosen_before[:], 0.0))
                for j in range(1, JT):
                    last = nc.vector.tensor_tensor(of(chosen_before, j), of(chosen_before, j - 1), of(chosen, j - 1), ALU.add)
                    if j < JT - 1:
                        chain.link(last)
                last.then_inc(chosen_ready, 1)
                dve.wait_ge(slot_counted, 1)
                chain.link(nc.vector.tensor_tensor(slot[:], c.bank[1][:, 0:NT], slot_base[:], ALU.add))
                chain.link(nc.vector.tensor_tensor(slot[:], slot[:], chosen[:], ALU.mult))
                chain.link(nc.vector.tensor_scalar(slot[:], slot[:], -1.0, None, ALU.add))
                nc.vector.tensor_tensor(slot_hot[:], iota[:].unsqueeze(1).broadcast_to((P, NT, P)),
                                        slot[:].unsqueeze(2).broadcast_to((P, NT, P)), ALU.is_equal).then_inc(hot_ready, 1)
                dve.wait_ge(gathered, 1)
                for g in range(GROUPS):
                    last = nc.vector.tensor_copy(gate[:, g:g + 1], c.bank[2 + g][:, DH:DH + 1])
                last.then_inc(gate_ready, 1)
                for g in range(GROUPS):
                    nc.vector.tensor_copy(picked[:, g, :], c.bank[g][:])
                    nc.vector.tensor_copy(x1[:, g, :], c.bank[g][:])
                    nc.vector.tensor_copy(angle[:, g, 0:2, :], c.bank[2 + g][:, 0:DH].rearrange("p (a d) -> p a d", a=2))
                    nc.vector.tensor_scalar(angle[:, g, 2, :], c.bank[2 + g][:, HALF:DH], -1.0, None, ALU.mult)
                dve.wait_ge(gate_exp, 1)
                chain.link(nc.vector.tensor_scalar(gate[:], gate[:], 1.0, None, ALU.add))
                nc.vector.reciprocal(gate[:], gate[:])

            @block.scalar
            def _(act):
                for k in range(CC):
                    if k == CC // 2:
                        act.wait_ge(scores_spread, 16)
                    rows = slice(k * P, (k + 1) * P)
                    for src, at, cols in ((c.dram["L0_ffn_wq"], 0, QH * DH), (c.dram["L0_ffn_wk"], QH * DH, DH),
                                          (c.dram["L0_ffn_wv"], (QH + 1) * DH, DH)):
                        act.dma_start(w_heads[:, k, :, at:at + cols],
                                     src[rows, :].rearrange("p (h n) -> p h n", n=cols)).then_inc(heads_loaded, 16)
                act.wait_ge(gate_ready, 1)
                nc.scalar.activation(gate[:], gate[:], ACT.Exp, scale=-1.0).then_inc(gate_exp, 1)
                act.wait_ge(hot_turned, 1)
                for q in range(4):
                    nc.scalar.copy(slot_hot_T[:, 4 * q:4 * q + 4, :], c.bank[4 + q][:].rearrange("p (t s) -> p t s", t=4))

            @block.tensor
            def _(pe):
                pe.wait_ge(score_ready, B)
                nc.tensor.transpose(c.bank[0][0:NT, 0:P], score[:], c.ident[:]).then_inc(score_turned, 1)
                pe.wait_ge(chosen_ready, 1)
                nc.tensor.matmul(c.bank[1][:, 0:NT], tri[:], chosen[:], start=True, stop=False)
                nc.tensor.matmul(c.bank[1][:, 0:NT], ones[:], chosen_before[:], start=False, stop=True).then_inc(slot_counted, 1)
                pe.wait_ge(hot_ready, 1)
                per = NT // GROUPS
                for g in range(GROUPS):
                    for n in range(per):
                        t = g * per + n
                        nc.tensor.matmul(c.bank[g][:], slot_hot[:, t, :], hs[:, t, :], start=(n == 0), stop=(n == per - 1))
                    for n in range(per):
                        t = g * per + n
                        nc.tensor.matmul(c.bank[2 + g][:, 0:DH], slot_hot[:, t, :], rope[:, t % JT, :],
                                         start=(n == 0), stop=(n == per - 1))
                    for n in range(per):
                        t = g * per + n
                        last = nc.tensor.matmul(c.bank[2 + g][:, DH:DH + 1], slot_hot[:, t, :], score[:, t:t + 1],
                                                start=(n == 0), stop=(n == per - 1))
                last.then_inc(gathered, 1)
                for t in range(NT):
                    last = nc.tensor.transpose(c.bank[4 + t // 4][:, (t % 4) * P:(t % 4 + 1) * P], slot_hot[:, t, :], c.ident[:])
                last.then_inc(hot_turned, 1)

        def rms_turned(stack, pre, row, sq, which):
            ms = sbuf(nc, stack, pre + "ms", [P, GROUPS])
            squared, ms_ready, r_ready, row_ready, turned, hT_ready, chained = sems(
                nc, c, pre, "squared ms_ready r_ready row_ready turned hT_ready chained")

            def on_act(act):
                for g in range(GROUPS):
                    nc.scalar.activation(sq[:, g, :], row[:, g, :], ACT.Square, accum_out=ms[:, g:g + 1]).then_inc(squared, 1)
                act.wait_ge(turned, 1)
                for k in range(CC):
                    last = nc.scalar.mul(hT[:, k, :], c.bank[k // 2][:, (k % 2) * SLOTS:(k % 2 + 1) * SLOTS], ln_w[:, which, k:k + 1])
                last.then_inc(hT_ready, 1)

            def on_dve(dve):
                dve.wait_ge(squared, GROUPS)
                nc.vector.tensor_scalar(ms[:], ms[:], 1.0 / D, 1e-6, ALU.mult, ALU.add).then_inc(ms_ready, 1)
                dve.wait_ge(r_ready, 1)
                for g in range(GROUPS):
                    last = nc.vector.tensor_scalar(sq[:, g, :], row[:, g, :], ms[:, g:g + 1], None, ALU.mult)
                last.then_inc(row_ready, 1)

            def on_pool(pool):
                pool.wait_ge(ms_ready, 1)
                nc.gpsimd.tensor_tensor(ms[:], ms[:], c.minus_half[:, 0:GROUPS], ALU.pow).then_inc(r_ready, 1)

            def on_pe(pe):
                pe.wait_ge(row_ready, 1)
                for k in range(CC):
                    for g in range(GROUPS):
                        last = nc.tensor.transpose(c.bank[k // 2][:, (k % 2) * SLOTS + g * P:(k % 2) * SLOTS + (g + 1) * P],
                                                   sq[:, g, k * P:(k + 1) * P], c.ident[:])
                last.then_inc(turned, 1)
                pe.wait_ge(hT_ready, 1)

            return on_act, on_dve, on_pool, on_pe

        with ExitStack() as stack:
            w_o = sbuf(nc, stack, "b_w_o", [P, 2, QH, D])
            bias = sbuf(nc, stack, "b_bias", [P, KVH, HEAD_COLS])
            causal = sbuf(nc, stack, "b_causal", [P, GROUPS * SLOTS])
            qkv = sbuf(nc, stack, "b_qkv", [P, 2, GROUPS, HEAD_COLS])
            turn = sbuf(nc, stack, "b_turn", [P, GROUPS, QH + 1, DH])
            qk = sbuf(nc, stack, "b_qk", [P, GROUPS, QH + 1, DH])
            qT = sbuf(nc, stack, "b_qT", [P, QH, SLOTS])
            kT = sbuf(nc, stack, "b_kT", [P, SLOTS])
            prob = sbuf(nc, stack, "b_prob", [P, QH, GROUPS * SLOTS])
            probT = sbuf(nc, stack, "b_probT", [P, GROUPS, QH * SLOTS])
            oT = sbuf(nc, stack, "b_oT", [P, QH * SLOTS])
            nmax = sbuf(nc, stack, "b_nmax", [P, QH * GROUPS])
            rsum = sbuf(nc, stack, "b_rsum", [P, QH * GROUPS])
            wo_even, wo_odd, bias_loaded, projected, biased_ready, qk_ready, qk_turned, qkT_ready = sems(
                nc, c, "b_", "wo_even wo_odd bias_loaded projected biased_ready qk_ready qk_turned qkT_ready")
            scored, max_ready, exp_ready, prob_ready, prob_turned, probT_ready, valued, oT_ready, out_ready, added = sems(
                nc, c, "b_", "scored max_ready exp_ready prob_ready prob_turned probT_ready valued oT_ready out_ready added")
            wo_loaded = [wo_even, wo_odd]
            turn_ready, masked, inverted = sems(nc, c, "b_", "turn_ready masked inverted")
            block = stack.enter_context(nc.Block())
            rms_act, rms_dve, rms_pool, rms_pe = rms_turned(stack, "b_r1_", picked, qkv[:, 0], 0)
            SCALE = DH ** -0.5

            @block.sync
            def _(sp):
                for src, at, cols in ((c.dram["L0_ffn_bq"], 0, QH * DH), (c.dram["L0_ffn_bk"], QH * DH, DH),
                                      (c.dram["L0_ffn_bv"], (QH + 1) * DH, DH)):
                    sp.dma_start(bias[:, :, at:at + cols],
                                 src.partition_broadcast(P).rearrange("p (h n) -> p h n", n=cols)).then_inc(bias_loaded, 16)
                sp.dma_start(causal[:], c.dram["i_causal"]).then_inc(bias_loaded, 16)
                for h in range(KVH):
                    if h >= 2:
                        sp.wait_ge(out_ready, h - 1)
                    sp.dma_start(w_o[:, h % 2], c.dram["L0_ffn_wo"][h * QH * DH:(h + 1) * QH * DH, :].rearrange(
                        "(q d) n -> d q n", d=DH)).then_inc(wo_loaded[h % 2], 16)

            @block.gpsimd
            def _(pool):
                rms_pool(pool)

            @block.vector
            def _(dve):
                rms_dve(dve)
                dve.wait_ge(bias_loaded, 4 * 16)

                def rotate(h, par):
                    dve.wait_ge(projected, h + 1)
                    for g in range(GROUPS):
                        last = nc.vector.tensor_tensor(qkv[:, par, g, :].unsqueeze(1), c.bank[g][:].unsqueeze(1),
                                                       bias[:, bass.ds(h, 1), :], ALU.add)
                    last.then_inc(biased_ready, 1)
                    dve.wait_ge(biased_ready, h + 1)
                    rows = qkv[:, par, :, 0:(QH + 1) * DH]
                    cos = angle[:, :, 0:1, :].broadcast_to((P, GROUPS, 2 * (QH + 1), HALF))
                    nc.vector.tensor_tensor(qk[:].rearrange("p g h (a d) -> p g (h a) d", a=2),
                                            rows.rearrange("p g (n d) -> p g n d", d=HALF), cos, ALU.mult)
                    for half, which in ((0, 2), (1, 1)):
                        other = rows.rearrange("p g (h a d) -> p g h a d", a=2, d=HALF)[:, :, :, 1 - half, :]
                        sin = angle[:, :, which:which + 1, :].broadcast_to((P, GROUPS, QH + 1, HALF))
                        last = nc.vector.tensor_tensor(turn[:, :, :, half * HALF:(half + 1) * HALF], other, sin, ALU.mult)
                    last.then_inc(turn_ready, 1)
                    dve.wait_ge(turn_ready, h + 1)
                    nc.vector.tensor_tensor(qk[:], qk[:], turn[:], ALU.add).then_inc(qk_ready, 1)

                def add_out(h):
                    dve.wait_ge(out_ready, h + 1)
                    for g in range(GROUPS):
                        last = nc.vector.tensor_tensor(x1[:, g, :], x1[:, g, :], c.bank[6 + g][:], ALU.add)
                    last.then_inc(added, 1)

                def a_head(h, par, first=False, last_head=False):
                    dve.wait_ge(scored, h + 1)
                    for q in range(QH):
                        last = nc.vector.scalar_tensor_tensor(prob[:, q, :], c.bank[4 + q][:], SCALE, causal[:], ALU.mult, ALU.add)
                    last.then_inc(masked, 1)
                    dve.wait_ge(masked, h + 1)
                    nc.vector.reduce_max(nmax[:], prob[:].rearrange("p q (g s) -> p (q g) s", g=GROUPS), AX.X,
                                         negate=True).then_inc(max_ready, 1)
                    dve.wait_ge(exp_ready, h + 1)
                    nc.vector.reciprocal(rsum[:], rsum[:]).then_inc(inverted, 1)
                    dve.wait_ge(inverted, h + 1)
                    flat = prob[:].rearrange("p q (g s) -> p (q g) s", g=GROUPS)
                    nc.vector.tensor_tensor(flat, flat, rsum[:].unsqueeze(2).broadcast_to((P, QH * GROUPS, SLOTS)),
                                            ALU.mult).then_inc(prob_ready, 1)
                    if not last_head:
                        rotate(h + 1, 1 - par)
                    if not first:
                        add_out(h - 1)

                rotate(0, 0)
                a_head(0, 0, first=True)
                a_head(1, 1)
                with dve.Fori(1, KVH // 2 - 1) as n:
                    for par in range(2):
                        a_head(n * 2 + par, par)
                a_head(KVH - 2, 0)
                a_head(KVH - 1, 1, last_head=True)
                add_out(KVH - 1)

            @block.scalar
            def _(act):
                rms_act(act)
                with act.Fori(0, KVH) as h:
                    act.wait_ge(qk_turned, h + 1)
                    nc.scalar.copy(qT[:].rearrange("p q s -> p (q s)"), c.bank[2][:])
                    nc.scalar.copy(kT[:], c.bank[3][:, 0:SLOTS]).then_inc(qkT_ready, 1)
                    act.wait_ge(max_ready, h + 1)
                    for n in range(QH * GROUPS):
                        q, g = divmod(n, GROUPS)
                        part = prob[:, q, g * SLOTS:(g + 1) * SLOTS]
                        last = nc.scalar.activation(part, part, ACT.Exp, bias=nmax[:, n:n + 1], accum_out=rsum[:, n:n + 1])
                    last.then_inc(exp_ready, 1)
                    act.wait_ge(prob_turned, h + 1)
                    for n in range(GROUPS):
                        last = nc.scalar.copy(probT[:, n, :], c.bank[4 + n][:])
                    last.then_inc(probT_ready, 1)
                    act.wait_ge(valued, h + 1)
                    nc.scalar.copy(oT[:], c.bank[2][:]).then_inc(oT_ready, 1)

            @block.tensor
            def _(pe):
                rms_pe(pe)
                pe.wait_ge(heads_loaded, 3 * CC * 16)

                def project(h, first=False):
                    if not first:
                        pe.wait_ge(biased_ready, h)
                    for g in range(GROUPS):
                        for k in range(CC):
                            last = nc.tensor.matmul(c.bank[g][:], hT[:, k, g * P:(g + 1) * P], w_heads[:, k, bass.ds(h, 1), :],
                                                    start=(k == 0), stop=(k == CC - 1))
                    last.then_inc(projected, 1)

                def out(h, par, loads, first=False):
                    pe.wait_ge(oT_ready, h + 1)
                    pe.wait_ge(wo_loaded[par], loads * 16)
                    if not first:
                        pe.wait_ge(added, h)
                    for g in range(GROUPS):
                        for q in range(QH):
                            last = nc.tensor.matmul(c.bank[6 + g][:], oT[:, q * SLOTS + g * P:q * SLOTS + (g + 1) * P],
                                                    w_o[:, par, q, :], start=(q == 0), stop=(q == QH - 1))
                    last.then_inc(out_ready, 1)

                def a_head(h, par, loads=1, first=False, second=False, last_head=False):
                    pe.wait_ge(qk_ready, h + 1)
                    if not first:
                        pe.wait_ge(oT_ready, h)
                    for g in range(GROUPS):
                        for q in range(QH):
                            nc.tensor.transpose(c.bank[2][:, q * SLOTS + g * P:q * SLOTS + (g + 1) * P], qk[:, g, q, :], c.ident[:])
                        last = nc.tensor.transpose(c.bank[3][:, g * P:(g + 1) * P], qk[:, g, QH, :], c.ident[:])
                    last.then_inc(qk_turned, 1)
                    pe.wait_ge(qkT_ready, h + 1)
                    for q in range(QH):
                        for g in range(GROUPS):
                            last = nc.tensor.matmul(c.bank[4 + q][:, g * SLOTS:(g + 1) * SLOTS], qT[:, q, g * P:(g + 1) * P],
                                                    kT[:], start=True, stop=True)
                    last.then_inc(scored, 1)
                    if not last_head:
                        project(h + 1)
                    if not first:
                        out(h - 1, 1 - par, loads, second)
                    pe.wait_ge(prob_ready, h + 1)
                    for q in range(QH):
                        for g in range(GROUPS):
                            for n in range(GROUPS):
                                last = nc.tensor.transpose(c.bank[4 + n][:, q * SLOTS + g * P:q * SLOTS + (g + 1) * P],
                                                           prob[:, q, g * SLOTS + n * P:g * SLOTS + (n + 1) * P], c.ident[:])
                    last.then_inc(prob_turned, 1)
                    pe.wait_ge(probT_ready, h + 1)
                    for n in range(GROUPS):
                        last = nc.tensor.matmul(c.bank[2][:], qkv[:, par, n, (QH + 1) * DH:(QH + 2) * DH], probT[:, n, :],
                                                start=(n == 0), stop=(n == GROUPS - 1))
                    last.then_inc(valued, 1)

                project(0, first=True)
                a_head(0, 0, first=True)
                a_head(1, 1, second=True)
                with pe.Fori(1, KVH // 2 - 1) as n:
                    a_head(n * 2, 0, n)
                    a_head(n * 2 + 1, 1, n + 1)
                a_head(KVH - 2, 0, KVH // 2 - 1)
                a_head(KVH - 1, 1, KVH // 2, last_head=True)
                out(KVH - 1, 1, KVH // 2)
        heads_held.close()

        with ExitStack() as stack:
            PARTS = INNER // 512
            w_gate = sbuf(nc, stack, "b_w_gate", [P, CC, INNER])
            w_up = sbuf(nc, stack, "b_w_up", [P, CC, INNER])
            w_down = sbuf(nc, stack, "b_w_down", [P, INNER // P, D])
            act_g = sbuf(nc, stack, "b_act_g", [P, GROUPS, 512])
            mid = sbuf(nc, stack, "b_mid", [P, GROUPS, 512])
            midT = sbuf(nc, stack, "b_midT", [P, GROUPS, 512])
            part_loaded = sems(nc, c, "b_", " ".join(f"part{n}_loaded" for n in range(PARTS)))
            gated, upped, silu_ready, mid_ready, mid_turned, midT_ready, out_ready = sems(
                nc, c, "b_", "gated upped silu_ready mid_ready mid_turned midT_ready mlp_ready")
            chain_dve, diff_ready, spread, landed = sems(nc, c, "b_", "chain3 diff_ready spread landed")
            block = stack.enter_context(nc.Block())
            rms_act, rms_dve, rms_pool, rms_pe = rms_turned(stack, "b_r2_", x1, mid, 1)

            @block.sync
            def _(sp):
                for n in range(PARTS):
                    cols = slice(n * 512, (n + 1) * 512)
                    for dst, src in ((w_gate, c.dram["L0_ffn_w_gate"]), (w_up, c.dram["L0_ffn_w_up"])):
                        sp.dma_start(dst[:, :, cols], src.rearrange("(k p) n -> p k n", p=P)[:, :, cols]).then_inc(part_loaded[n], 16)
                    sp.dma_start(w_down[:, n * 4:(n + 1) * 4, :], c.dram["L0_ffn_w_down"].rearrange("(k p) n -> p k n", p=P)[
                        :, n * 4:(n + 1) * 4, :]).then_inc(part_loaded[n], 16)

            @block.gpsimd
            def _(pool):
                rms_pool(pool)

            @block.vector
            def _(dve):
                rms_dve(dve)
                with dve.Fori(0, PARTS) as n:
                    dve.wait_ge(silu_ready, n + 1)
                    dve.wait_ge(upped, n + 1)
                    for g in range(GROUPS):
                        last = nc.vector.tensor_tensor(mid[:, g, :], act_g[:, g, :], c.bank[2 + g][:], ALU.mult)
                    last.then_inc(mid_ready, 1)
                chain = Chain(dve, chain_dve)
                dve.wait_ge(out_ready, 1)
                for g in range(GROUPS):
                    last = nc.vector.tensor_tensor(x1[:, g, :], x1[:, g, :], c.bank[6 + g][:], ALU.add)
                chain.link(last)
                chain.link(nc.vector.tensor_tensor(x1[:], x1[:], picked[:], ALU.subtract))
                for g in range(GROUPS):
                    last = nc.vector.tensor_scalar(x1[:, g, :], x1[:, g, :], gate[:, g:g + 1], None, ALU.mult)
                last.then_inc(diff_ready, 1)
                for t in range(NT):
                    dve.wait_ge(spread, t + 1)
                    nc.vector.tensor_tensor(c.X[:, t, :], c.X[:, t, :], c.bank[t % 8][:], ALU.add).then_inc(landed, 1)
                    if t > 0:
                        row_stats(nc, dve, c, t - 1, landed, t)
                row_stats(nc, dve, c, NT - 1, landed, NT)

            @block.scalar
            def _(act):
                rms_act(act)
                with act.Fori(0, PARTS) as n:
                    act.wait_ge(gated, n + 1)
                    for g in range(GROUPS):
                        last = nc.scalar.activation(act_g[:, g, :], c.bank[g][:], ACT.Silu)
                    last.then_inc(silu_ready, 1)
                    act.wait_ge(mid_turned, n + 1)
                    for g in range(GROUPS):
                        last = nc.scalar.copy(midT[:, g, :], c.bank[4 + g][:])
                    last.then_inc(midT_ready, 1)

            @block.tensor
            def _(pe):
                rms_pe(pe)

                def product(at, w, n):
                    for g in range(GROUPS):
                        for k in range(CC):
                            last = nc.tensor.matmul(c.bank[at + g][:], hT[:, k, g * P:(g + 1) * P],
                                                    w[:, k, n * 512:(n + 1) * 512], start=(k == 0), stop=(k == CC - 1))
                    return last

                def turn_mid(n):
                    pe.wait_ge(mid_ready, n + 1)
                    for g in range(GROUPS):
                        for k in range(4):
                            last = nc.tensor.transpose(c.bank[4 + g][:, k * P:(k + 1) * P], mid[:, g, k * P:(k + 1) * P], c.ident[:])
                    last.then_inc(mid_turned, 1)

                def down(n):
                    pe.wait_ge(midT_ready, n + 1)
                    for g in range(GROUPS):
                        for k in range(4):
                            last = nc.tensor.matmul(c.bank[6 + g][:], midT[:, g, k * P:(k + 1) * P], w_down[:, n * 4 + k, :],
                                                    start=(n == 0 and k == 0), stop=(n == PARTS - 1 and k == 3))
                    return last

                for n in range(PARTS):
                    pe.wait_ge(part_loaded[n], 3 * 16)
                    if n >= 1:
                        pe.wait_ge(silu_ready, n)
                    product(0, w_gate, n).then_inc(gated, 1)
                    if n >= 1:
                        turn_mid(n - 1)
                    product(2, w_up, n).then_inc(upped, 1)
                    if n >= 1:
                        down(n - 1)
                turn_mid(PARTS - 1)
                down(PARTS - 1).then_inc(out_ready, 1)
                pe.wait_ge(diff_ready, 1)
                for t in range(NT):
                    if t >= 8:
                        pe.wait_ge(landed, t - 7)
                    nc.tensor.matmul(c.bank[t % 8][:], slot_hot_T[:, t, :], x1[:, t // (NT // GROUPS), :],
                                     start=True, stop=True).then_inc(spread, 1)


X_H = 16
X_HD = D // X_H
X_LAST = 16


def project_heads(nc, c):
    H, HD, LAST = X_H, X_HD, X_LAST
    MAIN = S - LAST
    SCALE = HD ** -0.5
    with ExitStack() as stack:
        w_q = sbuf(nc, stack, "x_w_q", [P, CC, D])
        w_kv = sbuf(nc, stack, "x_w_kv", [P, KC, 2 * D])
        w_last = sbuf(nc, stack, "x_w_last", [P, KC, 2 * D])
        b_q = sbuf(nc, stack, "x_b_q", [P, D])
        b_o = sbuf(nc, stack, "x_b_o", [P, D])
        b_kv = sbuf(nc, stack, "x_b_kv", [P, 2 * D])
        b_kv_end = sbuf(nc, stack, "x_b_kv_end", [P, 2 * D])
        head_mean = sbuf(nc, stack, "x_head_mean", [P, H])
        affine = sbuf(nc, stack, "x_affine", [P, 3, 2, HD])
        mv = sbuf(nc, stack, "x_mv", [P, NT, 2])
        rstd = sbuf(nc, stack, "x_rstd", [P, NT])
        rows = sbuf(nc, stack, "x_rows", [P, JT, D])
        squares = sbuf(nc, stack, "x_squares", [P, JT, D])
        rowsT = sbuf(nc, stack, "x_rowsT", [P, CC, S])
        ctx_b = sbuf(nc, stack, "x_ctx_b", [P, KC, S])
        ctx_end = sbuf(nc, stack, "x_ctx_end", [P, KC, P])
        ctx_last = sbuf(nc, stack, "x_ctx_last", [P, KC, P])
        q = sbuf(nc, stack, "x_q", [P, 2, JT, D])
        k = sbuf(nc, stack, "x_k", [P, 2, JT, D])
        v = sbuf(nc, stack, "x_v", [P, 2, JT, D])
        hrstd = sbuf(nc, stack, "x_hrstd", [P, 2, JT * H])
        q_loaded, loaded, kv_loaded, affine_loaded, var_ready, rstd_ready, rows_ready, rows_turned, rowsT_ready, ctx_ready = sems(
            nc, c, "x_", "q_loaded loaded kv_loaded affine_loaded var_ready rstd_ready rows_ready rows_turned rowsT_ready ctx_ready")
        q_weights_ready, kv_weights_ready, q_done, kv_done, q_copied, k_copied, hvar_ready, hrstd_ready, squared, dve_chain = sems(
            nc, c, "x_", "q_weights_ready kv_weights_ready q_done kv_done q_copied k_copied hvar_ready hrstd_ready squared dve_chain")
        q_scaled, k_scaled, zeroed, stored_even, stored_odd = sems(
            nc, c, "x_", "q_scaled k_scaled zeroed stored_even stored_odd")
        stored = [stored_even, stored_odd]
        block = stack.enter_context(nc.Block())

        def by_head(ap, d=HD):
            return ap.rearrange("p (h d) -> p h d", d=d)

        def keys_of(ap):
            return ap.rearrange("p (h a d) -> p h a d", a=2, d=HD)[:, :, 0, :]

        @block.sync
        def _(sp):
            end = slice(P - LAST, P)
            as_kv = lambda tile: tile.rearrange("p (h a d) -> p h a d", a=2, d=HD)
            sp.dma_start(w_q[:], c.dram["L1_xattn_Wq"].rearrange("(k p) n -> p k n", p=P)).then_inc(q_loaded, 16)
            sp.dma_start(b_q[:], c.dram["L1_xattn_bq"].partition_broadcast(P)).then_inc(q_loaded, 16)
            for dst, src in (
                    (w_kv[:, :, 0:D], c.dram["L1_xattn_Wk"].rearrange("(k p) n -> p k n", p=P)),
                    (w_kv[:, :, D:2 * D], c.dram["L1_xattn_Wv"].rearrange("(k p) n -> p k n", p=P)),
                    (w_last[:], c.dram["L1_xattn_Wkv_dca"].rearrange("(k p) n -> p k n", p=P)),
                    (b_o[:], c.dram["L1_xattn_bo"].partition_broadcast(P))):
                sp.dma_start(dst, src).then_inc(loaded, 16)
            for tile, n in ((b_kv, P), (b_kv_end, P - LAST)):
                sp.dma_start(tile[0:n, 0:D], c.dram["L1_xattn_bk"].partition_broadcast(n)).then_inc(kv_loaded, 16)
                sp.dma_start(tile[0:n, D:2 * D], c.dram["L1_xattn_bv"].partition_broadcast(n)).then_inc(kv_loaded, 16)
            for a in range(2):
                sp.dma_start(as_kv(b_kv_end[end, :])[:, :, a, :],
                             c.dram["L1_xattn_bkv_dca"][a * D:(a + 1) * D].partition_broadcast(LAST)
                             .rearrange("p (h d) -> p h d", d=HD)).then_inc(kv_loaded, 16)
            for n, at, rows_, name in ((0, 0, slice(0, P), "qn_w"), (0, 1, slice(0, P), "qn_b"),
                                       (1, 0, slice(0, P), "kn_w"), (1, 1, slice(0, P), "kn_b"),
                                       (2, 0, slice(0, P - LAST), "kn_w"), (2, 1, slice(0, P - LAST), "kn_b"),
                                       (2, 0, end, "kn_dca_w"), (2, 1, end, "kn_dca_b")):
                sp.dma_start(affine[rows_, n, at, :], c.dram["L1_xattn_" + name].partition_broadcast(
                    rows_.stop - rows_.start)).then_inc(affine_loaded, 16)
            for b in range(B):
                for tile, name, ready in ((v, "d_xv", k_copied), (q, "d_xq", q_scaled), (k, "d_xk", k_scaled)):
                    sp.wait_ge(ready, (b + 1) * (JT if ready is k_copied else 1))
                    sp.dma_start(c.dram[name][b].rearrange("(j p) d -> p j d", p=P), tile[:, b % 2]).then_inc(stored[b % 2], 16)
            for par in range(2):
                sp.wait_ge(stored[par], 16 * 3 * B // 2)

        @block.gpsimd
        def _(pool):
            nc.gpsimd.memset(ctx_end[:, :, P - LAST:P], 0.0)
            nc.gpsimd.memset(ctx_last[:, :, 0:P - LAST], 0.0).then_inc(zeroed, 1)
            pool.wait_ge(var_ready, 1)
            nc.gpsimd.tensor_tensor(rstd[:], rstd[:], c.minus_half[:, 0:NT], ALU.pow).then_inc(rstd_ready, 1)
            with pool.Fori(0, B) as b:
                for a in range(2):
                    pool.wait_ge(hvar_ready, b * 2 + a + 1)
                    nc.gpsimd.tensor_tensor(hrstd[:, a, :], hrstd[:, a, :], c.minus_half[:, 0:JT * H],
                                            ALU.pow).then_inc(hrstd_ready, 1)

        @block.vector
        def _(dve):
            chain = Chain(dve, dve_chain)
            norm_rows_into(nc, dve, chain, c, mv, rstd, var_ready, rstd_ready, 1e-5)

            def write_rows(b):
                for j in range(JT):
                    t = b * JT + j
                    last = nc.vector.tensor_scalar(rows[:, j, :], c.X[:, t, :], mv[:, t, 0:1], rstd[:, t:t + 1],
                                                   ALU.subtract, ALU.mult)
                last.then_inc(rows_ready, 1)

            def sum_squares(b, a):
                dve.wait_ge(squared, b * 2 + a + 1)
                chain.link(nc.vector.reduce_sum(hrstd[:, a, :], squares[:].rearrange("p j (h d) -> p (j h) d", d=HD), AX.X))
                nc.vector.tensor_scalar(hrstd[:, a, :], hrstd[:, a, :], 1.0 / HD, 1e-6, ALU.mult, ALU.add).then_inc(hvar_ready, 1)

            def finish(b, a, tile, scaled):
                dve.wait_ge(hrstd_ready, b * 2 + a + 1)
                heads = tile.rearrange("p j (h d) -> p (j h) d", d=HD)
                chain.link(nc.vector.tensor_tensor(heads, heads, hrstd[:, a, :].unsqueeze(2).broadcast_to((P, JT * H, HD)), ALU.mult))
                for at, op in enumerate((ALU.mult, ALU.add)):
                    if a == 0:
                        last = nc.vector.tensor_tensor(heads, heads, affine[:, 0, at, :].unsqueeze(1).broadcast_to((P, JT * H, HD)), op)
                    else:
                        most = tile[:, 0:JT - 1, :].rearrange("p j (h d) -> p (j h) d", d=HD)
                        nc.vector.tensor_tensor(most, most, affine[:, 1, at, :].unsqueeze(1).broadcast_to((P, (JT - 1) * H, HD)), op)
                        end = by_head(tile[:, JT - 1, :])
                        last = nc.vector.tensor_tensor(end, end, affine[:, 2, at, :].unsqueeze(1).broadcast_to((P, H, HD)), op)
                    if at == 0:
                        chain.link(last)
                    else:
                        last.then_inc(scaled, 1)

            write_rows(0)
            dve.wait_ge(q_loaded, 2 * 16)
            def centre(tiles, ready):
                for n, tile in enumerate(tiles):
                    mean = head_mean[:]
                    chain.link(nc.vector.reduce_sum(mean, tile, AX.X))
                    chain.link(nc.vector.tensor_scalar(mean, mean, 1.0 / HD, None, ALU.mult))
                    last = nc.vector.tensor_tensor(tile, tile, mean.unsqueeze(2).broadcast_to((P, H, HD)), ALU.subtract)
                    if n < len(tiles) - 1:
                        chain.link(last)
                last.then_inc(ready, 1)
                dve.wait_ge(ready, 1)

            centre([by_head(b_q[:])] + [by_head(w_q[:, n, :]) for n in range(CC)], q_weights_ready)
            dve.wait_ge(loaded, 4 * 16)
            dve.wait_ge(kv_loaded, 6 * 16)
            centre([keys_of(b_kv[:]), keys_of(b_kv_end[:])] + [keys_of(w_kv[:, n, :]) for n in range(KC)]
                   + [by_head(w_last[:, n, 0:D]) for n in range(KC)], kv_weights_ready)
            dve.wait_ge(affine_loaded, 8 * 16)
            chain.link(nc.vector.tensor_scalar(affine[:, 0], affine[:, 0], SCALE, None, ALU.mult))
            for b in range(B):
                par = b % 2
                if b >= 2:
                    dve.wait_ge(stored[par], 16 * 3)
                for j in range(JT):
                    dve.wait_ge(q_done, b * JT + j + 1)
                    nc.vector.tensor_tensor(q[:, par, j, :], c.bank[4 + j], b_q[:], ALU.add).then_inc(q_copied, 1)
                if b + 1 < B:
                    dve.wait_ge(rows_turned, b + 1)
                    write_rows(b + 1)
                for j in range(JT):
                    if j == JT // 2:
                        sum_squares(b, 0)
                    dve.wait_ge(kv_done, b * JT + j + 1)
                    bias = (b_kv if j < JT - 1 else b_kv_end)[:].rearrange("p (h a d) -> p h a d", a=2, d=HD)
                    nc.vector.tensor_tensor(by_head(v[:, par, j, :]), by_head(c.bank[2 * (j % 2) + 1]), bias[:, :, 1, :], ALU.add)
                    nc.vector.tensor_tensor(by_head(k[:, par, j, :]), by_head(c.bank[2 * (j % 2)]),
                                            bias[:, :, 0, :], ALU.add).then_inc(k_copied, 1)
                for j in range(JT):
                    t = b * JT + j
                    nc.vector.tensor_tensor(c.X[:, t, :], c.X[:, t, :], b_o[:], ALU.add)
                sum_squares(b, 1)
                finish(b, 0, q[:, par], q_scaled)
                finish(b, 1, k[:, par], k_scaled)

        @block.scalar
        def _(act):
            for b in range(B):
                if b >= 1:
                    act.wait_ge(kv_done, b * JT)
                nc.scalar.copy(ctx_b[:], c.ctxT[:, b])
                nc.scalar.copy(ctx_end[:, :, 0:P - LAST], c.ctxT[:, b, :, S - P:MAIN])
                nc.scalar.copy(ctx_last[:, :, P - LAST:P], c.ctxT[:, b, :, MAIN:S]).then_inc(ctx_ready, 1)
                act.wait_ge(rows_turned, b + 1)
                for n in range(CC):
                    last = nc.scalar.copy(rowsT[:, n, :], c.bank[n])
                last.then_inc(rowsT_ready, 1)
                for a, (tile, copied) in enumerate(((q, q_copied), (k, k_copied))):
                    act.wait_ge(copied, b * JT + JT)
                    if b > 0 or a > 0:
                        act.wait_ge(hvar_ready, b * 2 + a)
                    nc.scalar.activation(squares[:], tile[:, b % 2], ACT.Square).then_inc(squared, 1)

        @block.tensor
        def _(pe):
            pe.wait_ge(zeroed, 1)
            for b in range(B):
                pe.wait_ge(rows_ready, b + 1)
                if b >= 1:
                    pe.wait_ge(k_copied, b * JT)
                for n in range(CC):
                    for j in range(JT):
                        last = nc.tensor.transpose(c.bank[n][:, j * P:(j + 1) * P], rows[:, j, n * P:(n + 1) * P], c.ident[:])
                last.then_inc(rows_turned, 1)
                pe.wait_ge(rowsT_ready, b + 1)
                if b == 0:
                    pe.wait_ge(q_weights_ready, 1)
                if b >= 1:
                    pe.wait_ge(q_copied, b * JT)
                for j in range(JT):
                    for n in range(CC):
                        last = nc.tensor.matmul(c.bank[4 + j], rowsT[:, n, j * P:(j + 1) * P], w_q[:, n, :],
                                                start=(n == 0), stop=(n == CC - 1))
                    last.then_inc(q_done, 1)
                pe.wait_ge(ctx_ready, b + 1)
                if b == 0:
                    pe.wait_ge(kv_weights_ready, 1)
                for j in range(JT):
                    if j >= 2:
                        pe.wait_ge(k_copied, b * JT + j - 1)
                    for a in range(2):
                        bank = by_head(c.bank[2 * (j % 2) + a])
                        for n in range(KC):
                            main = w_kv[:, n, :].rearrange("p (h a d) -> p h a d", a=2, d=HD)[:, :, a, :]
                            if j < JT - 1:
                                last = nc.tensor.matmul(bank, ctx_b[:, n, j * P:(j + 1) * P], main, start=(n == 0), stop=(n == KC - 1))
                            else:
                                nc.tensor.matmul(bank, ctx_end[:, n, :], main, start=(n == 0), stop=False)
                                last = nc.tensor.matmul(bank, ctx_last[:, n, :], by_head(w_last[:, n, a * D:(a + 1) * D]),
                                                        start=False, stop=(n == KC - 1))
                    last.then_inc(kv_done, 1)


def context_attention(nc, c):
    H, HD, LAST = X_H, X_HD, X_LAST
    MAIN = S - LAST
    HPG = P // HD
    GROUPS = B * H // HPG
    PAIRS = HPG * JT // 2
    PARTS = 2 * HPG
    RING = 4
    with ExitStack() as stack:
        w_o = sbuf(nc, stack, "y_w_o", [P, CC, D])
        zeros = sbuf(nc, stack, "y_zeros", [P, JT, D])
        qk = [sbuf(nc, stack, "y_q", [P, 2, JT, P]), sbuf(nc, stack, "y_k", [P, 2, JT, P])]
        mixedT = sbuf(nc, stack, "y_mixedT", [P, GROUPS, S])
        part = sbuf(nc, stack, "y_part", [P, 2, JT, 4, HD], F32R)
        stacked = [sbuf(nc, stack, "y_q_stacked", [P, HPG, S], F32R), sbuf(nc, stack, "y_k_stacked", [P, HPG, S], F32R)]
        ident_r = sbuf(nc, stack, "y_ident_r", [P, P], F32R)
        group_v = sbuf(nc, stack, "y_group_v", [P, JT, P])
        prob = sbuf(nc, stack, "y_prob", [P, RING, 2, S])
        probT = sbuf(nc, stack, "y_probT", [P, HPG, JT, S])
        last_part = sbuf(nc, stack, "y_last_part", [P, RING, 2, LAST])
        nmax = sbuf(nc, stack, "y_nmax", [P, RING, 2, 2])
        rsum = sbuf(nc, stack, "y_rsum", [P, RING, 2, 2])
        rinv = sbuf(nc, stack, "y_rinv", [P, RING, 2, 2])
        w_loaded, loaded_even, loaded_odd, v_loaded, hi_ready, part_ready, part_turned, q_stacked, k_stacked = sems(
            nc, c, "y_", "w_loaded loaded_even loaded_odd v_loaded hi_ready part_ready part_turned q_stacked k_stacked")
        scored, max_found, max_ready, exp_ready, summed, rinv_ready, prob_ready, prob_turned, probT_act, probT_dve = sems(
            nc, c, "y_", "scored max_found max_ready exp_ready summed rinv_ready prob_ready prob_turned probT_act probT_dve")
        valued, mixedT_ready, ident_ready, out_ready, added, zeros_set, zeros_stored = sems(
            nc, c, "y_", "valued mixedT_ready ident_ready out_ready added zeros_set zeros_stored")
        loaded = [loaded_even, loaded_odd]
        stacked_ready = [q_stacked, k_stacked]
        block = stack.enter_context(nc.Block())
        SCORES, PROB_T, PART_T, VALUES = 0, 4, 6, 7

        @block.sync
        def _(sp):
            def of_group(name, group):
                b, hc = group // (H // HPG), group % (H // HPG)
                return c.dram[name][b, :, hc * P:(hc + 1) * P].rearrange("(j p) d -> p j d", p=P)

            def load(group):
                for kind, name in enumerate(("d_xq", "d_xk")):
                    sp.dma_start(qk[kind][:, group % 2], of_group(name, group)).then_inc(loaded[group % 2], 16)

            blank = c.dram["d_sorted"].rearrange("(n j p) d -> n p j d", p=P, j=JT)
            blanks = ROUTED_TILES // JT
            for group in range(2):
                load(group)
            sp.dma_start(group_v[:], of_group("d_xv", 0)).then_inc(v_loaded, 16)
            sp.dma_start(w_o[:], c.dram["L1_xattn_Wo"].rearrange("(k p) n -> p k n", p=P)).then_inc(w_loaded, 16)
            sp.wait_ge(zeros_set, 1)
            for group in range(1, GROUPS):
                if group + 1 < GROUPS:
                    sp.wait_ge(part_ready, PARTS * group)
                    load(group + 1)
                sp.wait_ge(valued, group)
                sp.dma_start(group_v[:], of_group("d_xv", group)).then_inc(v_loaded, 16)
                for n in range(blanks * (group - 1) // (GROUPS - 1), blanks * group // (GROUPS - 1)):
                    sp.dma_start(blank[n], zeros[:]).then_inc(zeros_stored, 16)
            sp.wait_ge(zeros_stored, 16 * blanks)

        @block.gpsimd
        def _(pool):
            nc.gpsimd.memset(zeros[:], 0.0).then_inc(zeros_set, 1)
            with pool.Fori(0, GROUPS * PAIRS // RING) as n:
                for r in range(RING):
                    pool.wait_ge(rinv_ready, n * RING + r + 1)
                    nc.gpsimd.tensor_tensor(prob[:, r, :, MAIN:S], last_part[:, r],
                                            rinv[:, r, 1, :].unsqueeze(2).broadcast_to((P, 2, LAST)), ALU.mult)
                    nc.gpsimd.tensor_tensor(prob[:, r, :, 0:MAIN], prob[:, r, :, 0:MAIN],
                                            rinv[:, r, 0, :].unsqueeze(2).broadcast_to((P, 2, MAIN)),
                                            ALU.mult).then_inc(prob_ready, 1)

        @block.vector
        def _(dve):
            nc.vector.tensor_copy(ident_r[:], c.ident[:]).then_inc(ident_ready, 1)

            def part_views(group, i):
                kind, ring, h = i % 2, i % 2, i // 2
                source = qk[kind][:, bass.ds(group % 2, 1), :, h * HD:(h + 1) * HD].rearrange("p a j d -> p (a j) d")
                if kind == 0:
                    hi, lo = part[:, ring, :, 0:2, :], part[:, ring, :, 2:4, :]
                else:
                    hi, lo = part[:, ring, :, 0:4:2, :], part[:, ring, :, 1:4:2, :]
                return source.unsqueeze(2).broadcast_to((P, JT, 2, HD)), hi, lo

            def write_hi(group, i):
                wide, hi, _ = part_views(group, i)
                nc.vector.tensor_copy(hi, wide).then_inc(hi_ready, 1)

            def write_lo(group, i):
                wide, hi, lo = part_views(group, i)
                dve.wait_ge(hi_ready, group * PARTS + i + 1)
                nc.vector.tensor_tensor(lo, wide, hi.bitcast(F32), ALU.subtract).then_inc(part_ready, 1)

            def find_max(group, pair, first=False):
                dve.wait_ge(scored, group * PAIRS + pair + 1)
                r = pair % RING
                if pair >= RING or not first:
                    dve.wait_ge(prob_ready, group * PAIRS + pair - RING + 1)
                banks = c.psum[:, SCORES + 2 * (pair % 2):SCORES + 2 * (pair % 2) + 2, :]
                nc.vector.reduce_max(nmax[:, r, 1, :], banks[:, :, MAIN:S], AX.X, negate=True)
                nc.vector.reduce_max(nmax[:, r, 0, :], banks[:, :, 0:MAIN], AX.X, negate=True).then_inc(max_found, 1)

            def subtract_last_max(group, pair):
                r = pair % RING
                banks = c.psum[:, SCORES + 2 * (pair % 2):SCORES + 2 * (pair % 2) + 2, :]
                dve.wait_ge(max_found, group * PAIRS + pair + 1)
                nc.vector.tensor_tensor(last_part[:, r], banks[:, :, MAIN:S],
                                        nmax[:, r, 1, :].unsqueeze(2).broadcast_to((P, 2, LAST)), ALU.add).then_inc(max_ready, 1)

            def sum_last(group, pair):
                dve.wait_ge(exp_ready, group * PAIRS + pair + 1)
                r = pair % RING
                nc.vector.reduce_sum(rsum[:, r, 1, :], last_part[:, r], AX.X).then_inc(summed, 1)

            def invert_sums(group, pair):
                r = pair % RING
                dve.wait_ge(summed, group * PAIRS + pair + 1)
                nc.vector.reciprocal(rinv[:, r], rsum[:, r]).then_inc(rinv_ready, 1)

            def copy_probT(group, pair):
                h, j = pair // 2 % HPG, pair % 2 * 2 + 1
                dve.wait_ge(prob_turned, (group * PAIRS + pair) * 2 + 2)
                nc.vector.tensor_copy(probT[:, h, :, j * P:(j + 1) * P],
                                      c.bank[PROB_T + 1].rearrange("p (n q) -> p n q", q=P)).then_inc(probT_dve, 1)

            def copy_values(group):
                dve.wait_ge(valued, group + 1)
                nc.vector.tensor_copy(mixedT[:, bass.ds(group, 1), :], c.bank[VALUES].unsqueeze(1)).then_inc(mixedT_ready, 1)

            def a_group(group, parity=None, first=False, more=True):
                for s in range(PAIRS):
                    if s + 1 < PAIRS or more:
                        find_max(group, s + 1, first)
                    sum_last(group, s)
                    if more:
                        if s == 0:
                            dve.wait_ge(loaded[parity], LOADS * ((group + 1) // 2 + 1))
                        dve.wait_ge(part_turned, (group + 1) * PARTS + s - 1)
                        write_hi(group + 1, s)
                    if s + 1 < PAIRS or more:
                        subtract_last_max(group, s + 1)
                    invert_sums(group, s)
                    if s >= 3 or not first:
                        copy_probT(group, s - 3)
                    if more:
                        write_lo(group + 1, s)
                    if s == 4 and not first:
                        copy_values(group - 1)

            LOADS = 2 * 16
            dve.wait_ge(loaded[0], LOADS)
            for i in range(PARTS):
                if i >= 2:
                    dve.wait_ge(part_turned, i - 1)
                write_hi(0, i)
                write_lo(0, i)
            find_max(0, 0, True)
            subtract_last_max(0, 0)
            a_group(0, 1, first=True)
            with dve.Fori(0, (GROUPS - 2) // 2) as n:
                for par in range(2):
                    a_group(n * 2 + 1 + par, par)
            final = GROUPS - 1
            a_group(final, more=False)
            for pair in range(PAIRS - 3, PAIRS):
                copy_probT(final, pair)
            copy_values(final)
            for t in range(NT):
                dve.wait_ge(out_ready, t + 1)
                nc.vector.tensor_tensor(c.X[:, t, :], c.X[:, t, :], c.bank[t % 8], ALU.add).then_inc(added, 1)
                if t > 0:
                    row_stats(nc, dve, c, t - 1, added, t)
            row_stats(nc, dve, c, NT - 1, added, NT)

        @block.scalar
        def _(act):
            def copy_part(group, i):
                act.wait_ge(part_turned, group * PARTS + i + 1)
                nc.scalar.copy(stacked[i % 2][:, i // 2 % HPG, :], c.bank[PART_T]).then_inc(stacked_ready[i % 2], 1)

            def exponentials(group, pair):
                act.wait_ge(max_ready, group * PAIRS + pair + 1)
                r = pair % RING
                nc.scalar.activation(last_part[:, r], last_part[:, r], ACT.Exp)
                for n in range(2):
                    last = nc.scalar.activation(prob[:, r, n, 0:MAIN], c.bank[SCORES + 2 * (pair % 2) + n][:, 0:MAIN], ACT.Exp,
                                                bias=nmax[:, r, 0, n:n + 1], accum_out=rsum[:, r, 0, n:n + 1])
                last.then_inc(exp_ready, 1)

            def copy_probT(group, pair):
                h, j = pair // 2 % HPG, pair % 2 * 2
                act.wait_ge(prob_turned, (group * PAIRS + pair) * 2 + 1)
                nc.scalar.copy(probT[:, h, :, j * P:(j + 1) * P],
                               c.bank[PROB_T].rearrange("p (n q) -> p n q", q=P)).then_inc(probT_act, 1)

            def a_group(group, first=False, more=True):
                for s in range(PAIRS):
                    if s >= RING or not first:
                        act.wait_ge(prob_turned, (group * PAIRS + s - RING) * 2 + 2)
                    exponentials(group, s)
                    if s >= 3 or not first:
                        copy_probT(group, s - 3)
                    if (s > 0 and more) or (s == 0 and not first):
                        copy_part(group + (1 if s > 0 else 0), (s - 1) % PARTS)

            for i in range(PARTS):
                copy_part(0, i)
            a_group(0, first=True)
            with act.Fori(1, GROUPS - 1) as group:
                a_group(group)
            final = GROUPS - 1
            a_group(final, more=False)
            for pair in range(PAIRS - 3, PAIRS):
                copy_probT(final, pair)

        @block.tensor
        def _(pe):
            def turn_part(group, i, first=False):
                pe.wait_ge(part_ready, group * PARTS + i + 1)
                if i >= 1:
                    pe.wait_ge(stacked_ready[(i + 1) % 2], group * HPG + (i - 1) // 2 + 1)
                elif not first:
                    pe.wait_ge(k_stacked, group * HPG)
                for j in range(JT):
                    last = nc.tensor.transpose(c.bank[PART_T][:, j * P:(j + 1) * P].bitcast(F32R),
                                               part[:, i % 2, j].rearrange("p r d -> p (r d)"), ident_r[:])
                last.then_inc(part_turned, 1)

            def scores(group, pair):
                h = pair // 2 % HPG
                if pair % 2 == 0:
                    for ready in stacked_ready:
                        pe.wait_ge(ready, group * HPG + pair // 2 + 1)
                for n in range(2):
                    j = pair % 2 * 2 + n
                    last = nc.tensor.matmul(c.bank[SCORES + j], stacked[0][:, h, j * P:(j + 1) * P], stacked[1][:, h, :],
                                            start=True, stop=True)
                last.then_inc(scored, 1)

            def turn(group, pair, bank_used=True):
                pe.wait_ge(prob_ready, group * PAIRS + pair + 1)
                for n, copied in enumerate((probT_act, probT_dve)):
                    if bank_used:
                        pe.wait_ge(copied, group * PAIRS + pair)
                    for k in range(JT):
                        last = nc.tensor.transpose(c.bank[PROB_T + n][:, k * P:(k + 1) * P],
                                                   prob[:, pair % RING, n, k * P:(k + 1) * P], c.ident[:])
                    last.then_inc(prob_turned, 1)

            def values(group, first=False):
                pe.wait_ge(probT_act, group * PAIRS + PAIRS)
                pe.wait_ge(probT_dve, group * PAIRS + PAIRS)
                pe.wait_ge(v_loaded, group * 16 + 16)
                if not first:
                    pe.wait_ge(mixedT_ready, group)
                for n in range(JT):
                    for h in range(HPG):
                        last = nc.tensor.matmul(c.bank[VALUES][h * HD:(h + 1) * HD, :], group_v[:, n, h * HD:(h + 1) * HD],
                                                probT[:, h, n, :], start=(n == 0), stop=(n == JT - 1),
                                                tile_position=(0, h * HD))
                last.then_inc(valued, 1)

            def a_group(group, first=False, second=False, more=True):
                for s in range(PAIRS):
                    if (s > 0 and more) or (s == 0 and not first):
                        turn_part(group + (1 if s > 0 else 0), (s - 1) % PARTS)
                    if s == 2 and not first:
                        values(group - 1, second)
                    if s + 2 < PAIRS or more:
                        pe.wait_ge(exp_ready, group * PAIRS + s + 1)
                        scores(group, s + 2)
                    if s >= 2 or not first:
                        turn(group, s - 2, bank_used=(s > 2 or not first))

            pe.wait_ge(ident_ready, 1)
            for i in range(PARTS):
                turn_part(0, i, first=True)
            for pair in range(2):
                scores(0, pair)
            a_group(0, first=True)
            a_group(1, second=True)
            with pe.Fori(2, GROUPS - 1) as group:
                a_group(group)
            final = GROUPS - 1
            a_group(final, more=False)
            for pair in range(PAIRS - 2, PAIRS):
                turn(final, pair)
            values(final)
            pe.wait_ge(w_loaded, 16)
            pe.wait_ge(mixedT_ready, GROUPS)
            pe.wait_ge(probT_act, GROUPS * PAIRS)
            for t in range(NT):
                if t >= 8:
                    pe.wait_ge(added, t - 7)
                for n in range(CC):
                    j = t % JT
                    last = nc.tensor.matmul(c.bank[t % 8], mixedT[:, t // JT * CC + n, j * P:(j + 1) * P], w_o[:, n, :],
                                            start=(n == 0), stop=(n == CC - 1))
                last.then_inc(out_ready, 1)


E_ = 32
TOPK = 6
EG = 4
EPG = E_ // EG
M = 352
ROUTED_TILES = TOK * TOPK // P + E_
ROUTED_END = NT + ROUTED_TILES
TILES = ROUTED_END + NT


def route_tokens(nc, c, hs, slots, weights, tile_set, tiles_through):
    with ExitStack() as stack:
        mv = sbuf(nc, stack, "r_mv", [P, NT, 2])
        rstd = sbuf(nc, stack, "r_rstd", [P, NT])
        rows = sbuf(nc, stack, "r_rows", [P, JT, D])
        rowsT = sbuf(nc, stack, "r_rowsT", [P, CC, S])
        w_gate = sbuf(nc, stack, "r_w_gate", [P, CC, E_])
        tri = sbuf(nc, stack, "r_tri", [P, P])
        ones = sbuf(nc, stack, "r_ones", [P, P])
        iota = sbuf(nc, stack, "r_iota", [P, P])
        part = sbuf(nc, stack, "r_part", [P, 1])
        earlier = sbuf(nc, stack, "r_earlier", [P, EG, EG])
        steps = sbuf(nc, stack, "r_steps", [P, NT])
        score = sbuf(nc, stack, "r_score", [P, NT, E_])
        best = sbuf(nc, stack, "r_best", [P, NT, EG])
        pair = sbuf(nc, stack, "r_pair", [P, NT, EG, EG])
        pair2 = sbuf(nc, stack, "r_pair2", [P, NT, EG, EG])
        top = sbuf(nc, stack, "r_top", [P, NT, 8])
        index = sbuf(nc, stack, "r_index", [P, NT, 8], U32)
        indexf = sbuf(nc, stack, "r_indexf", [P, NT, 8])
        hot = sbuf(nc, stack, "r_hot", [P, TOPK, NT, E_])
        member = sbuf(nc, stack, "r_member", [P, NT, E_])
        members_before = sbuf(nc, stack, "r_members_before", [P, NT, E_])
        place = sbuf(nc, stack, "r_place", [P, NT, E_])
        work = sbuf(nc, stack, "r_work", [P, NT, E_])
        slotsf = sbuf(nc, stack, "r_slotsf", [P, NT, TOPK])
        wsum = sbuf(nc, stack, "r_wsum", [P, NT])
        count = sbuf(nc, stack, "r_count", [P, E_])
        over = sbuf(nc, stack, "r_over", [P, E_, NT])
        tiles = sbuf(nc, stack, "r_tiles", [P, E_])
        through = sbuf(nc, stack, "r_through", [P, E_])
        first_slot = sbuf(nc, stack, "r_first_slot", [P, E_])
        expert_of = sbuf(nc, stack, "r_expert_of", [P, 1])
        small = sbuf(nc, stack, "r_small", [P, E_])
        loaded, var_ready, rstd_ready, rows_ready, rows_turned, rowsT_ready, gated, taken = sems(
            nc, c, "r_", "loaded var_ready rstd_ready rows_ready rows_turned rowsT_ready gated taken")
        exped, members_ready, counted, expert_ready, expert_turned, dve_chain, hs_stored, exp_ready, ones_set, hs_ready = sems(
            nc, c, "r_", "exped members_ready counted expert_ready expert_turned dve_chain hs_stored exp_ready ones_set hs_ready")
        block = stack.enter_context(nc.Block())

        @block.sync
        def _(sp):
            for dst, src in ((w_gate[:], c.dram["L1_ffn_gate_w"].rearrange("(k p) n -> p k n", p=P)), (tri[:], c.dram["i_tri"]),
                             (iota[:], c.dram["i_iota"]), (part[:], c.dram["i_part"]), (earlier[:], c.dram["i_earlier"]), (steps[:], c.dram["i_steps"])):
                sp.dma_start(dst, src).then_inc(loaded, 16)
            sp.wait_ge(hs_ready, B)
            sp.dma_start(c.dram["d_hs"].rearrange("(t p) d -> p t d", p=P), hs[:]).then_inc(hs_stored, 16)
            sp.wait_ge(hs_stored, 16)

        @block.gpsimd
        def _(pool):
            nc.gpsimd.memset(ones[:], 1.0).then_inc(ones_set, 1)
            pool.wait_ge(var_ready, 1)
            nc.gpsimd.tensor_tensor(rstd[:], rstd[:], c.minus_half[:, 0:NT], ALU.pow).then_inc(rstd_ready, 1)

        @block.vector
        def _(dve):
            chain = Chain(dve, dve_chain)
            link = chain.link
            norm_rows_into(nc, dve, chain, c, mv, rstd, var_ready, rstd_ready, 1e-5)
            with dve.Fori(0, B) as b:
                for j in range(JT):
                    t = bass.ds(b * JT + j, 1)
                    last = nc.vector.tensor_scalar(rows[:, j:j + 1, :], c.X[:, t, :], mv[:, t, 0:1], rstd[:, t],
                                                   ALU.subtract, ALU.mult)
                last.then_inc(rows_ready, 1)
                for j in range(JT):
                    t = bass.ds(b * JT + j, 1)
                    last = nc.vector.tensor_scalar(hs[:, t, :], c.X[:, t, :], mv[:, t, 0:1], rstd[:, t],
                                                   ALU.subtract, ALU.mult)
                last.then_inc(hs_ready, 1)
                dve.wait_ge(gated, b + 1)
                nc.vector.tensor_scalar(score[:, bass.ds(b * JT, JT), :], c.bank[4][:, 0:JT * E_].rearrange("p (j e) -> p j e", j=JT),
                                        -1.0, None, ALU.mult).then_inc(taken, 1)
            dve.wait_ge(exp_ready, 1)
            link(nc.vector.tensor_scalar(score[:], score[:], 1.0, None, ALU.add))
            link(nc.vector.reciprocal(score[:], score[:]))
            dve.wait_ge(loaded, 6 * 16)
            link(nc.vector.reduce_max(best[:], score[:].rearrange("p t (g e) -> p t g e", g=EG), AX.X))
            shape = (P, NT, EG, EG)
            this, other = best[:].unsqueeze(3).broadcast_to(shape), best[:].unsqueeze(2).broadcast_to(shape)
            nc.vector.tensor_tensor(pair[:], other, this, ALU.is_gt)
            link(nc.vector.tensor_tensor(pair2[:], other, this, ALU.is_equal))
            link(nc.vector.tensor_tensor(pair2[:], pair2[:], earlier[:].unsqueeze(1).broadcast_to(shape), ALU.mult))
            link(nc.vector.tensor_tensor(pair[:], pair[:], pair2[:], ALU.add))
            link(nc.vector.reduce_sum(best[:], pair[:], AX.X))
            link(nc.vector.tensor_scalar(best[:], best[:], 2.0, None, ALU.is_lt))
            by_group = best[:].unsqueeze(3).broadcast_to((P, NT, EG, EPG))
            grouped = lambda tile: tile[:].rearrange("p t (g e) -> p t g e", g=EG)
            link(nc.vector.tensor_tensor(grouped(score), grouped(score), by_group, ALU.mult))
            link(nc.vector.tensor_scalar(best[:], best[:], -1.0, None, ALU.add))
            link(nc.vector.tensor_tensor(grouped(score), grouped(score), by_group, ALU.add))
            for t in range(NT):
                last = nc.vector.max(top[:, t, :], score[:, t, :])
            link(last)
            for t in range(NT):
                last = nc.vector.max_index(index[:, t, :], top[:, t, :], score[:, t, :])
            link(last)
            link(nc.vector.tensor_copy(indexf[:], index[:]))
            link(nc.vector.reduce_sum(wsum[:], top[:, :, 0:TOPK], AX.X))
            link(nc.vector.reciprocal(wsum[:], wsum[:]))
            nc.vector.tensor_tensor(weights[:], top[:, :, 0:TOPK], wsum[:].unsqueeze(2).broadcast_to((P, NT, TOPK)), ALU.mult)
            wide = (P, NT, E_)
            for k in range(TOPK):
                last = nc.vector.tensor_tensor(hot[:, k], iota[:, 0:E_].unsqueeze(1).broadcast_to(wide),
                                               indexf[:, :, k:k + 1].broadcast_to(wide), ALU.is_equal)
            link(last)
            link(nc.vector.tensor_tensor(member[:], hot[:, 0], hot[:, 1], ALU.add))
            for k in range(2, TOPK):
                link(nc.vector.tensor_tensor(member[:], member[:], hot[:, k], ALU.add))
            link(nc.vector.memset(members_before[:, 0, :], 0.0))
            for t in range(1, NT):
                link(nc.vector.tensor_tensor(members_before[:, t, :], members_before[:, t - 1, :], member[:, t - 1, :], ALU.add))
            nc.vector.tensor_tensor(small[:], members_before[:, NT - 1, :], member[:, NT - 1, :], ALU.add).then_inc(members_ready, 1)
            dve.wait_ge(counted, 1)
            nc.vector.tensor_copy(place[:].rearrange("p t e -> p (t e)"), c.bank[5])
            link(nc.vector.tensor_copy(count[:], c.bank[6][:, 0:E_]))
            link(nc.vector.tensor_tensor(over[:], count[:].unsqueeze(2).broadcast_to((P, E_, NT)),
                                         steps[:].unsqueeze(1).broadcast_to((P, E_, NT)), ALU.is_gt))
            link(nc.vector.reduce_sum(tiles[:], over[:], AX.X))
            link(nc.vector.tensor_scalar(tiles[:], tiles[:], 1.0, None, ALU.max))
            link(nc.vector.tensor_tensor_scan(through[:], ones[:, 0:E_], tiles[:], 0.0, ALU.mult, ALU.add))
            link(nc.vector.tensor_tensor(first_slot[:], through[:], tiles[:], ALU.subtract))
            link(nc.vector.tensor_scalar(first_slot[:], first_slot[:], float(P), None, ALU.mult))
            link(nc.vector.tensor_scalar(small[:], through[:], part[:, 0:1], None, ALU.is_le, ALU.add, accum_out=expert_of[:]))
            nc.vector.tensor_scalar(expert_of[:], expert_of[:], float(E_ - 1), 1.0, ALU.min, ALU.add).then_inc(expert_ready, 1)
            link(nc.vector.tensor_tensor(place[:], place[:], first_slot[:].unsqueeze(1).broadcast_to(wide), ALU.add))
            for k in range(TOPK):
                link(nc.vector.tensor_tensor(work[:], hot[:, k], place[:], ALU.mult))
                link(nc.vector.reduce_sum(slotsf[:, :, k], work[:], AX.X))
            nc.vector.tensor_copy(slots[:], slotsf[:])
            nc.vector.tensor_scalar(tiles_through[:, 1:1 + E_], through[0:1, :], float(NT), None, ALU.add)
            nc.vector.memset(tiles_through[:, 0:1], NT)
            nc.vector.memset(tile_set[:, 0:NT], 0)
            nc.vector.memset(tile_set[:, ROUTED_END:], E_ + 1)
            dve.wait_ge(expert_turned, 1)
            nc.vector.tensor_copy(tile_set[:, NT:ROUTED_END], c.bank[7][0:1, 0:ROUTED_TILES])

        @block.scalar
        def _(act):
            with act.Fori(0, B) as b:
                act.wait_ge(rows_turned, b + 1)
                for k in range(CC):
                    last = nc.scalar.copy(rowsT[:, k, :], c.bank[k])
                last.then_inc(rowsT_ready, 1)
            act.wait_ge(taken, B)
            nc.scalar.activation(score[:], score[:], ACT.Exp).then_inc(exp_ready, 1)

        @block.tensor
        def _(pe):
            pe.wait_ge(loaded, 6 * 16)
            with pe.Fori(0, B) as b:
                pe.wait_ge(rows_ready, b + 1)
                for k in range(CC):
                    for j in range(JT):
                        last = nc.tensor.transpose(c.bank[k][:, j * P:(j + 1) * P], rows[:, j, k * P:(k + 1) * P], c.ident[:])
                last.then_inc(rows_turned, 1)
                pe.wait_ge(rowsT_ready, b + 1)
                for j in range(JT):
                    for k in range(CC):
                        last = nc.tensor.matmul(c.bank[4][:, j * E_:(j + 1) * E_], rowsT[:, k, j * P:(j + 1) * P], w_gate[:, k, :],
                                                start=(k == 0), stop=(k == CC - 1))
                last.then_inc(gated, 1)
            pe.wait_ge(ones_set, 1)
            pe.wait_ge(members_ready, 1)
            nc.tensor.matmul(c.bank[5], tri[:], member[:].rearrange("p t e -> p (t e)"), start=True, stop=False)
            nc.tensor.matmul(c.bank[5], ones[:], members_before[:].rearrange("p t e -> p (t e)"), start=False, stop=True)
            nc.tensor.matmul(c.bank[6][:, 0:E_], ones[:], small[:], start=True, stop=True).then_inc(counted, 1)
            pe.wait_ge(expert_ready, 1)
            nc.tensor.transpose(c.bank[7][0:1, 0:P], expert_of[:], c.ident[:]).then_inc(expert_turned, 1)


def expert_tiles(nc, c, hs, slots, weights, tile_set, tiles_through):
    ME = 3
    cuts = [0, P, 2 * P, M]
    LAST_M = M - 2 * P
    with ExitStack() as stack:
        ones = sbuf(nc, stack, "e_ones", [P, 1])
        gu_in = sbuf(nc, stack, "e_gu_in", [P, CC, 2 * M])
        d_in = sbuf(nc, stack, "e_d_in", [P, ME, D])
        gu_high, gu_low = [sbuf(nc, stack, f"e_gu_{part}", [P, 2, CC, 2 * M], F32R) for part in ("high", "low")]
        d_high, d_low = [sbuf(nc, stack, f"e_d_{part}", [P, 2, ME, D], F32R) for part in ("high", "low")]
        row = [sbuf(nc, stack, f"e_row{n}", [P, D]) for n in range(2)]
        rowT_high = [sbuf(nc, stack, f"e_rowT_high{n}", [P, CC, P], F32R) for n in range(2)]
        rowT_low = [sbuf(nc, stack, f"e_rowT_low{n}", [P, CC, P], F32R) for n in range(2)]
        silu = [sbuf(nc, stack, f"e_silu{n}", [P, M]) for n in range(2)]
        mid = [sbuf(nc, stack, f"e_mid{n}", [P, M]) for n in range(2)]
        midT_high = sbuf(nc, stack, "e_midT_high", [P, ME, P], F32R)
        midT_low = sbuf(nc, stack, "e_midT_low", [P, ME, P], F32R)
        y = [sbuf(nc, stack, f"e_y{n}", [P, D]) for n in range(2)]
        gathered = hs[:, 0:2 * TOPK].rearrange("p (s k) d -> p s k d", s=2)
        LAG = 4
        row_even, row_odd, y_even, y_odd, scattered = sems(nc, c, "e_", "row_even row_odd y_even y_odd scattered")
        gathered_even, gathered_odd, weighed, x_stored, sets_high = sems(
            nc, c, "e_", "gathered_even gathered_odd weighed x_stored sets_high")
        row_loaded, y_stored, gathered_in = [row_even, row_odd], [y_even, y_odd], [gathered_even, gathered_odd]
        gate_loaded, up_loaded, down_loaded, arrivals_seen, ones_set, high_ready, gate_split, up_split, down_split = sems(
            nc, c, "e_", "gate_loaded up_loaded down_loaded arrivals_seen ones_set high_ready gate_split up_split down_split")
        row_turned, rowT_high_ready, rowT_low_ready, gate_done, up_done, silu_ready, mid_ready, mid_turned = sems(
            nc, c, "e_", "row_turned rowT_high_ready rowT_low_ready gate_done up_done silu_ready mid_ready mid_turned")
        midT_high_ready, midT_low_ready, down_done, y_copied = sems(
            nc, c, "e_", "midT_high_ready midT_low_ready down_done y_copied")
        block = stack.enter_context(nc.Block())
        G, U, XT, HT, Y = [c.bank[0], c.bank[1]], [c.bank[2], c.bank[3]], c.bank[4], c.bank[5], [c.bank[6], c.bank[7]]

        @block.sync
        def _(sp):
            def load(n, gate, up, down, again=True):
                if again:
                    sp.wait_ge(gate_split, n)
                sp.dma_start(gu_in[:, :, 0:M], gate.rearrange("(k p) n -> p k n", p=P)).then_inc(gate_loaded, 16)
                if again:
                    sp.wait_ge(up_split, n)
                sp.dma_start(gu_in[:, :, M:2 * M], up.rearrange("(k p) n -> p k n", p=P)).then_inc(up_loaded, 16)
                if again:
                    sp.wait_ge(down_split, n)
                sp.dma_start(d_in[:, 0:2, :], down[0:2 * P, :].rearrange("(k p) n -> p k n", p=P)).then_inc(down_loaded, 16)
                sp.dma_start(d_in[0:LAST_M, 2, :], down[2 * P:M, :]).then_inc(down_loaded, 16)

            def shared(n, half, again=True):
                part = slice(half * M, (half + 1) * M)
                load(n, c.dram["L1_ffn_sw_gate"][:, part], c.dram["L1_ffn_sw_up"][:, part], c.dram["L1_ffn_sw_down"][part, :], again)

            shared(0, 0, again=False)
            with sp.Fori(0, E_) as e:
                load(e + 1, *(c.dram[w][bass.ds(e, 1)].rearrange("a k n -> (a k) n")
                              for w in ("L1_ffn_w_gate", "L1_ffn_w_up", "L1_ffn_w_down")))
            shared(E_ + 1, 1)
            for t in range(NT):
                sp.wait_ge(weighed, TOPK * (t + 1))
                sp.dma_start(c.out.rearrange("b (j p) d -> p (b j) d", p=P)[:, t, :], c.X[:, t, :]).then_inc(x_stored, 16)
            sp.wait_ge(x_stored, 16 * NT)

        @block.gpsimd
        def _(pool):
            def arrived(sem, n):
                pool.wait_ge(sem, n)
                pool.nop().then_inc(arrivals_seen, 1)

            def split(n, par):
                done = pool.value_load(tiles_through[0:1, bass.ds(n - 2, 1)], min_val=1, max_val=TILES)
                pool.wait_ge(up_done, done)
                arrived(gate_loaded, 16 * (n + 1))
                nc.gpsimd.tensor_tensor(gu_high[:, par, :, 0:M], gu_in[:, :, 0:M], ones[:].unsqueeze(2).broadcast_to((P, CC, M)), ALU.mult).then_inc(high_ready, 1)
                arrived(up_loaded, 16 * (n + 1))
                nc.gpsimd.tensor_tensor(gu_high[:, par, :, M:2 * M], gu_in[:, :, M:2 * M], ones[:].unsqueeze(2).broadcast_to((P, CC, M)), ALU.mult).then_inc(high_ready, 1)
                pool.wait_ge(high_ready, 3 * (n - 2) + 1)
                nc.gpsimd.tensor_tensor(gu_low[:, par, :, 0:M], gu_in[:, :, 0:M], gu_high[:, par, :, 0:M].bitcast(F32),
                                        ALU.subtract).then_inc(gate_split, 1)
                pool.wait_ge(high_ready, 3 * (n - 2) + 2)
                nc.gpsimd.tensor_tensor(gu_low[:, par, :, M:2 * M], gu_in[:, :, M:2 * M],
                                        gu_high[:, par, :, M:2 * M].bitcast(F32), ALU.subtract).then_inc(up_split, 1)
                pool.wait_ge(down_done, done)
                arrived(down_loaded, 32 * (n + 1))
                nc.gpsimd.tensor_tensor(d_high[:, par, 0:2, :], d_in[:, 0:2, :], ones[:].unsqueeze(2).broadcast_to((P, 2, D)), ALU.mult)
                nc.gpsimd.tensor_tensor(d_high[0:LAST_M, par, 2, :], d_in[0:LAST_M, 2, :], ones[0:LAST_M].broadcast_to((LAST_M, D)), ALU.mult).then_inc(high_ready, 1)
                pool.wait_ge(high_ready, 3 * (n - 2) + 3)
                nc.gpsimd.tensor_tensor(d_low[:, par, 0:2, :], d_in[:, 0:2, :], d_high[:, par, 0:2, :].bitcast(F32), ALU.subtract)
                nc.gpsimd.tensor_tensor(d_low[0:LAST_M, par, 2, :], d_in[0:LAST_M, 2, :],
                                        d_high[0:LAST_M, par, 2, :].bitcast(F32), ALU.subtract).then_inc(down_split, 1)

            nc.gpsimd.memset(ones[:], 1.0).then_inc(ones_set, 1)
            pool.wait_ge(ones_set, 1)
            for t in range(NT):
                for k in range(TOPK):
                    nc.gpsimd.indirect_dma_start(c.dram["d_sorted"], bass.IndirectOffsetOnAxis(ap=slots[:, t, k:k + 1], axis=0),
                                                 hs[:, t, :], None).then_inc(scattered, 16)
            with pool.Fori(1, E_ // 2 + 1) as n:
                for par in range(2):
                    split(n * 2 + par, par)
            pool.wait_ge(scattered, NT * TOPK * 16)
            for par in range(2):
                pool.wait_ge(y_stored[par], 16 * (ROUTED_TILES // 2))
            for t in range(NT):
                if t >= 2:
                    pool.wait_ge(weighed, TOPK * (t - 1))
                for k in range(TOPK):
                    nc.gpsimd.indirect_dma_start(gathered[:, t % 2, k, :], None, c.dram["d_y"],
                                                 bass.IndirectOffsetOnAxis(ap=slots[:, t, k:k + 1], axis=0)).then_inc(gathered_in[t % 2], 16)

        def pieces(par):
            return ((gate_loaded, gate_split, 16, [(gu_in[:, :, 0:M], gu_high[:, par, :, 0:M], gu_low[:, par, :, 0:M])]),
                    (up_loaded, up_split, 16, [(gu_in[:, :, M:2 * M], gu_high[:, par, :, M:2 * M], gu_low[:, par, :, M:2 * M])]),
                    (down_loaded, down_split, 32, [(d_in[:, 0:2, :], d_high[:, par, 0:2, :], d_low[:, par, 0:2, :]),
                                                   (d_in[0:LAST_M, 2, :], d_high[0:LAST_M, par, 2, :], d_low[0:LAST_M, par, 2, :])]))

        hs_tiles = c.dram["d_hs"].rearrange("(t p) d -> p t d", p=P)
        sorted_tiles = c.dram["d_sorted"].rearrange("(t p) d -> p t d", p=P)
        y_tiles = c.dram["d_y"].rearrange("(t p) d -> p t d", p=P)

        @block.scalar
        def _(act):
            def load(source, t, par):
                act.dma_start(row[par][:].unsqueeze(1), source[:, bass.ds(t, 1), :]).then_inc(row_loaded[par], 16)

            def silus(i, par):
                act.wait_ge(gate_done, i + 1)
                nc.scalar.activation(silu[par][:], G[par][:, 0:M], ACT.Silu).then_inc(silu_ready, 1)

            def copy_rowT(i, par):
                act.wait_ge(row_turned, i + 1)
                nc.scalar.copy(rowT_high[par][:], XT.rearrange("p (k n) -> p k n", k=CC)).then_inc(rowT_high_ready, 1)

            def copy_midT(i):
                act.wait_ge(mid_turned, i + 1)
                nc.scalar.copy(midT_high[:, 0:2, :], HT[:, 0:2 * P].rearrange("p (k n) -> p k n", k=2))
                nc.scalar.copy(midT_high[0:LAST_M, 2, :], HT[0:LAST_M, 2 * P:3 * P]).then_inc(midT_high_ready, 1)

            def store(i, par):
                act.wait_ge(y_copied, i + 1)
                act.dma_start(y_tiles[:, bass.ds(i - NT, 1), :], y[par][:].unsqueeze(1)).then_inc(y_stored[par], 16)

            def steps(i, par, more=True, source=None, t=None, stores=True, old=True):
                silus(i, par)
                if old:
                    copy_midT(i - 1)
                if more:
                    copy_rowT(i + 1, 1 - par)
                if source is not None:
                    load(source, t, 1 - par)
                if stores:
                    store(i - 2, par)

            def high_parts(n):
                for loaded, _, count, tiles in pieces(n):
                    act.wait_ge(loaded, count * (n + 1))
                    for whole, high, _ in tiles:
                        last = nc.scalar.copy(high, whole)
                    last.then_inc(sets_high, 1)

            load(hs_tiles, 0, 0)
            load(hs_tiles, 1, 1)
            copy_rowT(0, 0)
            load(hs_tiles, 2, 0)
            high_parts(0)
            for i in range(2):
                steps(i, i, source=hs_tiles, t=i + 3, stores=False, old=(i > 0))
            high_parts(1)
            with act.Fori(1, NT // 2 - 2) as n:
                for par in range(2):
                    steps(n * 2 + par, par, source=hs_tiles, t=n * 2 + par + 3, stores=False)
            for i in range(NT - 4, NT + 2):
                if i + 3 < NT:
                    steps(i, i % 2, source=hs_tiles, t=i + 3, stores=False)
                else:
                    if i + 3 == NT:
                        act.wait_ge(scattered, NT * TOPK * 16)
                    steps(i, i % 2, source=sorted_tiles, t=i + 3 - NT, stores=False)
            with act.Fori(NT // 2 + 1, ROUTED_END // 2 - 2) as n:
                for par in range(2):
                    steps(n * 2 + par, par, source=sorted_tiles, t=n * 2 + par + 3 - NT)
            for i in range(ROUTED_END - 4, ROUTED_END + 2):
                if i + 3 < ROUTED_END:
                    steps(i, i % 2, source=sorted_tiles, t=i + 3 - NT)
                else:
                    steps(i, i % 2, source=hs_tiles, t=i + 3 - ROUTED_END)
            with act.Fori(ROUTED_END // 2 + 1, TILES // 2 - 2) as n:
                for par in range(2):
                    steps(n * 2 + par, par, source=hs_tiles, t=n * 2 + par + 3 - ROUTED_END, stores=False)
            for i in range(TILES - 4, TILES):
                if i + 3 < TILES:
                    steps(i, i % 2, source=hs_tiles, t=i + 3 - ROUTED_END, stores=False)
                else:
                    steps(i, i % 2, more=(i + 1 < TILES), stores=False)
            copy_midT(TILES - 1)

        @block.vector
        def _(dve):
            def low_rowT(i, par):
                dve.wait_ge(rowT_high_ready, i + 1)
                nc.vector.tensor_tensor(rowT_low[par][:], XT.rearrange("p (k n) -> p k n", k=CC),
                                        rowT_high[par][:].bitcast(F32), ALU.subtract).then_inc(rowT_low_ready, 1)

            def low_midT(i):
                dve.wait_ge(midT_high_ready, i + 1)
                nc.vector.tensor_tensor(midT_low[:, 0:2, :], HT[:, 0:2 * P].rearrange("p (k n) -> p k n", k=2),
                                        midT_high[:, 0:2, :].bitcast(F32), ALU.subtract)
                nc.vector.tensor_tensor(midT_low[0:LAST_M, 2, :], HT[0:LAST_M, 2 * P:3 * P],
                                        midT_high[0:LAST_M, 2, :].bitcast(F32), ALU.subtract).then_inc(midT_low_ready, 1)

            def multiply(i, par):
                dve.wait_ge(silu_ready, i + 1)
                dve.wait_ge(up_done, i + 1)
                nc.vector.tensor_tensor(mid[par][:], silu[par][:], U[par][:, 0:M], ALU.mult).then_inc(mid_ready, 1)

            def copy_y(i, par, stored=None):
                dve.wait_ge(down_done, i + 1)
                if stored is not None:
                    dve.wait_ge(y_stored[par], stored)
                nc.vector.tensor_copy(y[par][:], Y[par]).then_inc(y_copied, 1)

            def add_y(i, par, t):
                dve.wait_ge(down_done, i + 1)
                x = c.X[:, bass.ds(t, 1), :]
                nc.vector.tensor_tensor(x, x, Y[par].unsqueeze(1), ALU.add).then_inc(y_copied, 1)

            def weigh(t, par, first, last):
                if first == 0:
                    dve.wait_ge(y_copied, ROUTED_END + t + 1)
                    dve.wait_ge(gathered_in[par], TOPK * 16 * ((t - par) // 2 + 1))
                x = c.X[:, bass.ds(t, 1), :]
                for k in range(first, last):
                    if k > 0:
                        dve.wait_ge(weighed, t * TOPK + k)
                    nc.vector.scalar_tensor_tensor(x, gathered[:, par, k:k + 1, :], weights[:, bass.ds(t, 1), k:k + 1], x,
                                                   ALU.mult, ALU.add).then_inc(weighed, 1)

            def low_parts(n):
                for p, (_, split, _, tiles) in enumerate(pieces(n)):
                    dve.wait_ge(sets_high, 3 * n + p + 1)
                    for whole, high, low in tiles:
                        last = nc.vector.tensor_tensor(low, whole, high.bitcast(F32), ALU.subtract)
                    last.then_inc(split, 1)

            def steps(i, par, more=True, weighs=None):
                low_midT(i - 1)
                if more:
                    low_rowT(i + 1, 1 - par)
                if weighs is not None:
                    weigh(weighs, par, 0, TOPK // 2)
                multiply(i, par)
                if weighs is not None:
                    weigh(weighs, par, TOPK // 2, TOPK)

            low_rowT(0, 0)
            low_parts(0)
            low_rowT(1, 1)
            multiply(0, 0)
            for i in range(1, 4):
                steps(i, i % 2)
                add_y(i - 1, (i - 1) % 2, i - 1)
                if i == 2:
                    low_parts(1)
            with dve.Fori(2, NT // 2) as n:
                for par in range(2):
                    steps(n * 2 + par, par)
                    add_y(n * 2 + par - 1, 1 - par, n * 2 + par - 1)
            for i in range(NT, NT + 4):
                steps(i, i % 2)
                if i == NT:
                    add_y(i - 1, 1, i - 1)
                else:
                    copy_y(i - 1, (i - 1) % 2, 16 if i == NT + 3 else None)
            with dve.Fori(NT // 2 + 2, ROUTED_END // 2) as n:
                for par in range(2):
                    steps(n * 2 + par, par)
                    copy_y(n * 2 + par - 1, 1 - par, 16 * (n - NT // 2 - 1 + par))
            for i in range(ROUTED_END, ROUTED_END + LAG):
                steps(i, i % 2)
                if i == ROUTED_END:
                    copy_y(i - 1, 1, 16 * (ROUTED_TILES // 2 - 1))
                else:
                    add_y(i - 1, (i - 1) % 2, i - 1 - ROUTED_END)
            with dve.Fori((ROUTED_END + LAG) // 2, TILES // 2 - 1) as n:
                for par in range(2):
                    steps(n * 2 + par, par, weighs=n * 2 + par - ROUTED_END - LAG)
                    add_y(n * 2 + par - 1, 1 - par, n * 2 + par - 1 - ROUTED_END)
            for i in (TILES - 2, TILES - 1):
                steps(i, i % 2, more=(i + 1 < TILES), weighs=i - ROUTED_END - LAG)
                add_y(i - 1, (i - 1) % 2, i - 1 - ROUTED_END)
            low_midT(TILES - 1)
            add_y(TILES - 1, 1, NT - 1)
            for t in range(NT - LAG, NT):
                weigh(t, t % 2, 0, TOPK)

        @block.tensor
        def _(pe):
            def turn_row(i, par, loads):
                pe.wait_ge(row_loaded[par], loads)
                for k in range(CC):
                    last = nc.tensor.transpose(XT[:, k * P:(k + 1) * P], row[par][:, k * P:(k + 1) * P], c.ident[:])
                last.then_inc(row_turned, 1)

            def turn_mid(i, par):
                pe.wait_ge(mid_ready, i + 1)
                for k in range(ME):
                    n = cuts[k + 1] - cuts[k]
                    last = nc.tensor.transpose(HT[0:n, k * P:(k + 1) * P], mid[par][:, cuts[k]:cuts[k + 1]], c.ident[:])
                last.then_inc(mid_turned, 1)

            def product(bank, par, buffer, at, low_parts=None):
                for k in range(CC):
                    for part, w in enumerate((gu_high, gu_low)):
                        nc.tensor.matmul(bank[:, 0:M].unsqueeze(1), rowT_high[par][:, k, :],
                                         w[:, bass.ds(buffer, 1), k, at:at + M], start=(k == 0 and part == 0), stop=False)
                if low_parts is not None:
                    pe.wait_ge(rowT_low_ready, low_parts)
                for k in range(CC):
                    last = nc.tensor.matmul(bank[:, 0:M].unsqueeze(1), rowT_low[par][:, k, :],
                                            gu_high[:, bass.ds(buffer, 1), k, at:at + M],
                                            start=False, stop=(k == CC - 1))
                return last

            def down(i, par, e, before=None):
                buffer = e % 2
                pe.wait_ge(midT_high_ready, i + 1)
                pe.wait_ge(down_split, e + 1)
                if before is not None:
                    pe.wait_ge(y_copied, before)
                for k in range(ME):
                    n = cuts[k + 1] - cuts[k]
                    for part, w in enumerate((d_high, d_low)):
                        nc.tensor.matmul(Y[par].unsqueeze(1), midT_high[0:n, k, :], w[0:n, bass.ds(buffer, 1), k, :],
                                         start=(k == 0 and part == 0), stop=False)
                pe.wait_ge(midT_low_ready, i + 1)
                for k in range(ME):
                    n = cuts[k + 1] - cuts[k]
                    last = nc.tensor.matmul(Y[par].unsqueeze(1), midT_low[0:n, k, :], d_high[0:n, bass.ds(buffer, 1), k, :],
                                            start=False, stop=(k == ME - 1))
                last.then_inc(down_done, 1)

            def set_of(i):
                return pe.value_load(tile_set[0:1, bass.ds(i, 1)], min_val=0, max_val=E_ + 1)

            def tile(i, par, old, more=True, loads=None, used=None, before=None):
                e = set_of(i)
                pe.wait_ge(rowT_high_ready, i + 1)
                pe.wait_ge(gate_split, e + 1)
                if used is not None:
                    pe.wait_ge(mid_ready, used)
                buffer = e % 2
                product(G[par], par, buffer, 0, i + 1).then_inc(gate_done, 1)
                if old is not None:
                    turn_mid(i - 1, 1 - par)
                if more:
                    turn_row(i + 1, 1 - par, loads)
                pe.wait_ge(up_split, e + 1)
                product(U[par], par, buffer, M).then_inc(up_done, 1)
                if old is not None:
                    down(i - 1, 1 - par, old, before)

            turn_row(0, 0, 16)
            tile(0, 0, None, loads=16)
            tile(1, 1, 0, loads=32)
            tile(2, 0, 0, loads=32, used=1)
            tile(3, 1, 0, loads=48, used=2, before=1)
            with pe.Fori(2, TILES // 2 - 1) as n:
                tile(n * 2, 0, set_of(n * 2 - 1), loads=16 * (n + 1), used=n * 2 - 1, before=n * 2 - 2)
                tile(n * 2 + 1, 1, set_of(n * 2), loads=16 * (n + 2), used=n * 2, before=n * 2 - 1)
            i = TILES - 2
            tile(i, 0, set_of(i - 1), loads=16 * (TILES // 2), used=i - 1, before=i - 2)
            tile(i + 1, 1, set_of(i), more=False, used=i, before=i - 1)
            turn_mid(i + 1, 1)
            down(i + 1, 1, set_of(i + 1), i)


def routed_ffn(nc, c):
    with ExitStack() as stack:
        slots = sbuf(nc, stack, "f_slots", [P, NT, TOPK], U32)
        weights = sbuf(nc, stack, "f_weights", [P, NT, TOPK])
        tile_set = sbuf(nc, stack, "f_tile_set", [1, TILES], I32)
        tiles_through = sbuf(nc, stack, "f_tiles_through", [1, 1 + E_], I32)
        hs = sbuf(nc, stack, "f_hs", [P, NT, D])
        route_tokens(nc, c, hs, slots, weights, tile_set, tiles_through)
        expert_tiles(nc, c, hs, slots, weights, tile_set, tiles_through)


def build(nc, aps, out):
    c = Core()
    c.dram = aps
    c.out = out
    c.of_stage = []
    with ExitStack() as stack:
        c.X = sbuf(nc, stack, "X", [P, NT, D])
        c.ctxT = sbuf(nc, stack, "ctxT", [P, B, KC, S])
        c.ident = sbuf(nc, stack, "ident", [P, P])
        c.stats = sbuf(nc, stack, "row_stats", [P, NT, 6])
        c.minus_half = sbuf(nc, stack, "minus_half", [P, 64])
        c.psum = stack.enter_context(nc.psum_tensor("psum", [P, 8, 512], F32))
        c.bank = [c.psum[:, n, :] for n in range(8)]
        half_set, = sems(nc, c, "g_", "half_set")
        with nc.Block() as block:
            @block.gpsimd
            def _(pool):
                nc.gpsimd.memset(c.minus_half[:], -0.5).then_inc(half_set, 1)
                pool.wait_ge(half_set, 1)
        load_constants(nc, c)
        end_stage(nc, c)
        for stage in (map_attention, token_choice_ffn, project_heads, context_attention):
            stage(nc, c)
            end_stage(nc, c)
        routed_ffn(nc, c)


def shape_tables():
    s, p = np.arange(S), np.arange(P)
    inv_freq = (np.float32(1.0) / np.float32(10000.0) ** (np.arange(0, 128, 2, dtype=np.float32) / np.float32(128))).astype(np.float32)
    ang = (s.astype(np.float32)[:, None] * inv_freq).astype(np.float32)
    slots = np.arange(2 * P)
    causal = np.stack([slots[None, :] <= (g * P + p)[:, None] for g in range(2)], 1)
    f = np.float32
    return {
        "i_ident": np.eye(P, dtype=f),
        "i_tri": (p[:, None] < p[None, :]).astype(f),
        "i_before": np.stack([s[None, :] < (j * P + p)[:, None] for j in range(JT)], 1).astype(f),
        "i_iota": np.broadcast_to(p.astype(f), (P, P)).copy(),
        "i_slot_base": np.broadcast_to(((np.arange(NT) // JT % 2) * (S // 8) + 1).astype(f), (P, NT)).copy(),
        "i_rope": np.concatenate([np.cos(ang), np.sin(ang)], 1).astype(f),
        "i_part": p.astype(f)[:, None].copy(),
        "i_earlier": np.broadcast_to(np.tri(EG, EG, -1, dtype=f), (P, EG, EG)).copy(),
        "i_steps": np.broadcast_to((np.arange(NT) * P).astype(f), (P, NT)).copy(),
        "i_causal": np.where(causal, f(0), f(-1e30)).reshape(P, 4 * P).astype(f),
    }


def kernel(**inputs):
    import concourse.bacc as _bacc
    from concourse.bass_utils import run_bass_kernel_spmd as _run

    nc = _bacc.Bacc("TRN2", target_bir_lowering=False, num_devices=1)
    arrays, aps = {}, {}
    for name, a in {**inputs, **shape_tables()}.items():
        a = np.ascontiguousarray(a)
        arrays[f"in_{name}"] = a
        aps[name] = nc.dram_tensor(f"in_{name}", a.shape, mybir.dt.from_np(a.dtype), kind="ExternalInput").ap()
    aps["d_scores"] = nc.dram_tensor("d_scores", (NT, P), F32).ap()
    for name in ("d_xq", "d_xk", "d_xv"):
        aps[name] = nc.dram_tensor(name, (B, S, D), F32).ap()
    aps["d_hs"] = nc.dram_tensor("d_hs", (TOK, D), F32).ap()
    aps["d_sorted"] = nc.dram_tensor("d_sorted", (ROUTED_TILES * P, D), F32).ap()
    aps["d_y"] = nc.dram_tensor("d_y", (ROUTED_TILES * P, D), F32).ap()
    out = nc.dram_tensor("out", (B, S, D), F32, kind="ExternalOutput").ap()
    build(nc, aps, out)
    r = _run(nc, [arrays], core_ids=[0])
    return r.results[0]["out"]
```
